# Optimizing a Trainium2 kernel written in Bass

```python
import numpy as np
import jax
import jax.numpy as jnp

def _softmax(x, axis=-1):
    return jax.nn.softmax(x, axis=axis)

def _gelu(x):
    return jax.nn.gelu(x, approximate=True)

def _silu(x):
    return jax.nn.silu(x)

def _sigmoid(x):
    return jax.nn.sigmoid(x)

def _layernorm(x, axis=-1, eps=1e-05):
    m = jnp.mean(x, axis=axis, keepdims=True)
    v = jnp.var(x, axis=axis, keepdims=True)
    return (x - m) / jnp.sqrt(v + eps)

def _scatter_add(tgt, idx, src, axis=0):
    return tgt.at[idx].add(src)

def _segment_sum(src, seg, n):
    return jax.ops.segment_sum(src, seg, n)
kernel_name = 'mk_adaln_d2_jaxref_r4_e69bd3'

def setup_inputs(seed: int=0):
    np.random.seed(seed)
    _w = jnp.asarray

    def _L0_attn_setup():
        import jax, jax.numpy as jnp
        import numpy as np
        key = jax.random.key(seed)
        ks = jax.random.split(key, 5)
        B, S, D = (2, 512, 256)
        scale = 0.02
        return {'x': jax.random.normal(ks[0], (B, S, D), dtype=jnp.float32), 'q_proj_weight': jax.random.normal(ks[1], (D, D), dtype=jnp.float32) * scale, 'k_proj_weight': jax.random.normal(ks[2], (D, D), dtype=jnp.float32) * scale, 'v_proj_weight': jax.random.normal(ks[3], (D, D), dtype=jnp.float32) * scale, 'o_proj_weight': jax.random.normal(ks[4], (D, D), dtype=jnp.float32) * scale}
    _L0_attn_in = _L0_attn_setup()

    def _L0_ffn_setup():
        import jax, jax.numpy as jnp
        import numpy as np
        TOP_K = 32
        TEMPERATURE = 1.0
        PARAM_SCALE = 0.02

        def _compose_weight(logits, A, B):
            vals, idx = jax.lax.top_k(logits, TOP_K)
            w = jax.nn.softmax(vals / TEMPERATURE)
            A_sel = A[idx]
            B_sel = B[idx]
            return jnp.einsum('k,kir,kro->io', w, A_sel, B_sel)
        key = jax.random.key(seed)
        ks = jax.random.split(key, 7)
        B, S, D, F, P, R = (2, 256, 256, 1024, 64, 64)
        x = jax.random.normal(ks[0], (B, S, D), dtype=jnp.float32)
        fc1_A = jax.random.normal(ks[1], (P, D, R), dtype=jnp.float32) * PARAM_SCALE
        fc1_B = jax.random.normal(ks[2], (P, R, F), dtype=jnp.float32) * PARAM_SCALE
        fc2_A = jax.random.normal(ks[3], (P, F, R), dtype=jnp.float32) * PARAM_SCALE
        fc2_B = jax.random.normal(ks[4], (P, R, D), dtype=jnp.float32) * PARAM_SCALE
        fc1_logits = jax.random.normal(ks[5], (P,), dtype=jnp.float32)
        fc2_logits = jax.random.normal(ks[6], (P,), dtype=jnp.float32)
        return {'x': x, 'fc1_A': fc1_A, 'fc1_B': fc1_B, 'fc2_A': fc2_A, 'fc2_B': fc2_B, 'fc1_logits': fc1_logits, 'fc2_logits': fc2_logits}
    _L0_ffn_in = _L0_ffn_setup()
    _L0_c = _w((lambda *s: np.random.randn(*s).astype(np.float32) * 0.05)(16, 256))
    _L0_wmod = _w((lambda *s: np.random.randn(*s).astype(np.float32) * 0.05)(256, 6 * 256) * 256 ** (-0.5))

    def _L1_attn_setup():
        import jax, jax.numpy as jnp
        import numpy as np
        N_HEAD = 16
        EPS = 1e-06

        def _linear_attention(q, k, v):
            B, H, D = (q.shape[1], q.shape[2], q.shape[3])

            def step(carry, qkv_t):
                S, z = carry
                qt, kt, vt = qkv_t
                S = S + kt[..., :, None] * vt[..., None, :]
                z = z + kt
                num = jnp.einsum('bhi,bhij->bhj', qt, S)
                den = jnp.sum(qt * z, axis=-1, keepdims=True)
                return ((S, z), num / (den + EPS))
            S0 = jnp.zeros((B, H, D, D), q.dtype)
            z0 = jnp.zeros((B, H, D), q.dtype)
            _, y = jax.lax.scan(step, (S0, z0), (q, k, v))
            return y
        key = jax.random.key(seed)
        k1, k2, k3 = jax.random.split(key, 3)
        B, T, C = (2, 512, 256)
        x = jax.random.normal(k1, (B, T, C), dtype=jnp.float32)
        w_attn = jax.random.normal(k2, (C, 3 * C), dtype=jnp.float32) * 0.02
        w_proj = jax.random.normal(k3, (C, C), dtype=jnp.float32) * 0.02
        return {'x': x, 'w_attn': w_attn, 'w_proj': w_proj}
    _L1_attn_in = _L1_attn_setup()

    def _L1_ffn_setup():
        import jax, jax.numpy as jnp
        import numpy as np
        ALPHA = 1.0
        key = jax.random.key(seed)
        ks = jax.random.split(key, 7)
        B, S, IN, OUT = (8, 2048, 256, 256)
        RANK, DDIM, UDIM = (4, 100, 50)
        return {'hidden_states': jax.random.normal(ks[0], (B, S, IN), dtype=jnp.float32), 'W': jax.random.normal(ks[1], (OUT, IN), dtype=jnp.float32) * 0.02, 'b': jax.random.normal(ks[2], (OUT,), dtype=jnp.float32) * 0.02, 'lora_down': jax.random.normal(ks[3], (RANK, DDIM), dtype=jnp.float32) * 0.1, 'lora_up': jax.random.normal(ks[4], (UDIM, RANK), dtype=jnp.float32) * 0.1, 'down_aux': jax.random.normal(ks[5], (DDIM, IN), dtype=jnp.float32) * 0.03, 'up_aux': jax.random.normal(ks[6], (OUT, UDIM), dtype=jnp.float32) * 0.03}
    _L1_ffn_in = _L1_ffn_setup()
    _L1_c = _w((lambda *s: np.random.randn(*s).astype(np.float32) * 0.05)(16, 256))
    _L1_wmod = _w((lambda *s: np.random.randn(*s).astype(np.float32) * 0.05)(256, 6 * 256) * 256 ** (-0.5))
    _d = {'L0_attn_x': _L0_attn_in['x'], 'L0_attn_q_proj_weight': _L0_attn_in['q_proj_weight'], 'L0_attn_k_proj_weight': _L0_attn_in['k_proj_weight'], 'L0_attn_v_proj_weight': _L0_attn_in['v_proj_weight'], 'L0_attn_o_proj_weight': _L0_attn_in['o_proj_weight'], 'L0_ffn_fc1_A': _L0_ffn_in['fc1_A'], 'L0_ffn_fc1_B': _L0_ffn_in['fc1_B'], 'L0_ffn_fc2_A': _L0_ffn_in['fc2_A'], 'L0_ffn_fc2_B': _L0_ffn_in['fc2_B'], 'L0_ffn_fc1_logits': _L0_ffn_in['fc1_logits'], 'L0_ffn_fc2_logits': _L0_ffn_in['fc2_logits'], 'L0_c': _L0_c, 'L0_wmod': _L0_wmod, 'L1_attn_w_attn': _L1_attn_in['w_attn'], 'L1_attn_w_proj': _L1_attn_in['w_proj'], 'L1_ffn_W': _L1_ffn_in['W'], 'L1_ffn_b': _L1_ffn_in['b'], 'L1_ffn_lora_down': _L1_ffn_in['lora_down'], 'L1_ffn_lora_up': _L1_ffn_in['lora_up'], 'L1_ffn_down_aux': _L1_ffn_in['down_aux'], 'L1_ffn_up_aux': _L1_ffn_in['up_aux'], 'L1_c': _L1_c, 'L1_wmod': _L1_wmod}
    _x0 = _d['L0_attn_x']
    _d['L0_attn_x'] = jax.random.normal(jax.random.fold_in(jax.random.key(seed), 1), (16, 512, 256), dtype=_x0.dtype)
    del _x0
    return _d

def reference(L0_attn_x, L0_attn_q_proj_weight, L0_attn_k_proj_weight, L0_attn_v_proj_weight, L0_attn_o_proj_weight, L0_ffn_fc1_A, L0_ffn_fc1_B, L0_ffn_fc2_A, L0_ffn_fc2_B, L0_ffn_fc1_logits, L0_ffn_fc2_logits, L0_c, L0_wmod, L1_attn_w_attn, L1_attn_w_proj, L1_ffn_W, L1_ffn_b, L1_ffn_lora_down, L1_ffn_lora_up, L1_ffn_down_aux, L1_ffn_up_aux, L1_c, L1_wmod):

    def _L0_attn_ref(x, q_proj_weight, k_proj_weight, v_proj_weight, o_proj_weight):
        import jax, jax.numpy as jnp
        import numpy as np
        num_heads = 16
        B, S, d_in = x.shape
        d_k = q_proj_weight.shape[0]
        head_size = d_k // num_heads

        def split_heads(t):
            return t.reshape(B, S, num_heads, head_size).transpose(0, 2, 1, 3)
        q = split_heads(jnp.einsum('bsd,kd->bsk', x, q_proj_weight))
        k = split_heads(jnp.einsum('bsd,kd->bsk', x, k_proj_weight))
        v = split_heads(jnp.einsum('bsd,kd->bsk', x, v_proj_weight))
        scale = jnp.float32(head_size) ** (-0.5)
        scores = jnp.einsum('bhtc,bhkc->bhtk', q, k) * scale
        causal = jnp.tril(jnp.ones((S, S), dtype=bool))
        scores = jnp.where(causal, scores, -jnp.inf)
        attn = jax.nn.softmax(scores, axis=-1)
        out = jnp.einsum('bhtk,bhkc->bhtc', attn, v)
        out = out.transpose(0, 2, 1, 3).reshape(B, S, d_k)
        return jnp.einsum('bsv,dv->bsd', out, o_proj_weight)

    def _L0_ffn_ref(x, fc1_A, fc1_B, fc2_A, fc2_B, fc1_logits, fc2_logits):
        import jax, jax.numpy as jnp
        import numpy as np
        TOP_K = 32
        TEMPERATURE = 1.0
        PARAM_SCALE = 0.02

        def _compose_weight(logits, A, B):
            vals, idx = jax.lax.top_k(logits, TOP_K)
            w = jax.nn.softmax(vals / TEMPERATURE)
            A_sel = A[idx]
            B_sel = B[idx]
            return jnp.einsum('k,kir,kro->io', w, A_sel, B_sel)
        W1 = _compose_weight(fc1_logits, fc1_A, fc1_B)
        W2 = _compose_weight(fc2_logits, fc2_A, fc2_B)
        h = jax.nn.gelu(jnp.einsum('bsd,df->bsf', x, W1))
        return jnp.einsum('bsf,fd->bsd', h, W2)

    def _L1_attn_ref(x, w_attn, w_proj):
        import jax, jax.numpy as jnp
        import numpy as np
        N_HEAD = 16
        EPS = 1e-06

        def _linear_attention(q, k, v):
            B, H, D = (q.shape[1], q.shape[2], q.shape[3])

            def step(carry, qkv_t):
                S, z = carry
                qt, kt, vt = qkv_t
                S = S + kt[..., :, None] * vt[..., None, :]
                z = z + kt
                num = jnp.einsum('bhi,bhij->bhj', qt, S)
                den = jnp.sum(qt * z, axis=-1, keepdims=True)
                return ((S, z), num / (den + EPS))
            S0 = jnp.zeros((B, H, D, D), q.dtype)
            z0 = jnp.zeros((B, H, D), q.dtype)
            _, y = jax.lax.scan(step, (S0, z0), (q, k, v))
            return y
        B, T, C = x.shape
        H = N_HEAD
        D = C // H
        qkv = x @ w_attn
        q, k, v = jnp.split(qkv, 3, axis=-1)

        def to_tbhd(a):
            return a.reshape(B, T, H, D).transpose(1, 0, 2, 3)
        q = jax.nn.elu(to_tbhd(q)) + 1.0
        k = jax.nn.elu(to_tbhd(k)) + 1.0
        v = to_tbhd(v)
        y = _linear_attention(q, k, v)
        y = y.transpose(1, 0, 2, 3).reshape(B, T, C)
        return y @ w_proj

    def _L1_ffn_ref(hidden_states, W, b, lora_down, lora_up, down_aux, up_aux):
        import jax, jax.numpy as jnp
        import numpy as np
        ALPHA = 1.0
        lilora_weight = up_aux @ (lora_up @ (lora_down @ down_aux))
        base = jnp.einsum('bsi,oi->bso', hidden_states, W) + b
        delta = jnp.einsum('bsi,oi->bso', hidden_states, lilora_weight)
        return base + ALPHA * delta
    x = L0_attn_x
    mod = (_silu(L0_c) @ L0_wmod).reshape(L0_c.shape[0], 6, 1, -1)
    sa, ca, ga, sb, cb, gb = (mod[:, 0], mod[:, 1], mod[:, 2], mod[:, 3], mod[:, 4], mod[:, 5])
    ga = (2 * (ga >= 0) - 1) * jnp.maximum(jnp.abs(ga), 0.25)
    gb = (2 * (gb >= 0) - 1) * jnp.maximum(jnp.abs(gb), 0.25)
    h = _layernorm(x, axis=-1) * (1 + ca) + sa
    x = x + ga * _L0_attn_ref(h, L0_attn_q_proj_weight, L0_attn_k_proj_weight, L0_attn_v_proj_weight, L0_attn_o_proj_weight)
    h = _layernorm(x, axis=-1) * (1 + cb) + sb
    x = x + gb * _L0_ffn_ref(h, L0_ffn_fc1_A, L0_ffn_fc1_B, L0_ffn_fc2_A, L0_ffn_fc2_B, L0_ffn_fc1_logits, L0_ffn_fc2_logits)
    mod = (_silu(L1_c) @ L1_wmod).reshape(L1_c.shape[0], 6, 1, -1)
    sa, ca, ga, sb, cb, gb = (mod[:, 0], mod[:, 1], mod[:, 2], mod[:, 3], mod[:, 4], mod[:, 5])
    ga = (2 * (ga >= 0) - 1) * jnp.maximum(jnp.abs(ga), 0.25)
    gb = (2 * (gb >= 0) - 1) * jnp.maximum(jnp.abs(gb), 0.25)
    h = _layernorm(x, axis=-1) * (1 + ca) + sa
    x = x + ga * _L1_attn_ref(h, L1_attn_w_attn, L1_attn_w_proj)
    h = _layernorm(x, axis=-1) * (1 + cb) + sb
    x = x + gb * _L1_ffn_ref(h, L1_ffn_W, L1_ffn_b, L1_ffn_lora_down, L1_ffn_lora_up, L1_ffn_down_aux, L1_ffn_up_aux)
    return x

_drawn_inputs = setup_inputs


def setup_inputs(seed=0):
    import zlib

    import numpy as np

    out = dict(_drawn_inputs(seed))
    spreads = {}
    factors = {'L0_attn_q_proj_weight': 8.0,
     'L0_attn_k_proj_weight': 8.0,
     'L0_attn_v_proj_weight': 8.0,
     'L0_attn_o_proj_weight': 8.0,
     'L0_ffn_fc1_A': 8.0,
     'L0_ffn_fc1_B': 8.0,
     'L0_ffn_fc2_A': 8.0,
     'L0_ffn_fc2_B': 8.0,
     'L0_ffn_fc1_logits': 8.0,
     'L0_ffn_fc2_logits': 8.0,
     'L0_c': 8.0,
     'L0_wmod': 8.0,
     'L1_attn_w_attn': 8.0,
     'L1_attn_w_proj': 8.0,
     'L1_ffn_b': 200.0,
     'L1_ffn_lora_down': 8.0,
     'L1_ffn_lora_up': 8.0,
     'L1_ffn_down_aux': 8.0,
     'L1_ffn_up_aux': 8.0,
     'L1_ffn_W': 8.0}
    for name, (base, spread) in spreads.items():
        noise = np.random.default_rng([zlib.crc32(name.encode()), seed]).standard_normal(out[name].shape)
        drawn = base * np.exp(spread * noise) if base else spread * noise
        out[name] = jnp.asarray(drawn.astype(out[name].dtype))
    for name, factor in factors.items():
        out[name] = (out[name] * factor).astype(out[name].dtype)
    return out
```

```python
from contextlib import ExitStack

import numpy as np

import concourse.bass as bass
from concourse import mybir

ALU = mybir.AluOpType
ACT = mybir.ActivationFunctionType
F32 = mybir.dt.float32
F32R = mybir.dt.float32r
BF16 = mybir.dt.bfloat16
U32 = mybir.dt.uint32
AX_X = mybir.AxisListType.X

P = 128
D = 256
C = D // P
S = 512
T = S // P
HEADS = 16
HD = D // HEADS
F = 1024
FT = F // P
TOPK = 32
RANK = 64
SLOT = 64
ONES_ROW = 48
NEG = -1e30
LN_EPS = 1e-5
PASSES = ((0, 0), (1, 0), (0, 1))

ds = bass.ds


def since(e, sem, n):
    if not isinstance(n, int) or n > 0:
        e.wait_ge(sem, n)


class Memory:

    def __init__(self, nc, prefix):
        self.nc, self.prefix, self.tensors, self.semaphores = nc, prefix, ExitStack(), []

    def __enter__(self):
        return self

    def __exit__(self, *error):
        if error[0] is None:
            self.nc.all_engine_barrier()
            self.nc.clear_and_free_semaphores(self.semaphores)
            self.nc.all_engine_barrier()
        self.tensors.close()

    def sb(self, name, shape, dt=F32):
        return self.tensors.enter_context(self.nc.sbuf_tensor(f"{self.prefix}_{name}", shape, dt))

    def ps(self, name, shape=(P, 512), dt=F32):
        return self.tensors.enter_context(self.nc.psum_tensor(f"{self.prefix}_{name}", list(shape), dt))

    def sem(self, name):
        self.semaphores.append(self.nc.alloc_semaphore(name=f"{self.prefix}_{name}"))
        return self.semaphores[-1]


def bodies(e, n, body):
    pairs = max(0, (n - 3) // 2)
    for b in (-1, 0, 1):
        body(b, b % 2, b // 2)
    if pairs:
        with e.Fori(0, pairs) as i:
            body(i * 2 + 2, 0, i + 1)
            body(i * 2 + 3, 1, i + 1)
    for b in range(2 + 2 * pairs, n + 1):
        body(b, b % 2, b // 2)


def valid(b, n):
    return not isinstance(b, int) or 0 <= b < n


class Norm:

    def __init__(self, m, x_in, consts, scale, shift, copies):
        self.x_in, self.k, self.scale, self.shift = x_in, consts, scale, shift
        self.x = m.sb("ln_x", [P, T, D])
        self.stats = m.sb("ln_stats", [P, T, 6])
        self.mv = m.sb("ln_mv", [P, T, 2])
        self.veps = m.sb("ln_veps", [P, T])
        self.rstd = m.sb("ln_rstd", [P, T])
        self.nmr = m.sb("ln_nmr", [P, T])
        self.n = m.sb("ln_n", [P, T, D])
        self.h32 = m.sb("ln_h32", [P, C, S])
        self.h = [[m.sb(f"ln_h{i}_{part}", [P, C, S], F32R) for part in ("hi", "lo")] for i in range(copies)]
        self.s = {}
        for name in ("x_loaded", "bn_done", "aggregating", "mv_done", "veps_done", "rstd_done", "nmr_done", "normed",
                     "hT_ready", "h32_done", "h_hi_done", "h_lo_done"):
            self.s[name] = m.sem(f"ln_{name}")

    def load(self, e, b):
        since(e, self.s["normed"], T * b)
        e.dma_start(self.x[:], self.x_in[b]).then_inc(self.s["x_loaded"], 16)

    def statistics(self, e, b, t):
        if t == 0:
            e.wait_ge(self.s["x_loaded"], 16 * (b + 1))
            since(e, self.s["mv_done"], T * b)
        e.bn_stats(self.stats[:, t, :], self.x[:, t, :]).then_inc(self.s["bn_done"], 1)

    def variance(self, e, b):
        since(e, self.s["normed"], T * b)
        e.wait_ge(self.s["bn_done"], T * (b + 1))
        e.sem_inc(self.s["aggregating"], 1)
        for t in range(T):
            e.bn_aggr(self.mv[:, t, :], self.stats[:, t, :]).then_inc(self.s["mv_done"], 1)
        e.wait_ge(self.s["mv_done"], T * (b + 1))
        e.tensor_scalar(self.veps[:], self.mv[:, :, 1], LN_EPS, None, ALU.add).then_inc(self.s["veps_done"], 1)

    def rsqrt(self, e, b):
        e.wait_ge(self.s["veps_done"], b + 1)
        e.tensor_tensor(self.rstd[:], self.veps[:], self.k["minus_half"][:], ALU.pow).then_inc(self.s["rstd_done"], 1)

    def shift_of_mean(self, e, b):
        e.wait_ge(self.s["rstd_done"], b + 1)
        e.scalar_tensor_tensor(self.nmr[:], self.mv[:, :, 0], -1.0, self.rstd[:], ALU.mult,
                               ALU.mult).then_inc(self.s["nmr_done"], 1)

    def all_statistics(self, e, b):
        for t in range(T):
            self.statistics(e, b, t)
        self.variance(e, b)
        self.shift_of_mean(e, b)

    def normalise(self, e, b, t):
        if t == 0:
            e.wait_ge(self.s["nmr_done"], b + 1)
            since(e, self.s["hT_ready"], C * b)
        e.activation(self.n[:, t, :], self.x[:, t, :], ACT.Identity, scale=self.rstd[:, t:t + 1],
                     bias=self.nmr[:, t:t + 1]).then_inc(self.s["normed"], 1)

    def transpose(self, e, b, c, bank):
        e.wait_ge(self.s["normed"], T * (b + 1))
        for t in range(T):
            mm = e.transpose(bank[:, t * P:(t + 1) * P], self.n[:, t, c * P:(c + 1) * P], self.k["ident"][:])
        mm.then_inc(self.s["hT_ready"], 1)

    def modulate(self, e, b, c, bank):
        e.wait_ge(self.s["hT_ready"], C * b + c + 1)
        since(e, self.s["h_lo_done"], C * (b - 1) + c + 1)
        e.activation(self.h32[:, c, :], bank[:], ACT.Identity, scale=self.scale[:, c, ds(b, 1)],
                     bias=self.shift[:, c, ds(b, 1)]).then_inc(self.s["h32_done"], 1)

    def split(self, e, b, c, copy):
        hi, lo = self.h[copy]
        e.wait_ge(self.s["h32_done"], C * b + c + 1)
        e.tensor_copy(hi[:, c, :], self.h32[:, c, :]).then_inc(self.s["h_hi_done"], 1)
        e.wait_ge(self.s["h_hi_done"], C * b + c + 1)
        e.tensor_tensor(lo[:, c, :], self.h32[:, c, :], hi[:, c, :].bitcast(F32),
                        ALU.subtract).then_inc(self.s["h_lo_done"], 1)


def attention_phase(nc, m, n, layer, x_in, x_out, w_in, gates, consts, mods):
    softmax = layer == 0
    k = consts
    wt = [m.sb(f"w_{part}", [P, 4, C, D], F32R) for part in ("hi", "lo")]
    pack = [m.sb(f"pack{i}", [P, 2, 8, S], F32R) for i in range(2)]
    split = m.sb("split", [P, 4, C, S], F32R)
    QL, KH, QH, KL = range(4)
    vaug = [m.sb(f"vaug{i}", [P, T, HEADS, 32]) for i in range(2)]
    pT = [m.sb(f"pT{i}", [P, 2, 2560]) for i in range(2)]
    norm = Norm(m, x_in, k, *mods, copies=1)
    hh, hl = norm.h[0]
    h = (hh, hl)
    oT = m.sb("oT", [P, 2, S])
    rec = m.sb("rec", [P, T * 4])
    den = m.sb("den", [P, T * 4])
    on = m.sb("on", [P, T, D])
    aT = [m.sb(f"aT_{part}", [P, C, S], F32R) for part in ("hi", "lo")]
    xres = m.sb("xres", [P, T, D])
    gated = m.sb("gated", [P, T, D])
    gate = m.sb("gate", [P, D])
    mcol = m.sb("mcol", [P, 2, 8])
    mrow = m.sb("mrow", [8, 2, P], F32R)
    if not softmax:
        low = m.sb("low", [P, S])
        ex = m.sb("ex", [P, S])
        feat = m.sb("feat", [P, S])

    nat = [m.ps(f"nat{i}") for i in range(2)]
    st = [m.ps(f"st{i}") for i in range(2)]
    pv = m.ps("pv")
    gen = [m.ps(f"gen{i}") for i in range(2)]
    mt = m.ps("mt")

    names = """w_loaded w_hi_done w_split ones_set xres_loaded gate_loaded packed0_0 packed0_1 packed1_0 packed1_1
        maxima_in0 maxima_in1 stored qk_ready v_ready nat_ready st_ready mT_ready pv_ready nrm_ready aT_ready
        o_ready qk_hi_done qk_lo_done v_done exp0_done exp1_done mrow_done pv_copied aT_hi_done aT_lo_done max_done
        rec_done on_done gated_done masking masked x_done ex_done low_done feat_done den_done"""
    s = {name: m.sem(name) for name in names.split()}

    SHARED = [("hT", 0, 1, 0), ("hT", 1, 1, 1), ("nrm", 1, -1, 3), ("qk", 0, 1, 6), ("qk", 1, 1, 8), ("qk", 2, 1, 10),
              ("nrm", 2, -1, 12), ("qk", 3, 1, 13), ("v", 0, 1, 20), ("nrm", 3, -1, 22), ("v", 1, 1, 23),
              ("aT", 0, -1, 26), ("aT", 1, -1, 28), ("o", 0, -1, 31), ("nrm", 0, 0, 33), ("o", 1, -1, 36)]
    READ = {"nrm": ("on_done", 4), "hT": (None, C), "qk": ("qk_lo_done" if softmax else "feat_done", 4),
            "v": ("v_done", 2), "aT": ("aT_lo_done", C), "o": ("gated_done", 2)}
    ACT_STEPS = {"hT": (("hT", 1),), "v": (("v", 1),), "aT": (("aT", 1),),
                 "qk": (("qk_hi", 1),) if softmax else (("ex", 1), ("qk_hi", 2))}
    DVE_STEPS = {"hT": (("hT", 1),), "nrm": (("nrm", 1),), "aT": (("aT", 1),), "o": (("o", 1),),
                 "qk": (("qk_lo", 1),) if softmax else (("feat", 1), ("qk_lo", 2))}
    OTHERS = len(SHARED)
    SLOTS = 40

    def bank_of(j):
        return gen[j % 2]

    def bank_free(e, j, b):
        at, body = j - 2, b
        while True:
            if at < 0:
                at, body = at + OTHERS, body - 1
            if isinstance(body, int) and body < -1:
                return
            what, part, off, _ = SHARED[at]
            if valid(body + off, n):
                name, per = READ[what]
                sem = norm.s["h32_done"] if name is None else s[name]
                e.wait_ge(sem, per * (body + off) + part + 1)
                return
            at -= 2

    def due(steps, b, slot_):
        for j, (what, part, off, at) in enumerate(SHARED):
            for step, later in steps.get(what, ()):
                bb = b + off - (at + later) // SLOTS
                if (at + later) % SLOTS == slot_ and valid(bb, n):
                    yield step, part, bb, bank_of(j)

    def exps_done(e, b, unit):
        for i in range(2):
            count = (unit + 1 - i + 1) // 2
            since(e, s[f"exp{i}_done"], 20 * b + count)

    def pair_of(b, p):
        return (b, p - 2) if p >= 2 else (b - 1, p + 6)

    def group_of(b, p):
        return (b, p // 2 - 2) if p >= 4 else (b - 1, p // 2 + 2)

    def slot(tile, which, slot_, g, rows, a, z):
        return tile[SLOT * slot_:SLOT * slot_ + rows, which, g, a:z]

    def where(p):
        c, u, sl = p // 4, p // 2 % 2, p % 2
        return 4 * c + 2 * u, sl

    def wstage(i):
        return pT[0][:, 0, 0:2048].rearrange("p (i c d) -> p i c d", i=4, c=C)[:, i]

    with nc.Block() as block:

        @block.sync
        def _(e):
            for i in range(4):
                e.dma_start(wstage(i), w_in[i].rearrange("(c p) n -> p c n", p=P)).then_inc(s["w_loaded"], 16)

            def body(b, par, half_b):
                if isinstance(b, int) and b == -1:
                    norm.load(e, 0)
                    e.wait_ge(s["ones_set"], 6)
                if valid(b + 2, n):
                    norm.load(e, b + 2)
                if valid(b - 1, n):
                    since(e, s["stored"], 16 * (b - 1))
                    e.dma_start(xres[:], x_in[b - 1]).then_inc(s["xres_loaded"], 16)
                    since(e, s["gated_done"], 2 * (b - 1))
                    e.dma_start(gate[:], gates[ds(b - 1, 1), :].to_broadcast([P, D])).then_inc(s["gate_loaded"], 16)
                for p in range(8):
                    if softmax:
                        bm, pm = (b, p - 1) if p else (b - 1, 7)
                        if valid(bm, n):
                            g0, sl = where(pm)
                            copy = pack[par if p else 1 - par]
                            row = copy[SLOT * sl + ONES_ROW:SLOT * sl + ONES_ROW + 1, 0, g0:g0 + 2, :]
                            e.wait_ge(s["mrow_done"], 8 * bm + pm + 1)
                            e.dma_start(row.bitcast(F32).rearrange("o g (t q) -> o (g t) q", q=P),
                                        mrow[:, pm % 2, :].bitcast(F32)).then_inc(s[f"maxima_in{pm % 2}"], 16)
                    if 3 <= p < 7 and valid(b + 1, n):
                        if p == 3:
                            since(e, s["st_ready"], 40 * b)
                            e.wait_ge(s["qk_lo_done"], 4 * (b + 2))
                        for hh in ((0, 2), (1, 3), (4, 6), (5, 7))[p - 3]:
                            sl, gg = hh % 2, hh // 2
                            done = s[f"packed{1 - par}_{hh // 4}"]
                            src = split[HD * hh:HD * hh + HD].bitcast(F32)
                            for r, qv, kv in ((0, QH, KH), (1, QH, KL), (2, QL, KH)):
                                rows = pack[1 - par][SLOT * sl + HD * r:SLOT * sl + HD * r + HD].bitcast(F32)
                                dst = rows.rearrange("p w (c g) s -> p w c g s", c=C)[:, :, :, gg, :]
                                if kv == qv + 1:
                                    e.dma_start(dst, src[:, qv:qv + 2]).then_inc(done, 16)
                                else:
                                    e.dma_start(dst[:, 0], src[:, qv]).then_inc(done, 16)
                                    e.dma_start(dst[:, 1], src[:, kv]).then_inc(done, 16)
                if valid(b - 1, n):
                    e.wait_ge(s["x_done"], 2 * b)
                    e.dma_start(x_out[b - 1], xres[:]).then_inc(s["stored"], 16)

            bodies(e, n, body)
            e.wait_ge(s["stored"], 16 * n)

        @block.gpsimd
        def _(e):
            for i in range(2):
                e.memset(pack[i][32:64, 1, :, :].bitcast(F32), 1.0).then_inc(s["ones_set"], 1)
                e.memset(pack[i][96:128, 1, :, :].bitcast(F32), 1.0).then_inc(s["ones_set"], 1)
                e.wait_ge(s["ones_set"], 3 * i + 2)
                e.memset(vaug[i][:, :, :, HD:32], 1.0).then_inc(s["ones_set"], 1)
                e.wait_ge(s["ones_set"], 3 * i + 3)

            def body(b, par, half_b):
                if isinstance(b, int) and b == -1:
                    norm.rsqrt(e, 0)
                for p in range(8):
                    if p == 6 and valid(b + 2, n):
                        norm.rsqrt(e, b + 2)
                    bp, q = pair_of(b, p)
                    if valid(bp, n):
                        exps_done(e, bp, 5 * q + 4)
                        e.sem_inc(s["masking"], 1)
                        rows = pT[q // 2 % 2][:, q % 2, :]
                        for part in (rows[:, 0:2048].rearrange("p (a x) -> p a x", a=4)[:, :, 0:P],
                                     rows[:, 0:2048].rearrange("p (a x) -> p a x", a=2)[:, :, 640:640 + P],
                                     rows[:, 2048:2560].rearrange("p (a x) -> p a x", a=2)[:, :, 0:P]):
                            e.affine_select(out=part, in_=part, pattern=[[0, part.shape[1]], [1, P]],
                                            compare_op=ALU.is_ge, fill=0.0, base=0,
                                            channel_multiplier=-1).then_inc(s["masked"], 1)
                if valid(b - 1, n):
                    for i in range(2):
                        e.wait_ge(s["gated_done"], 2 * (b - 1) + i + 1)
                        if i == 0:
                            e.wait_ge(s["xres_loaded"], 16 * b)
                        e.tensor_tensor(xres[:, 2 * i:2 * i + 2, :], xres[:, 2 * i:2 * i + 2, :],
                                        gated[:, 2 * i:2 * i + 2, :], ALU.add).then_inc(s["x_done"], 1)

            bodies(e, n, body)

        @block.scalar
        def _(e):
            def exp_unit(bp, q, u):
                i = (5 * q + u) % 2
                if softmax or i == 0:
                    if q % 2 == 0 and u < 2:
                        since(e, s["pv_ready"], 4 * bp + q // 2 - 1)
                    e.wait_ge(s["st_ready"], 40 * bp + 5 * q + u + 1)
                    dst = pT[q // 2 % 2][:, q % 2, 512 * u:512 * u + 512]
                    if softmax:
                        e.activation(dst, st[i][:], ACT.Exp, scale=float(HD) ** -0.5).then_inc(s[f"exp{i}_done"], 1)
                    else:
                        e.activation(dst, st[i][:], ACT.Copy).then_inc(s["exp0_done"], 1)

            def body(b, par, half_b):
                if isinstance(b, int) and b == -1:
                    for t in range(T):
                        norm.normalise(e, 0, t)
                for p in range(8):
                    bp, q = pair_of(b, p)
                    for u in range(5):
                        if valid(bp, n):
                            exp_unit(bp, q, u)
                        if u == 2 and softmax:
                            bm, pm = (b, p - 1) if p else (b - 1, 7)
                            if valid(bm, n):
                                e.wait_ge(s["mT_ready"], 8 * bm + pm + 1)
                                since(e, s[f"maxima_in{pm % 2}"], 16 * (4 * bm + pm // 2))
                                e.activation(mrow[:, pm % 2, :], mt[0:8, 0:P], ACT.Copy,
                                             scale=-1.0).then_inc(s["mrow_done"], 1)
                        if p % 2 == 0 and u == 0:
                            bg, G = group_of(b, p)
                            bg, G = (bg, G - 1) if G else (bg - 1, 3)
                            if valid(bg, n):
                                e.wait_ge(s["pv_ready"], 4 * bg + G + 1)
                                since(e, s["nrm_ready"], 4 * bg + G - 1)
                                e.activation(oT[:, G % 2, :], pv[:], ACT.Copy).then_inc(s["pv_copied"], 1)
                        if 5 * p + u in (32, 33, 34, 35) and valid(b + 2, n):
                            norm.normalise(e, b + 2, 5 * p + u - 32)
                        for step, part, bb, bank in due(ACT_STEPS, b, 5 * p + u):
                            if step == "hT":
                                norm.modulate(e, bb, part, bank)
                            if step == "ex":
                                e.wait_ge(s["qk_ready"], 4 * bb + part + 1)
                                since(e, s["low_done"], 4 * bb + part)
                                e.activation(ex[:], bank[:], ACT.Exp).then_inc(s["ex_done"], 1)
                            if step == "qk_hi":
                                which, c = (QH, KH)[part // 2], part % 2
                                if part == 0:
                                    since(e, s[f"packed{par}_0"], 256 * (half_b + 1))
                                    since(e, s[f"packed{par}_1"], 256 * (half_b + 1))
                                e.wait_ge(s["qk_ready" if softmax else "feat_done"], 4 * bb + part + 1)
                                e.activation(split[:, which, c, :], bank[:] if softmax else feat[:],
                                             ACT.Copy).then_inc(s["qk_hi_done"], 1)
                            if step == "v":
                                e.wait_ge(s["v_ready"], 2 * bb + part + 1)
                                if part == 0:
                                    since(e, s["pv_ready"], 4 * (bb - 1))
                                e.activation(vaug[1 - par][:, 2 * part:2 * part + 2, :, 0:HD],
                                             bank[:].rearrange("p (t h d) -> p t h d", t=2, d=HD),
                                             ACT.Copy).then_inc(s["v_done"], 1)
                            if step == "aT":
                                e.wait_ge(s["aT_ready"], C * bb + part + 1)
                                since(e, s["o_ready"], 2 * bb)
                                e.activation(aT[0][:, part, :], bank[:], ACT.Copy).then_inc(s["aT_hi_done"], 1)

            bodies(e, n, body)

        @block.vector
        def _(e):
            e.wait_ge(s["w_loaded"], 64)
            for i in range(4):
                e.tensor_copy(wt[0][:, i], wstage(i)).then_inc(s["w_hi_done"], 1)
                e.wait_ge(s["w_hi_done"], i + 1)
                e.tensor_tensor(wt[1][:, i], wstage(i), wt[0][:, i].bitcast(F32), ALU.subtract).then_inc(s["w_split"], 1)

            def maxima(b, p, u):
                unit = 40 * b + 5 * p + u
                e.wait_ge(s["nat_ready"], unit + 1)
                if u == 0:
                    since(e, s["mT_ready"], 8 * b + p - 1)
                bank, cols = nat[(5 * p + u) % 2], mcol[:, p % 2, :]
                g = u // 2
                if u < 4 and u % 2 == 0:
                    e.tensor_reduce(cols[:, 4 * g + 3:4 * g + 4], bank[:], AX_X, ALU.max).then_inc(s["max_done"], 1)
                elif u < 4:
                    e.tensor_reduce(cols[:, 4 * g:4 * g + 1], bank[:, 384:512], AX_X, ALU.max)
                    e.tensor_reduce(cols[:, 4 * g + 2:4 * g + 3], bank[:, 0:384], AX_X,
                                    ALU.max).then_inc(s["max_done"], 1)
                else:
                    e.tensor_reduce(cols[:, 1:8:4], bank[:].rearrange("p (g k) -> p g k", g=2), AX_X,
                                    ALU.max).then_inc(s["max_done"], 1)

            def copy_unit(bp, q, u):
                if (5 * q + u) % 2:
                    if q % 2 == 0 and u < 2:
                        since(e, s["pv_ready"], 4 * bp + q // 2 - 1)
                    e.wait_ge(s["st_ready"], 40 * bp + 5 * q + u + 1)
                    e.tensor_copy(pT[q // 2 % 2][:, q % 2, 512 * u:512 * u + 512],
                                  st[1][:]).then_inc(s["exp1_done"], 1)

            def body(b, par, half_b):
                if isinstance(b, int) and b == -1:
                    norm.all_statistics(e, 0)
                for slot_ in range(SLOTS):
                    p, u = slot_ // 5, slot_ % 5
                    bp, q = pair_of(b, p)
                    if softmax and valid(b, n):
                        maxima(b, p, u)
                    if not softmax and valid(bp, n):
                        copy_unit(bp, q, u)
                    if valid(b + 2, n):
                        if 25 <= slot_ < 29:
                            norm.statistics(e, b + 2, slot_ - 25)
                        if slot_ == 29:
                            norm.variance(e, b + 2)
                        if slot_ == 31:
                            norm.shift_of_mean(e, b + 2)
                    for step, part, bb, bank in due(DVE_STEPS, b, slot_):
                        if step == "hT":
                            since(e, s["v_ready"], 2 * bb)
                            norm.split(e, bb, part, 0)
                        if step == "feat":
                            e.wait_ge(s["ex_done"], 4 * bb + part + 1)
                            since(e, s["qk_lo_done"], 4 * bb + part)
                            e.tensor_scalar(low[:], ex[:], 1.0, None, ALU.min).then_inc(s["low_done"], 1)
                            e.wait_ge(s["low_done"], 4 * bb + part + 1)
                            e.scalar_tensor_tensor(feat[:], bank[:], 0.0, low[:], ALU.max,
                                                   ALU.add).then_inc(s["feat_done"], 1)
                        if step == "qk_lo":
                            hi, lo, c = (QH, KH)[part // 2], (QL, KL)[part // 2], part % 2
                            e.wait_ge(s["qk_hi_done"], 4 * bb + part + 1)
                            e.tensor_tensor(split[:, lo, c, :], bank[:] if softmax else feat[:],
                                            split[:, hi, c, :].bitcast(F32), ALU.subtract).then_inc(s["qk_lo_done"], 1)
                        if step == "nrm":
                            e.wait_ge(s["nrm_ready"], 4 * bb + part + 1)
                            heads = bank[:].rearrange("p (t h x) -> p t h x", t=T, h=4)
                            flat = bank[:].rearrange("p (a x) -> p a x", x=32)
                            src = flat[:, :, HD]
                            since(e, s["on_done"], 4 * bb + part)
                            if not softmax:
                                e.tensor_scalar(den[:], src, 1e-6, None, ALU.add).then_inc(s["den_done"], 1)
                                e.wait_ge(s["den_done"], 4 * bb + part + 1)
                                src = den[:]
                            e.reciprocal(rec[:], src).then_inc(s["rec_done"], 1)
                            e.wait_ge(s["rec_done"], 4 * bb + part + 1)
                            if part == 0:
                                since(e, s["aT_ready"], C * bb)
                            e.tensor_tensor(on[:, :, 64 * part:64 * part + 64].rearrange("p t (h x) -> p t h x", h=4),
                                            heads[:, :, :, 0:HD],
                                            rec[:].rearrange("p (t h o) -> p t h o", t=T, o=1).to_broadcast([P, T, 4, HD]),
                                            ALU.mult).then_inc(s["on_done"], 1)
                        if step == "aT":
                            e.wait_ge(s["aT_hi_done"], C * bb + part + 1)
                            e.tensor_tensor(aT[1][:, part, :], bank[:], aT[0][:, part, :].bitcast(F32),
                                            ALU.subtract).then_inc(s["aT_lo_done"], 1)
                        if step == "o":
                            e.wait_ge(s["o_ready"], 2 * bb + part + 1)
                            if part == 0:
                                e.wait_ge(s["gate_loaded"], 16 * (bb + 1))
                                since(e, s["x_done"], 2 * bb)
                            e.tensor_tensor(gated[:, 2 * part:2 * part + 2, :],
                                            bank[:].rearrange("p (t d) -> p t d", t=2),
                                            gate[:].rearrange("p (o d) -> p o d", o=1).to_broadcast([P, 2, D]),
                                            ALU.mult).then_inc(s["gated_done"], 1)

            bodies(e, n, body)

        @block.tensor
        def _(e):
            e.wait_ge(s["w_split"], 4)
            e.wait_ge(s["ones_set"], 6)

            def scores(b, p, u, par, half_b):
                g0, sl = where(p)
                if p in (0, 2) and u == 0:
                    e.wait_ge(s[f"packed{par}_{p // 2}"], 256 * (half_b + 1))
                since(e, s["max_done"], 40 * b + 5 * p + u - 1)
                bank = nat[(5 * p + u) % 2]
                parts = [[(g0, 3, 0)], [(g0, 2, 0), (g0, 0, 384)], [(g0 + 1, 3, 0)], [(g0 + 1, 2, 0), (g0 + 1, 0, 384)],
                         [(g0, 1, 0), (g0 + 1, 1, 256)]][u]
                for g, t, at in parts:
                    keys = P * (t + 1)
                    e.matmul(bank[:, at:at + keys], slot(pack[par], 0, sl, g, 48, P * t, P * t + P),
                             slot(pack[par], 1, sl, g, 48, 0, keys), start=True, stop=False, skip_group_check=True)
                    mm = e.matmul(bank[:, at + keys - P:at + keys], k["ident_bf"][:], k["neg_mask"][:], start=False,
                                  stop=True, skip_group_check=True)
                mm.then_inc(s["nat_ready"], 1)

            def scores_t(b, p, u, par, half_b):
                g0, sl = where(p)
                if u == 0 and softmax:
                    e.wait_ge(s[f"maxima_in{p % 2}"], 16 * (4 * b + p // 2 + 1))
                if u == 0 and not softmax and p in (0, 2):
                    e.wait_ge(s[f"packed{par}_{p // 2}"], 256 * (half_b + 1))
                since(e, s[f"exp{(5 * p + u) % 2}_done"], 20 * b + (5 * p + u) // 2)
                bank = st[(5 * p + u) % 2]
                parts = [[(g0, 0, 0)], [(g0, 3, 0), (g0, 1, P)], [(g0 + 1, 0, 0)], [(g0 + 1, 3, 0), (g0 + 1, 1, P)],
                         [(g0, 2, 0), (g0 + 1, 2, 256)]][u]
                rows = ONES_ROW + 1 if softmax else ONES_ROW
                for g, t, at in parts:
                    mm = e.matmul(bank[:, at:at + S - P * t], slot(pack[par], 1, sl, g, rows, P * t, P * t + P),
                                  slot(pack[par], 0, sl, g, rows, P * t, S), start=True, stop=True,
                                  skip_group_check=True)
                mm.then_inc(s["st_ready"], 1)

            def values(bg, G, js, par):
                if 0 in js:
                    e.wait_ge(s["masked"], 24 * bg + 6 * (G + 1))
                    e.wait_ge(s["v_done"], 2 * (bg + 1))
                    since(e, s["pv_copied"], 4 * bg + G)
                for j in js:
                    for hd in range(4):
                        gi, sl = hd // 2, hd % 2
                        at = [1024 * gi, 1024 * gi + 640, 2048 + 256 * gi, 1024 * gi + 512][j]
                        mm = e.matmul(pv[32 * hd:32 * hd + 32, P * j:S], vaug[par][:, j, 4 * G + hd, :],
                                      pT[G % 2][:, sl, at:at + S - P * j], start=(j == 0), stop=(j == 3),
                                      tile_position=(0, 32 * hd), skip_group_check=True)
                if 3 in js:
                    mm.then_inc(s["pv_ready"], 1)

            def shared(what, part, bb, bank):
                if what == "nrm":
                    e.wait_ge(s["pv_copied"], 4 * bb + part + 1)
                    for t in range(T):
                        mm = e.transpose(bank[:, t * P:(t + 1) * P], oT[:, part % 2, t * P:(t + 1) * P], k["ident"][:])
                    mm.then_inc(s["nrm_ready"], 1)
                if what == "hT":
                    norm.transpose(e, bb, part, bank)
                if what == "qk":
                    which, c = part // 2, part % 2
                    if part == 0:
                        e.wait_ge(norm.s["h_lo_done"], C * (bb + 1))
                    first = True
                    for a, z in PASSES:
                        for kc in range(C):
                            mm = e.matmul(bank[:], wt[a][:, which, kc, c * P:(c + 1) * P], h[z][:, kc, :],
                                          start=first, stop=(a, z, kc) == (*PASSES[-1], C - 1))
                            first = False
                    mm.then_inc(s["qk_ready"], 1)
                if what == "v":
                    for t in (2 * part, 2 * part + 1):
                        first = True
                        for a, z in PASSES:
                            for kc in range(C):
                                mm = e.matmul(bank[:, t % 2 * D:(t % 2 + 1) * D], h[z][:, kc, t * P:(t + 1) * P],
                                              wt[a][:, 2, kc, :], start=first,
                                              stop=(a, z, kc) == (*PASSES[-1], C - 1))
                                first = False
                    mm.then_inc(s["v_ready"], 1)
                if what == "aT":
                    e.wait_ge(s["on_done"], 4 * (bb + 1))
                    for t in range(T):
                        mm = e.transpose(bank[:, t * P:(t + 1) * P], on[:, t, part * P:(part + 1) * P], k["ident"][:])
                    mm.then_inc(s["aT_ready"], 1)
                if what == "o":
                    if part == 0:
                        e.wait_ge(s["aT_lo_done"], C * (bb + 1))
                    for t in (2 * part, 2 * part + 1):
                        first = True
                        for a, z in PASSES:
                            for kc in range(C):
                                mm = e.matmul(bank[:, t % 2 * D:(t % 2 + 1) * D], aT[z][:, kc, t * P:(t + 1) * P],
                                              wt[a][:, 3, kc, :], start=first,
                                              stop=(a, z, kc) == (*PASSES[-1], C - 1))
                                first = False
                    mm.then_inc(s["o_ready"], 1)

            def body(b, par, half_b):
                for p in range(8):
                    bp, q = pair_of(b, p)
                    parq = par if p >= 2 else 1 - par
                    for u in range(5):
                        if softmax and valid(b, n):
                            scores(b, p, u, par, half_b)
                        if valid(bp, n):
                            scores_t(bp, q, u, parq, half_b if p >= 2 else half_b - 1 + par)
                        if u == 2 and softmax:
                            bm, pm = (b, p - 1) if p else (b - 1, 7)
                            if valid(bm, n):
                                e.wait_ge(s["max_done"], 40 * bm + 5 * (pm + 1))
                                since(e, s["mrow_done"], 8 * bm + pm)
                                e.transpose(mt[0:8, 0:P], mcol[:, pm % 2, :], k["ident"][:]).then_inc(s["mT_ready"], 1)
                        bg, G = group_of(b, p - p % 2)
                        if u in (1, 4) and valid(bg, n):
                            values(bg, G, (p % 2 * 2 + u // 4,), par if p >= 4 else 1 - par)
                        for j, (what, part, off, at) in enumerate(SHARED):
                            if at == 5 * p + u and valid(b + off, n):
                                bank_free(e, j, b)
                                shared(what, part, b + off, bank_of(j))

            bodies(e, n, body)



def setup_phase(nc, m, n, c_in, wmod_in, consts, mods, gates):
    k = consts
    ct = [m.sb(f"ct{i}", [P, C, n]) for i in range(2)]
    ce = [m.sb(f"ce{i}", [P, C, n]) for i in range(2)]
    sc = [m.sb(f"sc{i}", [P, C, n]) for i in range(2)]
    wm = [m.sb(f"wm{i}", [P, C, 6 * D]) for i in range(2)]
    mag = m.sb("mag", [n, 2, 2 * D])
    minus = m.sb("minus", [n, 2, 2 * D])
    sign = m.sb("sign", [n, 2, 2 * D])
    guarded = m.sb("guarded", [n, 2, 2 * D])
    pm = [m.ps(f"pm{i}") for i in range(2)]
    pg = [m.ps(f"pg{i}") for i in range(2)]
    names = "loaded exp_done silu mods_ready mods_done gates_ready negated guard gates_stored blank chain"
    s = {name: m.sem(name) for name in names.split()}
    COLS = (0, 1, 3, 4)

    with nc.Block() as block:

        @block.sync
        def _(e):
            for i in range(2):
                e.dma_start(ct[i][:], c_in[i].rearrange("(c p) b -> p c b", p=P)).then_inc(s["loaded"], 16)
                e.dma_start(wm[i][:], wmod_in[i].rearrange("(c p) j -> p c j", p=P)).then_inc(s["loaded"], 16)
            e.wait_ge(s["guard"], 6)
            e.dma_start(gates.rearrange("(l g) b d -> b l g d", l=2),
                        guarded[:].rearrange("b l (g d) -> b l g d", g=2)).then_inc(s["gates_stored"], 16)
            e.wait_ge(s["gates_stored"], 16)

        @block.gpsimd
        def _(e):
            e.memset(k["ident"][:], 0.0).then_inc(s["blank"], 1)
            e.memset(k["ident_bf"][:], 0.0).then_inc(s["blank"], 1)
            e.memset(k["neg_mask"][:], 0.0).then_inc(s["blank"], 1)
            e.memset(k["minus_half"][:], -0.5).then_inc(s["blank"], 1)
            e.wait_ge(s["blank"], 4)
            for t in ("ident", "ident_bf"):
                e.affine_select(out=k[t][:], in_=k[t][:], compare_op=ALU.not_equal, fill=1.0, base=0,
                                pattern=[[-1, P]], channel_multiplier=1).then_inc(s["blank"], 1)
            e.affine_select(out=k["neg_mask"][:], in_=k["neg_mask"][:], compare_op=ALU.is_ge, fill=NEG, base=0,
                            pattern=[[-1, P]], channel_multiplier=1).then_inc(s["blank"], 1)

        @block.scalar
        def _(e):
            e.wait_ge(s["loaded"], 64)
            for i in range(2):
                e.activation(ce[i][:], ct[i][:], ACT.Exp, scale=-1.0).then_inc(s["exp_done"], 1)

        @block.vector
        def _(e):
            for i in range(2):
                e.wait_ge(s["exp_done"], i + 1)
                e.tensor_scalar(ce[i][:], ce[i][:], 1.0, None, ALU.add).then_inc(s["chain"], 1)
                e.wait_ge(s["chain"], 2 * i + 1)
                e.reciprocal(ce[i][:], ce[i][:]).then_inc(s["chain"], 1)
                e.wait_ge(s["chain"], 2 * i + 2)
                e.tensor_tensor(sc[i][:], ct[i][:], ce[i][:], ALU.mult).then_inc(s["silu"], 1)
            for i in range(2):
                e.wait_ge(s["mods_ready"], i + 1)
                for j in range(4):
                    src = pm[i][:, j * C * n:(j + 1) * C * n].rearrange("p (c b) -> p c b", c=C)
                    e.tensor_scalar(mods[i][:, j], src, float(j % 2), None, ALU.add).then_inc(s["mods_done"], 1)
                e.wait_ge(s["gates_ready"], i + 1)
                e.tensor_scalar(minus[:, i], pg[i][0:n, :], -1.0, None, ALU.mult).then_inc(s["negated"], 1)
                e.wait_ge(s["negated"], i + 1)
                e.scalar_tensor_tensor(mag[:, i], pg[i][0:n, :], 0.25, minus[:, i], ALU.max,
                                       ALU.max).then_inc(s["guard"], 1)
                e.tensor_scalar(sign[:, i], pg[i][0:n, :], 0.0, 2.0, ALU.is_ge, ALU.mult).then_inc(s["guard"], 1)
                e.wait_ge(s["guard"], 3 * i + 2)
                e.scalar_tensor_tensor(guarded[:, i], sign[:, i], -1.0, mag[:, i], ALU.add,
                                       ALU.mult).then_inc(s["guard"], 1)

        @block.tensor
        def _(e):
            for i in range(2):
                e.wait_ge(s["silu"], i + 1)
                for jj, j in enumerate(COLS):
                    for c in range(C):
                        for kc in range(C):
                            at = (jj * C + c) * n
                            mm = e.matmul(pm[i][:, at:at + n], wm[i][:, kc, j * D + c * P:j * D + (c + 1) * P],
                                          sc[i][:, kc, :], start=(kc == 0), stop=(kc == C - 1))
                mm.then_inc(s["mods_ready"], 1)
                for jj, j in enumerate((2, 5)):
                    for kc in range(C):
                        mm = e.matmul(pg[i][0:n, jj * D:(jj + 1) * D], sc[i][:, kc, :],
                                      wm[i][:, kc, j * D:(j + 1) * D], start=(kc == 0), stop=(kc == C - 1))
                mm.then_inc(s["gates_ready"], 1)


def compose(nc, m, w_ab, logits_in, w1, w2, consts):
    RING = 4
    SLOTS = TOPK // 2
    ROUNDS = TOPK // 8
    logit = m.sb("logit", [1, 2, 64])
    rest = m.sb("rest", [1, 2, 64])
    vals = m.sb("vals", [1, 2, TOPK])
    idx = m.sb("idx", [1, 2, TOPK], U32)
    shift = m.sb("shift", [1, 2])
    ew = m.sb("ew", [1, 2, TOPK])
    total = m.sb("total", [1, 2])
    rtotal = m.sb("rtotal", [1, 2])
    weight = m.sb("weight", [1, 2, TOPK])
    ones = m.sb("ones", [1, P])
    wcol = m.sb("wcol", [P, 2, SLOTS])
    a_st = m.sb("a_st", [P, RING, F])
    b_st = m.sb("b_st", [P, RING, F])
    a_w = m.sb("a_w", [P, RING, F])
    acc = [m.ps(f"acc{i}") for i in range(4)]
    pw = m.ps("pw")
    names = """logits_loaded ones_set picked exp_done weights_done spread_ready spread_done chain
        a_scaled slot_used sum_ready hi_done lo_done""" + "".join(f" st_loaded{i}" for i in range(RING))
    s = {name: m.sem(name) for name in names.split()}
    WIDTH = ((D, F), (F, D))
    out = (w1, w2)

    def hi_of(part, f, i):
        if f == 0:
            return out[0][part][:, i // 2, (i % 2) * 512:(i % 2) * 512 + 512]
        return out[1][part][:, 2 * i:2 * i + 2, :].rearrange("p a d -> p (a d)")

    with nc.Block() as block:

        @block.sync
        def _(e):
            e.dma_start(logit[:], logits_in.rearrange("(o f) x -> o f x", o=1)).then_inc(s["logits_loaded"], 16)
            e.wait_ge(s["picked"], 6 * ROUNDS - 2)

            def load(f, slot, r):
                wa, wb = WIDTH[f]
                since(e, s["slot_used"], f * SLOTS + slot - RING + 1)
                for hf in range(2):
                    which = e.value_load(idx[0:1, f, ds(slot * 2 + hf, 1)], min_val=0, max_val=63)
                    e.dma_start(a_st[64 * hf:64 * hf + 64, r, 0:wa], w_ab[f][0][ds(which, 1)].rearrange("o r x -> (o r) x")).then_inc(s[f"st_loaded{r}"], 16)
                    e.dma_start(b_st[64 * hf:64 * hf + 64, r, 0:wb], w_ab[f][1][ds(which, 1)].rearrange("o r x -> (o r) x")).then_inc(s[f"st_loaded{r}"], 16)

            for f in range(2):
                for r in range(RING):
                    load(f, r, r)
                with e.Fori(1, SLOTS // RING) as i:
                    for r in range(RING):
                        load(f, i * RING + r, r)

        @block.scalar
        def _(e):
            e.wait_ge(s["picked"], 6 * ROUNDS)
            for f in range(2):
                e.activation(ew[:, f, :], vals[:, f, :], ACT.Exp, bias=shift[:, f:f + 1],
                             accum_out=total[:, f:f + 1]).then_inc(s["exp_done"], 1)

            for f in range(2):
                for i in range(4):
                    e.wait_ge(s["sum_ready"], f + 1)
                    dst = hi_of(0, f, i)
                    e.activation(dst, acc[i][:], ACT.Copy).then_inc(s["hi_done"], 1)

        @block.vector
        def _(e):
            e.memset(ones[:], 1.0).then_inc(s["ones_set"], 1)
            e.wait_ge(s["logits_loaded"], 16)
            e.tensor_copy(rest[:], logit[:]).then_inc(s["chain"], 1)
            e.wait_ge(s["chain"], 1)
            done = 0
            for r in range(ROUNDS):
                top = slice(8 * r, 8 * r + 8)
                for f in range(2):
                    e.max(vals[:, f, top], rest[:, f, :]).then_inc(s["picked"], 1)
                done += 2
                e.wait_ge(s["picked"], done)
                for f in range(2):
                    e.max_index(idx[:, f, top], vals[:, f, top], rest[:, f, :]).then_inc(s["picked"], 1)
                done += 2
                e.wait_ge(s["picked"], done)
                if r < ROUNDS - 1:
                    for f in range(2):
                        e.match_replace(rest[:, f, :], vals[:, f, top], rest[:, f, :], -3.4e38).then_inc(s["picked"], 1)
                    done += 2
                    e.wait_ge(s["picked"], done)
            e.tensor_scalar(shift[:], vals[:, :, 0], -1.0, None, ALU.mult).then_inc(s["picked"], 2)
            assert done + 2 == 6 * ROUNDS
            e.wait_ge(s["exp_done"], 2)
            e.reciprocal(rtotal[:], total[:]).then_inc(s["weights_done"], 1)
            e.wait_ge(s["weights_done"], 1)
            for f in range(2):
                e.tensor_scalar(weight[:, f, :], ew[:, f, :], rtotal[:, f:f + 1], None, ALU.mult).then_inc(s["weights_done"], 1)
            e.wait_ge(s["spread_ready"], 1)
            for hf in range(2):
                src = pw[64 * hf:64 * hf + 64, 0:2 * TOPK].rearrange("p (f k o) -> p f k o", f=2, o=2)[:, :, :, hf]
                e.tensor_copy(wcol[64 * hf:64 * hf + 64], src).then_inc(s["spread_done"], 1)
            e.wait_ge(s["spread_done"], 2)

            def scale_a(f, slot, r, round_):
                wa, _ = WIDTH[f]
                e.wait_ge(s[f"st_loaded{r}"], 64 * (round_ + 1))
                e.tensor_scalar(a_w[:, r, 0:wa], a_st[:, r, 0:wa], wcol[:, f, ds(slot, 1)], None,
                                ALU.mult).then_inc(s["a_scaled"], 1)

            for f in range(2):
                for r in range(RING):
                    scale_a(f, r, r, f * SLOTS // RING)
                with e.Fori(1, SLOTS // RING) as i:
                    for r in range(RING):
                        scale_a(f, i * RING + r, r, f * SLOTS // RING + i)
                for i in range(4):
                    e.wait_ge(s["hi_done"], 4 * f + i + 1)
                    e.tensor_tensor(hi_of(1, f, i), acc[i][:], hi_of(0, f, i).bitcast(F32),
                                    ALU.subtract).then_inc(s["lo_done"], 1)

        @block.tensor
        def _(e):
            e.wait_ge(s["ones_set"], 1)
            e.wait_ge(s["weights_done"], 3)
            e.matmul(pw[:, 0:2 * TOPK], ones[:], weight[:].rearrange("o f k -> o (f k)"), start=True,
                     stop=True).then_inc(s["spread_ready"], 1)

            def multiply(f, slot, r, first):
                e.wait_ge(s["a_scaled"], f * SLOTS + slot + 1)
                if f == 0:
                    for c in range(C):
                        for hf in range(2):
                            mm = e.matmul(acc[2 * c + hf][:], a_w[:, r, c * P:(c + 1) * P],
                                          b_st[:, r, hf * 512:hf * 512 + 512], start=first, stop=False,
                                          skip_group_check=True)
                else:
                    for ft in range(FT):
                        mm = e.matmul(acc[ft // 2][:, ft % 2 * D:(ft % 2 + 1) * D], a_w[:, r, ft * P:(ft + 1) * P],
                                      b_st[:, r, 0:D], start=first and ft % 2 == 0, stop=False,
                                      skip_group_check=True)
                return mm

            for f in range(2):
                since(e, s["lo_done"], 4 * f)
                for r in range(RING):
                    multiply(f, r, r, r == 0).then_inc(s["slot_used"], 1)
                with e.Fori(1, SLOTS // RING - 1) as i:
                    for r in range(RING):
                        multiply(f, i * RING + r, r, False).then_inc(s["slot_used"], 1)
                for r in range(RING):
                    mm = multiply(f, SLOTS - RING + r, r, False)
                    mm.then_inc(s["slot_used"], 1)
                e.matmul(pw[:, 0:2 * TOPK], ones[:], weight[:].rearrange("o f k -> o (f k)"), start=True,
                         stop=True).then_inc(s["sum_ready"], 1)


class Residual:

    def __init__(self, m, x_in, x_out, gates, read_sem):
        self.x_in, self.x_out, self.gates = x_in, x_out, gates
        self.x = m.sb("res_x", [P, T, D])
        self.gated = m.sb("res_gated", [P, T, D])
        self.gate = m.sb("res_gate", [P, D])
        self.s = {name: m.sem(f"res_{name}") for name in ("x_loaded", "gate_loaded", "gated_done", "x_done", "stored")}

    def load(self, e, b):
        since(e, self.s["stored"], 16 * b)
        e.dma_start(self.x[:], self.x_in[b]).then_inc(self.s["x_loaded"], 16)
        since(e, self.s["gated_done"], 2 * b)
        e.dma_start(self.gate[:], self.gates[ds(b, 1), :].to_broadcast([P, D])).then_inc(self.s["gate_loaded"], 16)

    def multiply(self, e, b, part, product):
        if part == 0:
            e.wait_ge(self.s["gate_loaded"], 16 * (b + 1))
            since(e, self.s["x_done"], 2 * b)
        e.tensor_tensor(self.gated[:, 2 * part:2 * part + 2, :], product,
                        self.gate[:].rearrange("p (o d) -> p o d", o=1).to_broadcast([P, 2, D]),
                        ALU.mult).then_inc(self.s["gated_done"], 1)

    def add(self, e, b, part):
        e.wait_ge(self.s["gated_done"], 2 * b + part + 1)
        if part == 0:
            e.wait_ge(self.s["x_loaded"], 16 * (b + 1))
        rows = slice(2 * part, 2 * part + 2)
        e.tensor_tensor(self.x[:, rows, :], self.x[:, rows, :], self.gated[:, rows, :],
                        ALU.add).then_inc(self.s["x_done"], 1)

    def store(self, e, b):
        e.wait_ge(self.s["x_done"], 2 * (b + 1))
        e.dma_start(self.x_out[b], self.x[:]).then_inc(self.s["stored"], 16)


def ffn_phase(nc, m, n, x_in, x_out, w_ab, logits_in, gates, consts, mods):
    w1 = [m.sb(f"w1_{part}", [P, C, F], F32R) for part in ("hi", "lo")]
    w2 = [m.sb(f"w2_{part}", [P, FT, D], F32R) for part in ("hi", "lo")]
    with Memory(nc, "comp") as own:
        compose(nc, own, w_ab, logits_in, w1, w2, consts)

    norm = Norm(m, x_in, consts, *mods, copies=2)
    res = Residual(m, x_in, x_out, gates, None)
    RING = 4
    g32 = m.sb("g32", [P, 2, S])
    g = [m.sb(f"g_{part}", [P, RING, S], F32R) for part in ("hi", "lo")]
    up = [m.ps(f"up{i}") for i in range(2)]
    down = [[m.ps(f"down{i}{j}") for j in range(2)] for i in range(2)]
    hT = [m.ps(f"hT{i}") for i in range(2)]
    names = "up_ready gelu_done g_hi_done g_lo_done down_ready"
    s = {name: m.sem(name) for name in names.split()}

    with nc.Block() as block:

        @block.sync
        def _(e):
            def body(b, par, half_b):
                if isinstance(b, int) and b == -1:
                    norm.load(e, 0)
                if valid(b + 2, n):
                    norm.load(e, b + 2)
                if valid(b - 1, n):
                    res.load(e, b - 1)
                    res.store(e, b - 1)

            bodies(e, n, body)
            e.wait_ge(res.s["stored"], 16 * n)

        @block.gpsimd
        def _(e):
            def body(b, par, half_b):
                if valid(b + 1, n):
                    norm.rsqrt(e, b + 1)
                if valid(b - 1, n):
                    res.add(e, b - 1, 0)
                    res.add(e, b - 1, 1)

            bodies(e, n, body)

        @block.scalar
        def _(e):
            def body(b, par, half_b):
                for j in range(FT):
                    if j == 2 and valid(b + 1, n):
                        for t in range(T):
                            norm.normalise(e, b + 1, t)
                    if valid(b, n):
                        e.wait_ge(s["up_ready"], FT * b + j + 1)
                        since(e, s["g_lo_done"], FT * b + j - 1)
                        e.activation(g32[:, j % 2, :], up[j % 2][:], ACT.Gelu_apprx_tanh).then_inc(s["gelu_done"], 1)
                    if j == 5 and valid(b + 1, n):
                        for c in range(C):
                            norm.modulate(e, b + 1, c, hT[c])

            bodies(e, n, body)

        @block.vector
        def _(e):
            def body(b, par, half_b):
                for j in range(FT):
                    if j == 0 and valid(b + 1, n):
                        norm.all_statistics(e, b + 1)
                    if j == 2 and valid(b - 1, n):
                        for part in range(2):
                            e.wait_ge(s["down_ready"], FT * b)
                            res.multiply(e, b - 1, part, down[1 - par][part][:].rearrange("p (t d) -> p t d", t=2))
                    if valid(b, n):
                        e.wait_ge(s["gelu_done"], FT * b + j + 1)
                        since(e, s["down_ready"], FT * b + j - RING + 1)
                        e.tensor_copy(g[0][:, j % RING, :], g32[:, j % 2, :]).then_inc(s["g_hi_done"], 1)
                        e.wait_ge(s["g_hi_done"], FT * b + j + 1)
                        e.tensor_tensor(g[1][:, j % RING, :], g32[:, j % 2, :], g[0][:, j % RING, :].bitcast(F32),
                                        ALU.subtract).then_inc(s["g_lo_done"], 1)
                    if j == 5 and valid(b + 1, n):
                        since(e, s["up_ready"], FT * b)
                        for c in range(C):
                            norm.split(e, b + 1, c, 1 - par)

            bodies(e, n, body)

        @block.tensor
        def _(e):
            def up_tile(b, j, par):
                if j == 0:
                    e.wait_ge(norm.s["h_lo_done"], C * (b + 1))
                since(e, s["gelu_done"], FT * b + j - 1)
                first = True
                for a, z in PASSES:
                    for kc in range(C):
                        mm = e.matmul(up[j % 2][:], w1[a][:, kc, j * P:(j + 1) * P], norm.h[par][z][:, kc, :],
                                      start=first, stop=(a, z, kc) == (*PASSES[-1], C - 1))
                        first = False
                mm.then_inc(s["up_ready"], 1)

            def down_tile(b, j, par):
                e.wait_ge(s["g_lo_done"], FT * b + j + 1)
                if j == 0:
                    since(e, res.s["gated_done"], 2 * (b - 1))
                for t in range(T):
                    bank = down[par][t // 2]
                    for i, (a, z) in enumerate(PASSES):
                        mm = e.matmul(bank[:, t % 2 * D:(t % 2 + 1) * D], g[z][:, j % RING, t * P:(t + 1) * P],
                                      w2[a][:, j, :], start=(i == 0 and j == 0 and t % 2 == 0),
                                      stop=(j == FT - 1 and i == 2), skip_group_check=True)
                mm.then_inc(s["down_ready"], 1)

            def body(b, par, half_b):
                for j in range(FT):
                    if valid(b, n):
                        up_tile(b, j, par)
                    if j < 2 and valid(b - 1, n):
                        down_tile(b - 1, FT - 2 + j, 1 - par)
                    if j >= 2 and valid(b, n):
                        down_tile(b, j - 2, par)
                    if j == 5 and valid(b + 1, n):
                        for c in range(C):
                            since(e, norm.s["h32_done"], C * (b + 1))
                            norm.transpose(e, b + 1, c, hT[c])

            bodies(e, n, body)


def linear_phase(nc, m, n, x_in, x_out, w_t, bias, low_rank, gates, consts, mods):
    lora_down_t, down_aux, lora_up_t, up_aux_t = low_rank
    rank, dd, ud = lora_down_t.shape[1], lora_down_t.shape[0], lora_up_t.shape[1]
    w = [m.sb(f"w_{part}", [P, C, D], F32R) for part in ("hi", "lo")]
    base = m.sb("base", [P, C, D])
    whole = m.sb("whole", [P, C, D])
    ldt = m.sb("ldt", [dd, rank])
    da = m.sb("da", [dd, D])
    lut = m.sb("lut", [rank, ud])
    uat = m.sb("uat", [ud, D])
    t1 = m.sb("t1", [rank, D])
    t2 = m.sb("t2", [ud, D])
    bias_b = m.sb("bias_b", [P, D])
    norm = Norm(m, x_in, consts, *mods, copies=2)
    res = Residual(m, x_in, x_out, gates, None)
    biased = m.sb("biased", [P, 2, 2, D])
    out = [[m.ps(f"out{i}{j}") for j in range(2)] for i in range(2)]
    hT = [m.ps(f"hT{i}") for i in range(2)]
    names = "w_loaded t1_ready t1_done t2_ready t2_done w_ready whole_done w_hi_done w_split out_ready biased_done"
    s = {name: m.sem(name) for name in names.split()}

    with nc.Block() as block:

        @block.sync
        def _(e):
            for dst, src in ((base[:], w_t.rearrange("(c p) n -> p c n", p=P)), (ldt[:], lora_down_t), (da[:], down_aux),
                             (lut[:], lora_up_t), (uat[:], up_aux_t), (bias_b[:], bias.to_broadcast([P, D]))):
                e.dma_start(dst, src).then_inc(s["w_loaded"], 16)

            def body(b, par, half_b):
                if isinstance(b, int) and b == -1:
                    norm.load(e, 0)
                if valid(b + 2, n):
                    norm.load(e, b + 2)
                if valid(b, n):
                    res.load(e, b)
                    res.store(e, b)

            bodies(e, n, body)
            e.wait_ge(res.s["stored"], 16 * n)

        @block.gpsimd
        def _(e):
            def body(b, par, half_b):
                if valid(b + 1, n):
                    norm.rsqrt(e, b + 1)
                if valid(b, n):
                    res.add(e, b, 0)
                    res.add(e, b, 1)

            bodies(e, n, body)

        @block.scalar
        def _(e):
            def body(b, par, half_b):
                if valid(b + 1, n):
                    for t in range(T):
                        norm.normalise(e, b + 1, t)
                    for c in range(C):
                        norm.modulate(e, b + 1, c, hT[c])

            bodies(e, n, body)

        @block.vector
        def _(e):
            e.wait_ge(s["t1_ready"], 1)
            e.tensor_copy(t1[:], out[0][0][0:rank, 0:D]).then_inc(s["t1_done"], 1)
            e.wait_ge(s["t2_ready"], 1)
            e.tensor_copy(t2[:], out[0][0][0:ud, 0:D]).then_inc(s["t2_done"], 1)
            e.wait_ge(s["w_ready"], 1)
            e.tensor_tensor(whole[:], out[0][1][:].rearrange("p (c d) -> p c d", c=C), base[:],
                            ALU.add).then_inc(s["whole_done"], 1)
            e.wait_ge(s["whole_done"], 1)
            e.tensor_copy(w[0][:], whole[:]).then_inc(s["w_hi_done"], 1)
            e.wait_ge(s["w_hi_done"], 1)
            e.tensor_tensor(w[1][:], whole[:], w[0][:].bitcast(F32), ALU.subtract).then_inc(s["w_split"], 1)

            def body(b, par, half_b):
                if valid(b + 1, n):
                    norm.all_statistics(e, b + 1)
                if valid(b, n):
                    for part in range(2):
                        e.wait_ge(s["out_ready"], 2 * b + part + 1)
                        e.tensor_tensor(biased[:, part], out[par][part][:].rearrange("p (t d) -> p t d", t=2),
                                        bias_b[:].rearrange("p (o d) -> p o d", o=1).to_broadcast([P, 2, D]),
                                        ALU.add).then_inc(s["biased_done"], 1)
                    for part in range(2):
                        e.wait_ge(s["biased_done"], 2 * b + part + 1)
                        res.multiply(e, b, part, biased[:, part])
                if valid(b + 1, n):
                    since(e, s["out_ready"], 2 * b)
                    for c in range(C):
                        norm.split(e, b + 1, c, 1 - par)

            bodies(e, n, body)

        @block.tensor
        def _(e):
            e.wait_ge(s["w_loaded"], 96)
            e.matmul(out[0][0][0:rank, 0:D], ldt[:], da[:], start=True, stop=True).then_inc(s["t1_ready"], 1)
            e.wait_ge(s["t1_done"], 1)
            e.matmul(out[0][0][0:ud, 0:D], lut[:], t1[:], start=True, stop=True).then_inc(s["t2_ready"], 1)
            e.wait_ge(s["t2_done"], 1)
            for c in range(C):
                mm = e.matmul(out[0][1][:, c * D:(c + 1) * D], t2[:, c * P:(c + 1) * P], uat[:], start=True, stop=True)
            mm.then_inc(s["w_ready"], 1)
            e.wait_ge(s["w_split"], 1)

            def body(b, par, half_b):
                if valid(b + 1, n):
                    for c in range(C):
                        since(e, norm.s["h32_done"], C * (b + 1))
                        norm.transpose(e, b + 1, c, hT[c])
                if valid(b, n):
                    e.wait_ge(norm.s["h_lo_done"], C * (b + 1))
                    since(e, s["biased_done"], 2 * (b - 1))
                    for part in range(2):
                        for t in (2 * part, 2 * part + 1):
                            first = True
                            for a, z in PASSES:
                                for kc in range(C):
                                    mm = e.matmul(out[par][part][:, t % 2 * D:(t % 2 + 1) * D],
                                                  norm.h[par][z][:, kc, t * P:(t + 1) * P], w[a][:, kc, :], start=first,
                                                  stop=(a, z, kc) == (*PASSES[-1], C - 1))
                                    first = False
                        mm.then_inc(s["out_ready"], 1)

            bodies(e, n, body)


def program(nc, a, out):
    n = a["x"].shape[0]
    shape = [n, P, T, D]
    mid = [nc.dram_tensor(f"x_after{i}", shape, F32, kind="Internal").ap() for i in range(3)]
    gates = nc.dram_tensor("gates", [4, n, D], F32, kind="Internal").ap()
    with Memory(nc, "top") as top:
        consts = {"ident": top.sb("ident", [P, P]), "ident_bf": top.sb("ident_bf", [P, P], BF16),
                  "neg_mask": top.sb("neg_mask", [P, P], BF16), "minus_half": top.sb("minus_half", [P, T])}
        mods = [top.sb(f"mods{i}", [P, 4, C, n]) for i in range(2)]

        def pair(layer, which):
            return mods[layer][:, 2 * which + 1], mods[layer][:, 2 * which]

        with Memory(nc, "set") as m:
            setup_phase(nc, m, n, a["c"], a["wmod"], consts, mods, gates)
        with Memory(nc, "soft") as m:
            attention_phase(nc, m, n, 0, a["x"], mid[0], a["w_attn0"], gates[0], consts, pair(0, 0))
        with Memory(nc, "ffn") as m:
            ffn_phase(nc, m, n, mid[0], mid[1], ((a["a1"], a["b1"]), (a["a2"], a["b2"])), a["logits"], gates[1], consts,
                      pair(0, 1))
        with Memory(nc, "lin") as m:
            attention_phase(nc, m, n, 1, mid[1], mid[2], a["w_attn1"], gates[2], consts, pair(1, 0))
        with Memory(nc, "out") as m:
            linear_phase(nc, m, n, mid[2], out, a["w_lin"], a["bias"],
                         (a["lora_down_t"], a["down_aux"], a["lora_up_t"], a["up_aux_t"]), gates[3], consts, pair(1, 1))


def kernel(**inputs):
    import concourse.bacc as bacc
    from concourse.bass_utils import run_bass_kernel_spmd

    v = {name: np.asarray(x) for name, x in inputs.items()}
    n = v["L0_attn_x"].shape[0]
    flip = lambda x: np.ascontiguousarray(np.swapaxes(x, -1, -2))
    arrays = {
        "x": np.ascontiguousarray(v["L0_attn_x"].reshape(n, T, P, D).transpose(0, 2, 1, 3)),
        "c": np.stack([flip(v["L0_c"]), flip(v["L1_c"])]),
        "wmod": np.stack([v["L0_wmod"], v["L1_wmod"]]),
        "w_attn0": np.stack([flip(v[f"L0_attn_{x}_proj_weight"]) for x in "qkvo"]),
        "w_attn1": np.stack([v["L1_attn_w_attn"][:, i * D:(i + 1) * D] for i in range(3)] + [v["L1_attn_w_proj"]]),
        "a1": flip(v["L0_ffn_fc1_A"]), "b1": v["L0_ffn_fc1_B"], "a2": flip(v["L0_ffn_fc2_A"]), "b2": v["L0_ffn_fc2_B"],
        "logits": np.stack([v["L0_ffn_fc1_logits"], v["L0_ffn_fc2_logits"]]),
        "w_lin": flip(v["L1_ffn_W"]), "bias": v["L1_ffn_b"].reshape(1, D),
        "lora_down_t": flip(v["L1_ffn_lora_down"]), "down_aux": v["L1_ffn_down_aux"],
        "lora_up_t": flip(v["L1_ffn_lora_up"]), "up_aux_t": flip(v["L1_ffn_up_aux"]),
    }
    nc = bacc.Bacc("TRN2", target_bir_lowering=False, num_devices=1)
    aps = {name: nc.dram_tensor(f"in_{name}", x.shape, mybir.dt.from_np(x.dtype), kind="ExternalInput").ap()
           for name, x in arrays.items()}
    out = nc.dram_tensor("out", arrays["x"].shape, F32, kind="ExternalOutput").ap()
    program(nc, aps, out)
    r = run_bass_kernel_spmd(nc, [{f"in_{name}": x for name, x in arrays.items()}], core_ids=[0])
    y = r.results[0]["out"]
    return np.ascontiguousarray(y.transpose(0, 2, 1, 3)).reshape(n, T * P, D)
```

```python
from contextlib import ExitStack

import numpy as np

import concourse.bass as bass
from concourse import mybir

ALU = mybir.AluOpType
ACT = mybir.ActivationFunctionType
F32 = mybir.dt.float32
F32R = mybir.dt.float32r
BF16 = mybir.dt.bfloat16
U32 = mybir.dt.uint32
AX_X = mybir.AxisListType.X

P = 128
D = 256
C = D // P
S = 512
T = S // P
HEADS = 16
HD = D // HEADS
F = 1024
FT = F // P
TOPK = 32
RANK = 64
SLOT = 64
ONES_ROW = 48
NEG = -1e30
LN_EPS = 1e-5
PASSES = ((0, 0), (1, 0), (0, 1))

ds = bass.ds


def since(e, sem, n):
    if not isinstance(n, int) or n > 0:
        e.wait_ge(sem, n)


class Memory:

    def __init__(self, nc, prefix):
        self.nc, self.prefix, self.tensors, self.semaphores = nc, prefix, ExitStack(), []

    def __enter__(self):
        return self

    def __exit__(self, *error):
        if error[0] is None:
            self.nc.all_engine_barrier()
            self.nc.clear_and_free_semaphores(self.semaphores)
            self.nc.all_engine_barrier()
        self.tensors.close()

    def sb(self, name, shape, dt=F32):
        return self.tensors.enter_context(self.nc.sbuf_tensor(f"{self.prefix}_{name}", shape, dt))

    def ps(self, name, shape=(P, 512), dt=F32):
        return self.tensors.enter_context(self.nc.psum_tensor(f"{self.prefix}_{name}", list(shape), dt))

    def sem(self, name):
        self.semaphores.append(self.nc.alloc_semaphore(name=f"{self.prefix}_{name}"))
        return self.semaphores[-1]


def bodies(e, n, body, ahead=2):
    pairs = max(0, (n - 2 - ahead) // 2)
    for b in (-1, 0, 1):
        body(b, b % 2, b // 2)
    if pairs:
        with e.Fori(0, pairs) as i:
            body(i * 2 + 2, 0, i + 1)
            body(i * 2 + 3, 1, i + 1)
    for b in range(2 + 2 * pairs, n + 1):
        body(b, b % 2, b // 2)


def valid(b, n):
    return not isinstance(b, int) or 0 <= b < n


class Stream:

    def __init__(self, m, x_in, x_out, gates):
        self.x_in, self.x_out, self.gates, self.n = x_in, x_out, gates, x_in.shape[0]
        self.x = m.sb("x", [P, self.n, T, D])
        self.gated = m.sb("gated", [P, T, D])
        self.gate = m.sb("gate", [P, self.n, D])
        names = "x_loaded0 x_loaded1 gates_loaded gated_done x_done stored"
        self.s = {name: m.sem(name) for name in names.split()}

    def load_gates(self, e):
        e.dma_start(self.gate[:], self.gates.rearrange("(o b) d -> o b d", o=1).to_broadcast([P, self.n, D])).then_inc(
            self.s["gates_loaded"], 16)

    def load(self, e, b, par, half_b):
        since(e, self.s[f"x_loaded{par}"], 16 * half_b)
        e.dma_start(self.x[:, ds(b, 1)].rearrange("p o t d -> p (o t) d"),
                    self.x_in[ds(b, 1)].rearrange("o p t d -> p (o t) d")).then_inc(self.s[f"x_loaded{par}"], 16)

    def loaded(self, e, par, half_b):
        e.wait_ge(self.s[f"x_loaded{par}"], 16 * (half_b + 1))

    def multiply(self, e, b, part, bank):
        if part == 0:
            e.wait_ge(self.s["gates_loaded"], 16)
            since(e, self.s["x_done"], 2 * b)
        e.tensor_tensor(self.gated[:, 2 * part:2 * part + 2, :], bank[:].rearrange("p (t d) -> p t d", t=2),
                        self.gate[:, ds(b, 1), :].to_broadcast([P, 2, D]), ALU.mult).then_inc(self.s["gated_done"], 1)

    def add(self, e, b, part):
        e.wait_ge(self.s["gated_done"], 2 * b + part + 1)
        rows = slice(2 * part, 2 * part + 2)
        x = self.x[:, ds(b, 1), rows, :].rearrange("p o t d -> p (o t) d")
        e.tensor_tensor(x, x, self.gated[:, rows, :], ALU.add).then_inc(self.s["x_done"], 1)

    def store(self, e, b):
        e.wait_ge(self.s["x_done"], 2 * (b + 1))
        e.dma_start(self.x_out[ds(b, 1)].rearrange("o p t d -> p (o t) d"),
                    self.x[:, ds(b, 1)].rearrange("p o t d -> p (o t) d")).then_inc(self.s["stored"], 16)


class Norm:

    def __init__(self, m, x_in, consts, scale, shift, copies):
        self.x_in, self.k, self.scale, self.shift = x_in, consts, scale, shift
        self.stream = x_in if isinstance(x_in, Stream) else None
        self.x = self.stream.x if self.stream else m.sb("ln_x", [P, T, D])
        self.stats = m.sb("ln_stats", [P, T, 6])
        self.mv = m.sb("ln_mv", [P, T, 2])
        self.veps = m.sb("ln_veps", [P, T])
        self.rstd = m.sb("ln_rstd", [P, T])
        self.nmr = m.sb("ln_nmr", [P, T])
        self.n = m.sb("ln_n", [P, T, D])
        self.h32 = m.sb("ln_h32", [P, C, S])
        self.h = [[m.sb(f"ln_h{i}_{part}", [P, C, S], F32R) for part in ("hi", "lo")] for i in range(copies)]
        self.s = {}
        for name in ("x_loaded", "bn_done", "aggregating", "mv_done", "veps_done", "rstd_done", "nmr_done", "normed",
                     "hT_ready", "h32_done", "h_hi_done", "h_lo_done"):
            self.s[name] = m.sem(f"ln_{name}")

    def load(self, e, b):
        since(e, self.s["normed"], T * b)
        e.dma_start(self.x[:], self.x_in[b]).then_inc(self.s["x_loaded"], 16)

    def rows(self, b, t):
        return self.x[:, ds(b, 1), t, :].rearrange("p o d -> p (o d)") if self.stream else self.x[:, t, :]

    def statistics(self, e, b, t):
        if t == 0:
            if not self.stream:
                e.wait_ge(self.s["x_loaded"], 16 * (b + 1))
            since(e, self.s["mv_done"], T * b)
        e.bn_stats(self.stats[:, t, :], self.rows(b, t)).then_inc(self.s["bn_done"], 1)

    def variance(self, e, b):
        since(e, self.s["normed"], T * b)
        e.wait_ge(self.s["bn_done"], T * (b + 1))
        e.sem_inc(self.s["aggregating"], 1)
        for t in range(T):
            e.bn_aggr(self.mv[:, t, :], self.stats[:, t, :]).then_inc(self.s["mv_done"], 1)
        e.wait_ge(self.s["mv_done"], T * (b + 1))
        e.tensor_scalar(self.veps[:], self.mv[:, :, 1], LN_EPS, None, ALU.add).then_inc(self.s["veps_done"], 1)

    def rsqrt(self, e, b):
        e.wait_ge(self.s["veps_done"], b + 1)
        e.tensor_tensor(self.rstd[:], self.veps[:], self.k["minus_half"][:], ALU.pow).then_inc(self.s["rstd_done"], 1)

    def shift_of_mean(self, e, b):
        e.wait_ge(self.s["rstd_done"], b + 1)
        e.scalar_tensor_tensor(self.nmr[:], self.mv[:, :, 0], -1.0, self.rstd[:], ALU.mult,
                               ALU.mult).then_inc(self.s["nmr_done"], 1)

    def all_statistics(self, e, b):
        for t in range(T):
            self.statistics(e, b, t)
        self.variance(e, b)
        self.shift_of_mean(e, b)

    def normalise(self, e, b, t):
        if t == 0:
            e.wait_ge(self.s["nmr_done"], b + 1)
            since(e, self.s["hT_ready"], C * b)
        e.activation(self.n[:, t, :], self.rows(b, t), ACT.Identity, scale=self.rstd[:, t:t + 1],
                     bias=self.nmr[:, t:t + 1]).then_inc(self.s["normed"], 1)

    def transpose(self, e, b, c, bank):
        e.wait_ge(self.s["normed"], T * (b + 1))
        for t in range(T):
            mm = e.transpose(bank[:, t * P:(t + 1) * P], self.n[:, t, c * P:(c + 1) * P], self.k["ident"][:])
        mm.then_inc(self.s["hT_ready"], 1)

    def modulate(self, e, b, c, bank):
        e.wait_ge(self.s["hT_ready"], C * b + c + 1)
        since(e, self.s["h_lo_done"], C * (b - 1) + c + 1)
        e.activation(self.h32[:, c, :], bank[:], ACT.Identity, scale=self.scale[:, c, ds(b, 1)],
                     bias=self.shift[:, c, ds(b, 1)]).then_inc(self.s["h32_done"], 1)

    def modulate_hi(self, e, b, c, bank, copy):
        e.activation(self.h[copy][0][:, c, :], bank[:], ACT.Identity, scale=self.scale[:, c, ds(b, 1)],
                     bias=self.shift[:, c, ds(b, 1)]).then_inc(self.s["h_hi_done"], 1)

    def lo(self, e, b, c, copy):
        hi, lo = self.h[copy]
        e.wait_ge(self.s["h32_done"], C * b + c + 1)
        e.wait_ge(self.s["h_hi_done"], C * b + c + 1)
        e.tensor_tensor(lo[:, c, :], self.h32[:, c, :], hi[:, c, :].bitcast(F32),
                        ALU.subtract).then_inc(self.s["h_lo_done"], 1)

    def split(self, e, b, c, copy):
        hi, lo = self.h[copy]
        e.wait_ge(self.s["h32_done"], C * b + c + 1)
        e.tensor_copy(hi[:, c, :], self.h32[:, c, :]).then_inc(self.s["h_hi_done"], 1)
        e.wait_ge(self.s["h_hi_done"], C * b + c + 1)
        e.tensor_tensor(lo[:, c, :], self.h32[:, c, :], hi[:, c, :].bitcast(F32),
                        ALU.subtract).then_inc(self.s["h_lo_done"], 1)


def attention_phase(nc, m, n, layer, x_in, x_out, w_in, gates, consts, mods):
    softmax = layer == 0
    k = consts
    wt = [m.sb(f"w_{part}", [P, 4, C, D], F32R) for part in ("hi", "lo")]
    pack = [m.sb(f"pack{i}", [P, 2, 8, S], F32R) for i in range(2)]
    split = m.sb("split", [P, 4, C, S], F32R)
    QL, KH, QH, KL = range(4)
    vaug = [m.sb(f"vaug{i}", [P, T, HEADS, 32]) for i in range(2)]
    pT = [m.sb(f"pT{i}", [P, 2, 2560]) for i in range(2)]
    norm = Norm(m, x_in, k, *mods, copies=1)
    hh, hl = norm.h[0]
    h = (hh, hl)
    oT = m.sb("oT", [P, 2, S])
    rec = m.sb("rec", [P, T * 4])
    den = m.sb("den", [P, T * 4])
    on = m.sb("on", [P, T, D])
    aT = [m.sb(f"aT_{part}", [P, C, S], F32R) for part in ("hi", "lo")]
    xres = m.sb("xres", [P, T, D])
    gated = m.sb("gated", [P, T, D])
    gate = m.sb("gate", [P, D])
    mcol = m.sb("mcol", [P, 2, 8])
    mrow = m.sb("mrow", [8, 2, P], F32R)
    if not softmax:
        low = m.sb("low", [P, S])
        ex = m.sb("ex", [P, S])
        feat = m.sb("feat", [P, S])

    nat = [m.ps(f"nat{i}") for i in range(2)] if softmax else []
    st = [m.ps(f"st{i}") for i in range(2 if softmax else 4)]
    pv = m.ps("pv")
    gen = [m.ps(f"gen{i}") for i in range(2)]
    mt = m.ps("mt")

    names = """w_loaded w_hi_done w_split ones_set xres_loaded gate_loaded packed0_0 packed0_1 packed1_0 packed1_1
        maxima_in0 maxima_in1 stored qk_ready v_ready nat_ready st_ready mT_ready pv_ready nrm_ready aT_ready
        o_ready qk_hi_done qk_lo_done v_done exp0_done exp1_done mrow_done pv_copied aT_hi_done aT_lo_done max_done
        rec_done on_done gated_done masking masked x_done ex_done low_done feat_done den_done"""
    s = {name: m.sem(name) for name in names.split()}

    SHARED = [("hT", 0, 1, 0), ("hT", 1, 1, 1), ("nrm", 1, -1, 3), ("qk", 0, 1, 5), ("qk", 1, 1, 8), ("qk", 2, 1, 10),
              ("qk", 3, 1, 13), ("nrm", 2, -1, 15), ("v", 0, 1, 18), ("v", 1, 1, 20), ("nrm", 3, -1, 23),
              ("aT", 0, -1, 25), ("aT", 1, -1, 26), ("o", 0, -1, 30), ("nrm", 0, 0, 33), ("o", 1, -1, 35)]
    READ = {"nrm": ("on_done", 4), "hT": (None, C), "qk": ("qk_lo_done" if softmax else "feat_done", 4),
            "v": ("v_done", 2), "aT": ("aT_lo_done", C), "o": ("gated_done", 2)}
    ACT_STEPS = {"hT": (("hT", 1),), "v": (("v", 1),), "aT": (("aT", 1),),
                 "qk": (("qk_hi", 1),) if softmax else (("ex", 1), ("qk_hi", 2))}
    DVE_STEPS = {"hT": (("hT", 1),), "nrm": (("nrm", 1),), "aT": (("aT", 1),), "o": (("o", 1),),
                 "qk": (("qk_lo", 1),) if softmax else (("feat", 1), ("qk_lo", 2))}
    STATISTICS = (12, 14, 17, 19)
    OTHERS = len(SHARED)
    SLOTS = 40

    def bank_of(j):
        return gen[j % 2]

    def bank_free(e, j, b):
        at, body = j - 2, b
        while True:
            if at < 0:
                at, body = at + OTHERS, body - 1
            if isinstance(body, int) and body < -1:
                return
            what, part, off, _ = SHARED[at]
            if valid(body + off, n):
                name, per = READ[what]
                sem = norm.s["h32_done"] if name is None else s[name]
                e.wait_ge(sem, per * (body + off) + part + 1)
                return
            at -= 2

    def due(steps, b, slot_):
        for j, (what, part, off, at) in enumerate(SHARED):
            for step, later in steps.get(what, ()):
                bb = b + off - (at + later) // SLOTS
                if (at + later) % SLOTS == slot_ and valid(bb, n):
                    yield step, part, bb, bank_of(j)

    def exps_done(e, b, unit):
        for i in range(2):
            count = (unit + 1 - i + 1) // 2
            since(e, s[f"exp{i}_done"], 20 * b + count)

    def pair_of(b, p):
        return (b, p - 2) if p >= 2 else (b - 1, p + 6)

    def group_of(b, p):
        return (b, p // 2 - 2) if p >= 4 else (b - 1, p // 2 + 2)

    def slot(tile, which, slot_, g, rows, a, z):
        return tile[SLOT * slot_:SLOT * slot_ + rows, which, g, a:z]

    def where(p):
        c, u, sl = p // 4, p // 2 % 2, p % 2
        return 4 * c + 2 * u, sl

    def wstage(i):
        return pT[0][:, 0, 0:2048].rearrange("p (i c d) -> p i c d", i=4, c=C)[:, i]

    with nc.Block() as block:

        @block.sync
        def _(e):
            for i in range(4):
                e.dma_start(wstage(i), w_in[i].rearrange("(c p) n -> p c n", p=P)).then_inc(s["w_loaded"], 16)

            def store(b):
                e.wait_ge(s["x_done"], 2 * (b + 1))
                e.dma_start(x_out[b], xres[:]).then_inc(s["stored"], 16)

            def body(b, par, half_b):
                if isinstance(b, int) and b == -1:
                    norm.load(e, 0)
                    e.wait_ge(s["ones_set"], 6)
                if valid(b + 2, n):
                    norm.load(e, b + 2)
                for p in range(8):
                    if softmax:
                        bm, pm = (b, p - 1) if p else (b - 1, 7)
                        if valid(bm, n):
                            g0, sl = where(pm)
                            copy = pack[par if p else 1 - par]
                            row = copy[SLOT * sl + ONES_ROW:SLOT * sl + ONES_ROW + 1, 0, g0:g0 + 2, :]
                            e.wait_ge(s["mrow_done"], 8 * bm + pm + 1)
                            e.dma_start(row.bitcast(F32).rearrange("o g (t q) -> o (g t) q", q=P),
                                        mrow[:, pm % 2, :].bitcast(F32)).then_inc(s[f"maxima_in{pm % 2}"], 16)
                    if p == 1 and valid(b - 2, n):
                        store(b - 2)
                    if p == 2 and valid(b - 1, n):
                        since(e, s["stored"], 16 * (b - 1))
                        e.dma_start(xres[:], x_in[b - 1]).then_inc(s["xres_loaded"], 16)
                        since(e, s["gated_done"], 2 * (b - 1))
                        e.dma_start(gate[:], gates[ds(b - 1, 1), :].to_broadcast([P, D])).then_inc(s["gate_loaded"], 16)
                    if 3 <= p < 7 and valid(b + 1, n):
                        if p == 3:
                            since(e, s["st_ready"], 40 * b)
                            e.wait_ge(s["qk_lo_done"], 4 * (b + 2))
                        for hh in ((0, 2), (1, 3), (4, 6), (5, 7))[p - 3]:
                            sl, gg = hh % 2, hh // 2
                            done = s[f"packed{1 - par}_{hh // 4}"]
                            src = split[HD * hh:HD * hh + HD].bitcast(F32)
                            for r, qv, kv in ((0, QH, KH), (1, QH, KL), (2, QL, KH)):
                                rows = pack[1 - par][SLOT * sl + HD * r:SLOT * sl + HD * r + HD].bitcast(F32)
                                dst = rows.rearrange("p w (c g) s -> p w c g s", c=C)[:, :, :, gg, :]
                                if kv == qv + 1:
                                    e.dma_start(dst, src[:, qv:qv + 2]).then_inc(done, 16)
                                else:
                                    e.dma_start(dst[:, 0], src[:, qv]).then_inc(done, 16)
                                    e.dma_start(dst[:, 1], src[:, kv]).then_inc(done, 16)

            bodies(e, n, body)
            store(n - 1)
            e.wait_ge(s["stored"], 16 * n)

        @block.gpsimd
        def _(e):
            for i in range(2):
                e.memset(pack[i][32:64, 1, :, :].bitcast(F32), 1.0).then_inc(s["ones_set"], 1)
                e.memset(pack[i][96:128, 1, :, :].bitcast(F32), 1.0).then_inc(s["ones_set"], 1)
                e.wait_ge(s["ones_set"], 3 * i + 2)
                e.memset(vaug[i][:, :, :, HD:32], 1.0).then_inc(s["ones_set"], 1)
                e.wait_ge(s["ones_set"], 3 * i + 3)

            def add(b, i):
                e.wait_ge(s["gated_done"], 2 * b + i + 1)
                half = xres[:, 2 * i:2 * i + 2, :]
                e.tensor_tensor(half, half, gated[:, 2 * i:2 * i + 2, :], ALU.add).then_inc(s["x_done"], 1)

            def body(b, par, half_b):
                if isinstance(b, int) and b == -1:
                    norm.rsqrt(e, 0)
                for p in range(8):
                    if p == 5 and valid(b + 2, n):
                        norm.rsqrt(e, b + 2)
                    bp, q = pair_of(b, p)
                    if valid(bp, n):
                        exps_done(e, bp, 5 * q + 4)
                        e.sem_inc(s["masking"], 1)
                        rows = pT[q // 2 % 2][:, q % 2, :]
                        for part in (rows[:, 0:2048].rearrange("p (a x) -> p a x", a=4)[:, :, 0:P],
                                     rows[:, 0:2048].rearrange("p (a x) -> p a x", a=2)[:, :, 640:640 + P],
                                     rows[:, 2048:2560].rearrange("p (a x) -> p a x", a=2)[:, :, 0:P]):
                            e.affine_select(out=part, in_=part, pattern=[[0, part.shape[1]], [1, P]],
                                            compare_op=ALU.is_ge, fill=0.0, base=0,
                                            channel_multiplier=-1).then_inc(s["masked"], 1)
                    if p == 1 and valid(b - 2, n):
                        add(b - 2, 1)
                    if p == 7 and valid(b - 1, n):
                        e.wait_ge(s["xres_loaded"], 16 * b)
                        add(b - 1, 0)

            bodies(e, n, body)
            add(n - 1, 1)

        @block.scalar
        def _(e):
            def exp_unit(bp, q, u):
                i, bank = (5 * q + u) % 2, st[(5 * q + u) % len(st)]
                if softmax or i == 0:
                    if q % 2 == 0 and u < 2:
                        since(e, s["pv_ready"], 4 * bp + q // 2 - 1)
                    e.wait_ge(s["st_ready"], 40 * bp + 5 * q + u + 1)
                    dst = pT[q // 2 % 2][:, q % 2, 512 * u:512 * u + 512]
                    if softmax:
                        e.activation(dst, bank[:], ACT.Exp, scale=float(HD) ** -0.5).then_inc(s[f"exp{i}_done"], 1)
                    else:
                        e.activation(dst, bank[:], ACT.Copy).then_inc(s["exp0_done"], 1)

            def body(b, par, half_b):
                if isinstance(b, int) and b == -1:
                    for t in range(T):
                        norm.normalise(e, 0, t)
                for p in range(8):
                    bp, q = pair_of(b, p)
                    for u in range(5):
                        if valid(bp, n):
                            exp_unit(bp, q, u)
                        if u == 2 and softmax:
                            bm, pm = (b, p - 1) if p else (b - 1, 7)
                            if valid(bm, n):
                                e.wait_ge(s["mT_ready"], 8 * bm + pm + 1)
                                since(e, s[f"maxima_in{pm % 2}"], 16 * (4 * bm + pm // 2))
                                e.activation(mrow[:, pm % 2, :], mt[0:8, 0:P], ACT.Copy,
                                             scale=-1.0).then_inc(s["mrow_done"], 1)
                        if p % 2 == 0 and u == 0:
                            bg, G = group_of(b, p)
                            bg, G = (bg, G - 1) if G else (bg - 1, 3)
                            if valid(bg, n):
                                e.wait_ge(s["pv_ready"], 4 * bg + G + 1)
                                since(e, s["nrm_ready"], 4 * bg + G - 1)
                                e.activation(oT[:, G % 2, :], pv[:], ACT.Copy).then_inc(s["pv_copied"], 1)
                        if 5 * p + u in (32, 33, 34, 35) and valid(b + 2, n):
                            norm.normalise(e, b + 2, 5 * p + u - 32)
                        for step, part, bb, bank in due(ACT_STEPS, b, 5 * p + u):
                            if step == "hT":
                                norm.modulate(e, bb, part, bank)
                            if step == "ex":
                                e.wait_ge(s["qk_ready"], 4 * bb + part + 1)
                                since(e, s["low_done"], 4 * bb + part)
                                e.activation(ex[:], bank[:], ACT.Exp).then_inc(s["ex_done"], 1)
                            if step == "qk_hi":
                                which, c = (QH, KH)[part // 2], part % 2
                                if part == 0:
                                    since(e, s[f"packed{par}_0"], 256 * (half_b + 1))
                                    since(e, s[f"packed{par}_1"], 256 * (half_b + 1))
                                e.wait_ge(s["qk_ready" if softmax else "feat_done"], 4 * bb + part + 1)
                                e.activation(split[:, which, c, :], bank[:] if softmax else feat[:],
                                             ACT.Copy).then_inc(s["qk_hi_done"], 1)
                            if step == "v":
                                e.wait_ge(s["v_ready"], 2 * bb + part + 1)
                                if part == 0:
                                    since(e, s["pv_ready"], 4 * (bb - 1))
                                e.activation(vaug[1 - par][:, 2 * part:2 * part + 2, :, 0:HD],
                                             bank[:].rearrange("p (t h d) -> p t h d", t=2, d=HD),
                                             ACT.Copy).then_inc(s["v_done"], 1)
                            if step == "aT":
                                e.wait_ge(s["aT_ready"], C * bb + part + 1)
                                since(e, s["o_ready"], 2 * bb)
                                e.activation(aT[0][:, part, :], bank[:], ACT.Copy).then_inc(s["aT_hi_done"], 1)

            bodies(e, n, body)

        @block.vector
        def _(e):
            e.wait_ge(s["w_loaded"], 64)
            for i in range(4):
                e.tensor_copy(wt[0][:, i], wstage(i)).then_inc(s["w_hi_done"], 1)
                e.wait_ge(s["w_hi_done"], i + 1)
                e.tensor_tensor(wt[1][:, i], wstage(i), wt[0][:, i].bitcast(F32), ALU.subtract).then_inc(s["w_split"], 1)

            def maxima(b, p, u):
                unit = 40 * b + 5 * p + u
                e.wait_ge(s["nat_ready"], unit + 1)
                if u == 0:
                    since(e, s["mT_ready"], 8 * b + p - 1)
                bank, cols = nat[(5 * p + u) % 2], mcol[:, p % 2, :]
                g = u // 2
                if u < 4 and u % 2 == 0:
                    e.tensor_reduce(cols[:, 4 * g + 3:4 * g + 4], bank[:], AX_X, ALU.max).then_inc(s["max_done"], 1)
                elif u < 4:
                    e.tensor_reduce(cols[:, 4 * g:4 * g + 1], bank[:, 384:512], AX_X, ALU.max)
                    e.tensor_reduce(cols[:, 4 * g + 2:4 * g + 3], bank[:, 0:384], AX_X,
                                    ALU.max).then_inc(s["max_done"], 1)
                else:
                    e.tensor_reduce(cols[:, 1:8:4], bank[:].rearrange("p (g k) -> p g k", g=2), AX_X,
                                    ALU.max).then_inc(s["max_done"], 1)

            def copy_unit(bp, q, u):
                if (5 * q + u) % 2:
                    if q % 2 == 0 and u < 2:
                        since(e, s["pv_ready"], 4 * bp + q // 2 - 1)
                    e.wait_ge(s["st_ready"], 40 * bp + 5 * q + u + 1)
                    e.tensor_copy(pT[q // 2 % 2][:, q % 2, 512 * u:512 * u + 512],
                                  st[(5 * q + u) % len(st)][:]).then_inc(s["exp1_done"], 1)

            def body(b, par, half_b):
                if isinstance(b, int) and b == -1:
                    norm.all_statistics(e, 0)
                for slot_ in range(SLOTS):
                    p, u = slot_ // 5, slot_ % 5
                    bp, q = pair_of(b, p)
                    if softmax and valid(b, n):
                        maxima(b, p, u)
                    if not softmax and valid(bp, n):
                        copy_unit(bp, q, u)
                    if valid(b + 2, n):
                        if slot_ in STATISTICS:
                            norm.statistics(e, b + 2, STATISTICS.index(slot_))
                        if slot_ == 22:
                            norm.variance(e, b + 2)
                        if slot_ == 28:
                            norm.shift_of_mean(e, b + 2)
                    for step, part, bb, bank in due(DVE_STEPS, b, slot_):
                        if step == "hT":
                            since(e, s["v_ready"], 2 * bb)
                            norm.split(e, bb, part, 0)
                        if step == "feat":
                            e.wait_ge(s["ex_done"], 4 * bb + part + 1)
                            since(e, s["qk_lo_done"], 4 * bb + part)
                            e.tensor_scalar(low[:], ex[:], 1.0, None, ALU.min).then_inc(s["low_done"], 1)
                            e.wait_ge(s["low_done"], 4 * bb + part + 1)
                            e.scalar_tensor_tensor(feat[:], bank[:], 0.0, low[:], ALU.max,
                                                   ALU.add).then_inc(s["feat_done"], 1)
                        if step == "qk_lo":
                            hi, lo, c = (QH, KH)[part // 2], (QL, KL)[part // 2], part % 2
                            e.wait_ge(s["qk_hi_done"], 4 * bb + part + 1)
                            e.tensor_tensor(split[:, lo, c, :], bank[:] if softmax else feat[:],
                                            split[:, hi, c, :].bitcast(F32), ALU.subtract).then_inc(s["qk_lo_done"], 1)
                        if step == "nrm":
                            e.wait_ge(s["nrm_ready"], 4 * bb + part + 1)
                            heads = bank[:].rearrange("p (t h x) -> p t h x", t=T, h=4)
                            flat = bank[:].rearrange("p (a x) -> p a x", x=32)
                            src = flat[:, :, HD]
                            since(e, s["on_done"], 4 * bb + part)
                            if not softmax:
                                e.tensor_scalar(den[:], src, 1e-6, None, ALU.add).then_inc(s["den_done"], 1)
                                e.wait_ge(s["den_done"], 4 * bb + part + 1)
                                src = den[:]
                            e.reciprocal(rec[:], src).then_inc(s["rec_done"], 1)
                            e.wait_ge(s["rec_done"], 4 * bb + part + 1)
                            if part == 0:
                                since(e, s["aT_ready"], C * bb)
                            e.tensor_tensor(on[:, :, 64 * part:64 * part + 64].rearrange("p t (h x) -> p t h x", h=4),
                                            heads[:, :, :, 0:HD],
                                            rec[:].rearrange("p (t h o) -> p t h o", t=T, o=1).to_broadcast([P, T, 4, HD]),
                                            ALU.mult).then_inc(s["on_done"], 1)
                        if step == "aT":
                            e.wait_ge(s["aT_hi_done"], C * bb + part + 1)
                            e.tensor_tensor(aT[1][:, part, :], bank[:], aT[0][:, part, :].bitcast(F32),
                                            ALU.subtract).then_inc(s["aT_lo_done"], 1)
                        if step == "o":
                            e.wait_ge(s["o_ready"], 2 * bb + part + 1)
                            if part == 0:
                                e.wait_ge(s["gate_loaded"], 16 * (bb + 1))
                                since(e, s["x_done"], 2 * bb)
                            e.tensor_tensor(gated[:, 2 * part:2 * part + 2, :],
                                            bank[:].rearrange("p (t d) -> p t d", t=2),
                                            gate[:].rearrange("p (o d) -> p o d", o=1).to_broadcast([P, 2, D]),
                                            ALU.mult).then_inc(s["gated_done"], 1)

            bodies(e, n, body)

        @block.tensor
        def _(e):
            e.wait_ge(s["w_split"], 4)
            e.wait_ge(s["ones_set"], 6)

            def scores(b, p, u, par, half_b):
                g0, sl = where(p)
                if p in (0, 2) and u == 0:
                    e.wait_ge(s[f"packed{par}_{p // 2}"], 256 * (half_b + 1))
                since(e, s["max_done"], 40 * b + 5 * p + u - 1)
                bank = nat[(5 * p + u) % 2]
                parts = [[(g0, 3, 0)], [(g0, 2, 0), (g0, 0, 384)], [(g0 + 1, 3, 0)], [(g0 + 1, 2, 0), (g0 + 1, 0, 384)],
                         [(g0, 1, 0), (g0 + 1, 1, 256)]][u]
                for g, t, at in parts:
                    keys = P * (t + 1)
                    e.matmul(bank[:, at:at + keys], slot(pack[par], 0, sl, g, 48, P * t, P * t + P),
                             slot(pack[par], 1, sl, g, 48, 0, keys), start=True, stop=False, skip_group_check=True)
                    mm = e.matmul(bank[:, at + keys - P:at + keys], k["ident_bf"][:], k["neg_mask"][:], start=False,
                                  stop=True, skip_group_check=True)
                mm.then_inc(s["nat_ready"], 1)

            def scores_t(b, p, u, par, half_b):
                g0, sl = where(p)
                if u == 0 and softmax:
                    e.wait_ge(s[f"maxima_in{p % 2}"], 16 * (4 * b + p // 2 + 1))
                if u == 0 and not softmax and p in (0, 2):
                    e.wait_ge(s[f"packed{par}_{p // 2}"], 256 * (half_b + 1))
                since(e, s[f"exp{(5 * p + u) % 2}_done"], 20 * b + (5 * p + u - len(st)) // 2 + 1)
                bank = st[(5 * p + u) % len(st)]
                parts = [[(g0, 0, 0)], [(g0, 3, 0), (g0, 1, P)], [(g0 + 1, 0, 0)], [(g0 + 1, 3, 0), (g0 + 1, 1, P)],
                         [(g0, 2, 0), (g0 + 1, 2, 256)]][u]
                rows = ONES_ROW + 1 if softmax else ONES_ROW
                for g, t, at in parts:
                    mm = e.matmul(bank[:, at:at + S - P * t], slot(pack[par], 1, sl, g, rows, P * t, P * t + P),
                                  slot(pack[par], 0, sl, g, rows, P * t, S), start=True, stop=True,
                                  skip_group_check=True)
                mm.then_inc(s["st_ready"], 1)

            def values(bg, G, js, par):
                if 0 in js:
                    e.wait_ge(s["masked"], 24 * bg + 6 * (G + 1))
                    e.wait_ge(s["v_done"], 2 * (bg + 1))
                    since(e, s["pv_copied"], 4 * bg + G)
                for j in js:
                    for hd in range(4):
                        gi, sl = hd // 2, hd % 2
                        at = [1024 * gi, 1024 * gi + 640, 2048 + 256 * gi, 1024 * gi + 512][j]
                        mm = e.matmul(pv[32 * hd:32 * hd + 32, P * j:S], vaug[par][:, j, 4 * G + hd, :],
                                      pT[G % 2][:, sl, at:at + S - P * j], start=(j == 0), stop=(j == 3),
                                      tile_position=(0, 32 * hd), skip_group_check=True)
                if 3 in js:
                    mm.then_inc(s["pv_ready"], 1)

            def shared(what, part, bb, bank):
                if what == "nrm":
                    e.wait_ge(s["pv_copied"], 4 * bb + part + 1)
                    for t in range(T):
                        mm = e.transpose(bank[:, t * P:(t + 1) * P], oT[:, part % 2, t * P:(t + 1) * P], k["ident"][:])
                    mm.then_inc(s["nrm_ready"], 1)
                if what == "hT":
                    norm.transpose(e, bb, part, bank)
                if what == "qk":
                    which, c = part // 2, part % 2
                    if part == 0:
                        e.wait_ge(norm.s["h_lo_done"], C * (bb + 1))
                    first = True
                    for a, z in PASSES:
                        for kc in range(C):
                            mm = e.matmul(bank[:], wt[a][:, which, kc, c * P:(c + 1) * P], h[z][:, kc, :],
                                          start=first, stop=(a, z, kc) == (*PASSES[-1], C - 1))
                            first = False
                    mm.then_inc(s["qk_ready"], 1)
                if what == "v":
                    for t in (2 * part, 2 * part + 1):
                        first = True
                        for a, z in PASSES:
                            for kc in range(C):
                                mm = e.matmul(bank[:, t % 2 * D:(t % 2 + 1) * D], h[z][:, kc, t * P:(t + 1) * P],
                                              wt[a][:, 2, kc, :], start=first,
                                              stop=(a, z, kc) == (*PASSES[-1], C - 1))
                                first = False
                    mm.then_inc(s["v_ready"], 1)
                if what == "aT":
                    e.wait_ge(s["on_done"], 4 * (bb + 1))
                    for t in range(T):
                        mm = e.transpose(bank[:, t * P:(t + 1) * P], on[:, t, part * P:(part + 1) * P], k["ident"][:])
                    mm.then_inc(s["aT_ready"], 1)
                if what == "o":
                    if part == 0:
                        e.wait_ge(s["aT_lo_done"], C * (bb + 1))
                    for t in (2 * part, 2 * part + 1):
                        first = True
                        for a, z in PASSES:
                            for kc in range(C):
                                mm = e.matmul(bank[:, t % 2 * D:(t % 2 + 1) * D], aT[z][:, kc, t * P:(t + 1) * P],
                                              wt[a][:, 3, kc, :], start=first,
                                              stop=(a, z, kc) == (*PASSES[-1], C - 1))
                                first = False
                    mm.then_inc(s["o_ready"], 1)

            def body(b, par, half_b):
                for p in range(8):
                    bp, q = pair_of(b, p)
                    parq = par if p >= 2 else 1 - par
                    for u in range(5):
                        if softmax and valid(b, n):
                            scores(b, p, u, par, half_b)
                        if valid(bp, n):
                            scores_t(bp, q, u, parq, half_b if p >= 2 else half_b - 1 + par)
                        if u == 2 and softmax:
                            bm, pm = (b, p - 1) if p else (b - 1, 7)
                            if valid(bm, n):
                                e.wait_ge(s["max_done"], 40 * bm + 5 * (pm + 1))
                                since(e, s["mrow_done"], 8 * bm + pm)
                                e.transpose(mt[0:8, 0:P], mcol[:, pm % 2, :], k["ident"][:]).then_inc(s["mT_ready"], 1)
                        bg, G = group_of(b, p - p % 2)
                        if u in (2, 4) and valid(bg, n):
                            values(bg, G, (p % 2 * 2 + u // 4,), par if p >= 4 else 1 - par)
                        for j, (what, part, off, at) in enumerate(SHARED):
                            if at == 5 * p + u and valid(b + off, n):
                                bank_free(e, j, b)
                                shared(what, part, b + off, bank_of(j))

            bodies(e, n, body)



def setup_phase(nc, m, n, c_in, wmod_in, consts, mods, gates):
    k = consts
    ct = [m.sb(f"ct{i}", [P, C, n]) for i in range(2)]
    ce = [m.sb(f"ce{i}", [P, C, n]) for i in range(2)]
    sc = [m.sb(f"sc{i}", [P, C, n]) for i in range(2)]
    wm = [m.sb(f"wm{i}", [P, C, 6 * D]) for i in range(2)]
    mag = m.sb("mag", [n, 2, 2 * D])
    minus = m.sb("minus", [n, 2, 2 * D])
    sign = m.sb("sign", [n, 2, 2 * D])
    guarded = m.sb("guarded", [n, 2, 2 * D])
    pm = [m.ps(f"pm{i}") for i in range(2)]
    pg = [m.ps(f"pg{i}") for i in range(2)]
    names = "loaded exp_done silu mods_ready mods_done gates_ready negated guard gates_stored blank chain"
    s = {name: m.sem(name) for name in names.split()}
    COLS = (0, 1, 3, 4)

    with nc.Block() as block:

        @block.sync
        def _(e):
            for i in range(2):
                e.dma_start(ct[i][:], c_in[i].rearrange("(c p) b -> p c b", p=P)).then_inc(s["loaded"], 16)
                e.dma_start(wm[i][:], wmod_in[i].rearrange("(c p) j -> p c j", p=P)).then_inc(s["loaded"], 16)
            e.wait_ge(s["guard"], 6)
            e.dma_start(gates.rearrange("(l g) b d -> b l g d", l=2),
                        guarded[:].rearrange("b l (g d) -> b l g d", g=2)).then_inc(s["gates_stored"], 16)
            e.wait_ge(s["gates_stored"], 16)

        @block.gpsimd
        def _(e):
            e.memset(k["ident"][:], 0.0).then_inc(s["blank"], 1)
            e.memset(k["ident_bf"][:], 0.0).then_inc(s["blank"], 1)
            e.memset(k["neg_mask"][:], 0.0).then_inc(s["blank"], 1)
            e.memset(k["minus_half"][:], -0.5).then_inc(s["blank"], 1)
            e.wait_ge(s["blank"], 4)
            for t in ("ident", "ident_bf"):
                e.affine_select(out=k[t][:], in_=k[t][:], compare_op=ALU.not_equal, fill=1.0, base=0,
                                pattern=[[-1, P]], channel_multiplier=1).then_inc(s["blank"], 1)
            e.affine_select(out=k["neg_mask"][:], in_=k["neg_mask"][:], compare_op=ALU.is_ge, fill=NEG, base=0,
                            pattern=[[-1, P]], channel_multiplier=1).then_inc(s["blank"], 1)

        @block.scalar
        def _(e):
            e.wait_ge(s["loaded"], 64)
            for i in range(2):
                e.activation(ce[i][:], ct[i][:], ACT.Exp, scale=-1.0).then_inc(s["exp_done"], 1)

        @block.vector
        def _(e):
            for i in range(2):
                e.wait_ge(s["exp_done"], i + 1)
                e.tensor_scalar(ce[i][:], ce[i][:], 1.0, None, ALU.add).then_inc(s["chain"], 1)
                e.wait_ge(s["chain"], 2 * i + 1)
                e.reciprocal(ce[i][:], ce[i][:]).then_inc(s["chain"], 1)
                e.wait_ge(s["chain"], 2 * i + 2)
                e.tensor_tensor(sc[i][:], ct[i][:], ce[i][:], ALU.mult).then_inc(s["silu"], 1)
            for i in range(2):
                e.wait_ge(s["mods_ready"], i + 1)
                for j in range(4):
                    src = pm[i][:, j * C * n:(j + 1) * C * n].rearrange("p (c b) -> p c b", c=C)
                    e.tensor_scalar(mods[i][:, j], src, float(j % 2), None, ALU.add).then_inc(s["mods_done"], 1)
                e.wait_ge(s["gates_ready"], i + 1)
                e.tensor_scalar(minus[:, i], pg[i][0:n, :], -1.0, None, ALU.mult).then_inc(s["negated"], 1)
                e.wait_ge(s["negated"], i + 1)
                e.scalar_tensor_tensor(mag[:, i], pg[i][0:n, :], 0.25, minus[:, i], ALU.max,
                                       ALU.max).then_inc(s["guard"], 1)
                e.tensor_scalar(sign[:, i], pg[i][0:n, :], 0.0, 2.0, ALU.is_ge, ALU.mult).then_inc(s["guard"], 1)
                e.wait_ge(s["guard"], 3 * i + 2)
                e.scalar_tensor_tensor(guarded[:, i], sign[:, i], -1.0, mag[:, i], ALU.add,
                                       ALU.mult).then_inc(s["guard"], 1)

        @block.tensor
        def _(e):
            for i in range(2):
                e.wait_ge(s["silu"], i + 1)
                for jj, j in enumerate(COLS):
                    for c in range(C):
                        for kc in range(C):
                            at = (jj * C + c) * n
                            mm = e.matmul(pm[i][:, at:at + n], wm[i][:, kc, j * D + c * P:j * D + (c + 1) * P],
                                          sc[i][:, kc, :], start=(kc == 0), stop=(kc == C - 1))
                mm.then_inc(s["mods_ready"], 1)
                for jj, j in enumerate((2, 5)):
                    for kc in range(C):
                        mm = e.matmul(pg[i][0:n, jj * D:(jj + 1) * D], sc[i][:, kc, :],
                                      wm[i][:, kc, j * D:(j + 1) * D], start=(kc == 0), stop=(kc == C - 1))
                mm.then_inc(s["gates_ready"], 1)


def compose(nc, m, w_ab, logits_in, w1, w2, consts):
    RING = 4
    SLOTS = TOPK // 2
    ROUNDS = TOPK // 8
    logit = m.sb("logit", [1, 2, 64])
    rest = m.sb("rest", [1, 2, 64])
    vals = m.sb("vals", [1, 2, TOPK])
    idx = m.sb("idx", [1, 2, TOPK], U32)
    shift = m.sb("shift", [1, 2])
    ew = m.sb("ew", [1, 2, TOPK])
    total = m.sb("total", [1, 2])
    rtotal = m.sb("rtotal", [1, 2])
    weight = m.sb("weight", [1, 2, TOPK])
    ones = m.sb("ones", [1, P])
    wcol = m.sb("wcol", [P, 2, SLOTS])
    a_st = m.sb("a_st", [P, RING, F])
    b_st = m.sb("b_st", [P, RING, F])
    a_w = m.sb("a_w", [P, RING, F])
    acc = [m.ps(f"acc{i}") for i in range(4)]
    pw = m.ps("pw")
    names = """logits_loaded ones_set picked exp_done weights_done spread_ready spread_done chain
        a_scaled slot_used sum_ready hi_done lo_done""" + "".join(f" st_loaded{i}" for i in range(RING))
    s = {name: m.sem(name) for name in names.split()}
    WIDTH = ((D, F), (F, D))
    out = (w1, w2)

    def hi_of(part, f, i):
        if f == 0:
            return out[0][part][:, i // 2, (i % 2) * 512:(i % 2) * 512 + 512]
        return out[1][part][:, 2 * i:2 * i + 2, :].rearrange("p a d -> p (a d)")

    with nc.Block() as block:

        @block.sync
        def _(e):
            e.dma_start(logit[:], logits_in.rearrange("(o f) x -> o f x", o=1)).then_inc(s["logits_loaded"], 16)
            e.wait_ge(s["picked"], 6 * ROUNDS - 2)

            def load(f, slot, r):
                wa, wb = WIDTH[f]
                since(e, s["slot_used"], f * SLOTS + slot - RING + 1)
                for hf in range(2):
                    which = e.value_load(idx[0:1, f, ds(slot * 2 + hf, 1)], min_val=0, max_val=63)
                    e.dma_start(a_st[64 * hf:64 * hf + 64, r, 0:wa], w_ab[f][0][ds(which, 1)].rearrange("o r x -> (o r) x")).then_inc(s[f"st_loaded{r}"], 16)
                    e.dma_start(b_st[64 * hf:64 * hf + 64, r, 0:wb], w_ab[f][1][ds(which, 1)].rearrange("o r x -> (o r) x")).then_inc(s[f"st_loaded{r}"], 16)

            for f in range(2):
                for r in range(RING):
                    load(f, r, r)
                with e.Fori(1, SLOTS // RING) as i:
                    for r in range(RING):
                        load(f, i * RING + r, r)

        @block.scalar
        def _(e):
            e.wait_ge(s["picked"], 6 * ROUNDS)
            for f in range(2):
                e.activation(ew[:, f, :], vals[:, f, :], ACT.Exp, bias=shift[:, f:f + 1],
                             accum_out=total[:, f:f + 1]).then_inc(s["exp_done"], 1)

            for f in range(2):
                for i in range(4):
                    e.wait_ge(s["sum_ready"], f + 1)
                    dst = hi_of(0, f, i)
                    e.activation(dst, acc[i][:], ACT.Copy).then_inc(s["hi_done"], 1)

        @block.vector
        def _(e):
            e.memset(ones[:], 1.0).then_inc(s["ones_set"], 1)
            e.wait_ge(s["logits_loaded"], 16)
            e.tensor_copy(rest[:], logit[:]).then_inc(s["chain"], 1)
            e.wait_ge(s["chain"], 1)
            done = 0
            for r in range(ROUNDS):
                top = slice(8 * r, 8 * r + 8)
                for f in range(2):
                    e.max(vals[:, f, top], rest[:, f, :]).then_inc(s["picked"], 1)
                done += 2
                e.wait_ge(s["picked"], done)
                for f in range(2):
                    e.max_index(idx[:, f, top], vals[:, f, top], rest[:, f, :]).then_inc(s["picked"], 1)
                done += 2
                e.wait_ge(s["picked"], done)
                if r < ROUNDS - 1:
                    for f in range(2):
                        e.match_replace(rest[:, f, :], vals[:, f, top], rest[:, f, :], -3.4e38).then_inc(s["picked"], 1)
                    done += 2
                    e.wait_ge(s["picked"], done)
            e.tensor_scalar(shift[:], vals[:, :, 0], -1.0, None, ALU.mult).then_inc(s["picked"], 2)
            assert done + 2 == 6 * ROUNDS
            e.wait_ge(s["exp_done"], 2)
            e.reciprocal(rtotal[:], total[:]).then_inc(s["weights_done"], 1)
            e.wait_ge(s["weights_done"], 1)
            for f in range(2):
                e.tensor_scalar(weight[:, f, :], ew[:, f, :], rtotal[:, f:f + 1], None, ALU.mult).then_inc(s["weights_done"], 1)
            e.wait_ge(s["spread_ready"], 1)
            for hf in range(2):
                src = pw[64 * hf:64 * hf + 64, 0:2 * TOPK].rearrange("p (f k o) -> p f k o", f=2, o=2)[:, :, :, hf]
                e.tensor_copy(wcol[64 * hf:64 * hf + 64], src).then_inc(s["spread_done"], 1)
            e.wait_ge(s["spread_done"], 2)

            def scale_a(f, slot, r, round_):
                wa, _ = WIDTH[f]
                e.wait_ge(s[f"st_loaded{r}"], 64 * (round_ + 1))
                e.tensor_scalar(a_w[:, r, 0:wa], a_st[:, r, 0:wa], wcol[:, f, ds(slot, 1)], None,
                                ALU.mult).then_inc(s["a_scaled"], 1)

            for f in range(2):
                for r in range(RING):
                    scale_a(f, r, r, f * SLOTS // RING)
                with e.Fori(1, SLOTS // RING) as i:
                    for r in range(RING):
                        scale_a(f, i * RING + r, r, f * SLOTS // RING + i)
                for i in range(4):
                    e.wait_ge(s["hi_done"], 4 * f + i + 1)
                    e.tensor_tensor(hi_of(1, f, i), acc[i][:], hi_of(0, f, i).bitcast(F32),
                                    ALU.subtract).then_inc(s["lo_done"], 1)

        @block.tensor
        def _(e):
            e.wait_ge(s["ones_set"], 1)
            e.wait_ge(s["weights_done"], 3)
            e.matmul(pw[:, 0:2 * TOPK], ones[:], weight[:].rearrange("o f k -> o (f k)"), start=True,
                     stop=True).then_inc(s["spread_ready"], 1)

            def multiply(f, slot, r, first):
                e.wait_ge(s["a_scaled"], f * SLOTS + slot + 1)
                if f == 0:
                    for c in range(C):
                        for hf in range(2):
                            mm = e.matmul(acc[2 * c + hf][:], a_w[:, r, c * P:(c + 1) * P],
                                          b_st[:, r, hf * 512:hf * 512 + 512], start=first, stop=False,
                                          skip_group_check=True)
                else:
                    for ft in range(FT):
                        mm = e.matmul(acc[ft // 2][:, ft % 2 * D:(ft % 2 + 1) * D], a_w[:, r, ft * P:(ft + 1) * P],
                                      b_st[:, r, 0:D], start=first and ft % 2 == 0, stop=False,
                                      skip_group_check=True)
                return mm

            for f in range(2):
                since(e, s["lo_done"], 4 * f)
                for r in range(RING):
                    multiply(f, r, r, r == 0).then_inc(s["slot_used"], 1)
                with e.Fori(1, SLOTS // RING - 1) as i:
                    for r in range(RING):
                        multiply(f, i * RING + r, r, False).then_inc(s["slot_used"], 1)
                for r in range(RING):
                    mm = multiply(f, SLOTS - RING + r, r, False)
                    mm.then_inc(s["slot_used"], 1)
                e.matmul(pw[:, 0:2 * TOPK], ones[:], weight[:].rearrange("o f k -> o (f k)"), start=True,
                         stop=True).then_inc(s["sum_ready"], 1)


def ffn_phase(nc, m, n, x_in, x_out, w_ab, logits_in, gates, consts, mods):
    w1 = [m.sb(f"w1_{part}", [P, C, F], F32R) for part in ("hi", "lo")]
    w2 = [m.sb(f"w2_{part}", [P, FT, D], F32R) for part in ("hi", "lo")]
    with Memory(nc, "comp") as own:
        compose(nc, own, w_ab, logits_in, w1, w2, consts)

    res = Stream(m, x_in, x_out, gates)
    norm = Norm(m, res, consts, *mods, copies=2)
    RING = 4
    g32 = m.sb("g32", [P, 2, S])
    g = [m.sb(f"g_{part}", [P, RING, S], F32R) for part in ("hi", "lo")]
    up = [m.ps(f"up{i}") for i in range(2)]
    down = [[m.ps(f"down{i}{j}") for j in range(2)] for i in range(2)]
    hT = [m.ps(f"hT{i}") for i in range(2)]
    names = "up_ready gelu_done g_hi_done g_lo_done down_ready"
    s = {name: m.sem(name) for name in names.split()}

    with nc.Block() as block:

        @block.sync
        def _(e):
            res.load(e, 0, 0, 0)
            res.load_gates(e)

            def body(b, par, half_b):
                if valid(b + 2, n):
                    res.load(e, b + 2, par, half_b + 1)
                if valid(b - 1, n):
                    res.store(e, b - 1)

            bodies(e, n, body)
            e.wait_ge(res.s["stored"], 16 * n)

        @block.gpsimd
        def _(e):
            def body(b, par, half_b):
                if valid(b + 1, n):
                    norm.rsqrt(e, b + 1)
                if valid(b - 1, n):
                    res.add(e, b - 1, 0)
                    res.add(e, b - 1, 1)

            bodies(e, n, body)

        @block.scalar
        def _(e):
            def body(b, par, half_b):
                for j in range(FT):
                    if j == 2 and valid(b + 1, n):
                        for t in range(T):
                            norm.normalise(e, b + 1, t)
                    if valid(b, n):
                        e.wait_ge(s["up_ready"], FT * b + j + 1)
                        since(e, s["g_lo_done"], FT * b + j - 1)
                        e.activation(g32[:, j % 2, :], up[j % 2][:], ACT.Gelu_apprx_tanh).then_inc(s["gelu_done"], 1)
                    if j == 5 and valid(b + 1, n):
                        for c in range(C):
                            norm.modulate(e, b + 1, c, hT[c])

            bodies(e, n, body)

        @block.vector
        def _(e):
            def body(b, par, half_b):
                for j in range(FT):
                    if j == 0 and valid(b + 1, n):
                        res.loaded(e, 1 - par, half_b + par)
                        norm.all_statistics(e, b + 1)
                    if j == 2 and valid(b - 1, n):
                        for part in range(2):
                            e.wait_ge(s["down_ready"], FT * b)
                            res.multiply(e, b - 1, part, down[1 - par][part])
                    if valid(b, n):
                        e.wait_ge(s["gelu_done"], FT * b + j + 1)
                        since(e, s["down_ready"], FT * b + j - RING + 1)
                        e.tensor_copy(g[0][:, j % RING, :], g32[:, j % 2, :]).then_inc(s["g_hi_done"], 1)
                        e.wait_ge(s["g_hi_done"], FT * b + j + 1)
                        e.tensor_tensor(g[1][:, j % RING, :], g32[:, j % 2, :], g[0][:, j % RING, :].bitcast(F32),
                                        ALU.subtract).then_inc(s["g_lo_done"], 1)
                    if j == 5 and valid(b + 1, n):
                        since(e, s["up_ready"], FT * b)
                        for c in range(C):
                            norm.split(e, b + 1, c, 1 - par)

            bodies(e, n, body)

        @block.tensor
        def _(e):
            def up_tile(b, j, par):
                if j == 0:
                    e.wait_ge(norm.s["h_lo_done"], C * (b + 1))
                since(e, s["gelu_done"], FT * b + j - 1)
                first = True
                for a, z in PASSES:
                    for kc in range(C):
                        mm = e.matmul(up[j % 2][:], w1[a][:, kc, j * P:(j + 1) * P], norm.h[par][z][:, kc, :],
                                      start=first, stop=(a, z, kc) == (*PASSES[-1], C - 1))
                        first = False
                mm.then_inc(s["up_ready"], 1)

            def down_tile(b, j, par):
                e.wait_ge(s["g_lo_done"], FT * b + j + 1)
                if j == 0:
                    since(e, res.s["gated_done"], 2 * (b - 1))
                for t in range(T):
                    bank = down[par][t // 2]
                    for i, (a, z) in enumerate(PASSES):
                        mm = e.matmul(bank[:, t % 2 * D:(t % 2 + 1) * D], g[z][:, j % RING, t * P:(t + 1) * P],
                                      w2[a][:, j, :], start=(i == 0 and j == 0 and t % 2 == 0),
                                      stop=(j == FT - 1 and i == 2), skip_group_check=True)
                mm.then_inc(s["down_ready"], 1)

            def body(b, par, half_b):
                for j in range(FT):
                    if valid(b, n):
                        up_tile(b, j, par)
                    if j < 2 and valid(b - 1, n):
                        down_tile(b - 1, FT - 2 + j, 1 - par)
                    if j >= 2 and valid(b, n):
                        down_tile(b, j - 2, par)
                    if j == 5 and valid(b + 1, n):
                        for c in range(C):
                            since(e, norm.s["h32_done"], C * (b + 1))
                            norm.transpose(e, b + 1, c, hT[c])

            bodies(e, n, body)


def linear_phase(nc, m, n, x_in, x_out, w_t, bias, low_rank, gates, consts, mods):
    lora_down_t, down_aux, lora_up_t, up_aux_t = low_rank
    rank, dd, ud = lora_down_t.shape[1], lora_down_t.shape[0], lora_up_t.shape[1]
    w = [m.sb(f"w_{part}", [P, C, D], F32R) for part in ("hi", "lo")]
    base = m.sb("base", [P, C, D])
    whole = m.sb("whole", [P, C, D])
    ldt = m.sb("ldt", [dd, rank])
    da = m.sb("da", [dd, D])
    lut = m.sb("lut", [rank, ud])
    uat = m.sb("uat", [ud, D])
    t1 = m.sb("t1", [rank, D])
    t2 = m.sb("t2", [ud, D])
    b32 = m.sb("b32", [1, D])
    bias_parts = [m.sb(f"b_{part}", [1, D], F32R) for part in ("hi", "lo")]
    ones = m.sb("ones", [1, P], F32R)
    res = Stream(m, x_in, x_out, gates)
    norm = Norm(m, res, consts, *mods, copies=2)
    out = [[m.ps(f"out{i}{j}") for j in range(2)] for i in range(2)]
    hT = [m.ps(f"hT{i}") for i in range(2)]
    names = """w_loaded t1_ready t1_done t2_ready t2_done w_ready whole_done w_hi_done w_split bias_hi_done bias_split
        ones_set out_ready"""
    s = {name: m.sem(name) for name in names.split()}

    with nc.Block() as block:

        @block.sync
        def _(e):
            res.load(e, 0, 0, 0)
            res.load(e, 1, 1, 0)
            for dst, src in ((base[:], w_t.rearrange("(c p) n -> p c n", p=P)), (ldt[:], lora_down_t), (da[:], down_aux),
                             (lut[:], lora_up_t), (uat[:], up_aux_t), (b32[:], bias)):
                e.dma_start(dst, src).then_inc(s["w_loaded"], 16)

            res.load_gates(e)

            def body(b, par, half_b):
                if valid(b + 3, n):
                    res.load(e, b + 3, 1 - par, half_b + 1 + par)
                if valid(b - 1, n):
                    res.store(e, b - 1)

            bodies(e, n, body, ahead=3)
            e.wait_ge(res.s["stored"], 16 * n)

        @block.gpsimd
        def _(e):
            norm.rsqrt(e, 0)

            def body(b, par, half_b):
                if valid(b + 2, n):
                    norm.rsqrt(e, b + 2)
                if valid(b - 1, n):
                    res.add(e, b - 1, 0)

            bodies(e, n, body)

        @block.scalar
        def _(e):
            def body(b, par, half_b):
                if valid(b + 1, n):
                    for t in range(T):
                        norm.normalise(e, b + 1, t)
                    since(e, s["out_ready"], 2 * b)
                    for c in range(C):
                        norm.modulate(e, b + 1, c, hT[c])
                        norm.modulate_hi(e, b + 1, c, hT[c], 1 - par)

            bodies(e, n, body)

        @block.vector
        def _(e):
            e.memset(ones[:].bitcast(F32), 1.0).then_inc(s["ones_set"], 1)
            res.loaded(e, 0, 0)
            norm.all_statistics(e, 0)
            e.wait_ge(s["w_loaded"], 96)
            e.tensor_copy(bias_parts[0][:], b32[:]).then_inc(s["bias_hi_done"], 1)
            e.wait_ge(s["bias_hi_done"], 1)
            e.tensor_tensor(bias_parts[1][:], b32[:], bias_parts[0][:].bitcast(F32), ALU.subtract).then_inc(s["bias_split"], 1)
            e.wait_ge(s["t1_ready"], 1)
            e.tensor_copy(t1[:], out[0][0][0:rank, 0:D]).then_inc(s["t1_done"], 1)
            e.wait_ge(s["t2_ready"], 1)
            e.tensor_copy(t2[:], out[0][0][0:ud, 0:D]).then_inc(s["t2_done"], 1)
            e.wait_ge(s["w_ready"], 1)
            e.tensor_tensor(whole[:], out[0][1][:].rearrange("p (c d) -> p c d", c=C), base[:],
                            ALU.add).then_inc(s["whole_done"], 1)
            e.wait_ge(s["whole_done"], 1)
            e.tensor_copy(w[0][:], whole[:]).then_inc(s["w_hi_done"], 1)
            e.wait_ge(s["w_hi_done"], 1)
            e.tensor_tensor(w[1][:], whole[:], w[0][:].bitcast(F32), ALU.subtract).then_inc(s["w_split"], 1)

            def body(b, par, half_b):
                if valid(b - 1, n):
                    for part in range(2):
                        e.wait_ge(s["out_ready"], 2 * (b - 1) + part + 1)
                        res.multiply(e, b - 1, part, out[1 - par][part])
                if valid(b + 2, n):
                    res.loaded(e, par, half_b + 1)
                    for t in range(T):
                        norm.statistics(e, b + 2, t)
                    norm.variance(e, b + 2)
                if valid(b - 1, n):
                    res.add(e, b - 1, 1)
                if valid(b + 1, n):
                    for c in range(C):
                        norm.lo(e, b + 1, c, 1 - par)
                if valid(b + 2, n):
                    norm.shift_of_mean(e, b + 2)

            bodies(e, n, body)

        @block.tensor
        def _(e):
            e.wait_ge(s["w_loaded"], 96)
            e.matmul(out[0][0][0:rank, 0:D], ldt[:], da[:], start=True, stop=True).then_inc(s["t1_ready"], 1)
            e.wait_ge(s["t1_done"], 1)
            e.matmul(out[0][0][0:ud, 0:D], lut[:], t1[:], start=True, stop=True).then_inc(s["t2_ready"], 1)
            e.wait_ge(s["t2_done"], 1)
            for c in range(C):
                mm = e.matmul(out[0][1][:, c * D:(c + 1) * D], t2[:, c * P:(c + 1) * P], uat[:], start=True, stop=True)
            mm.then_inc(s["w_ready"], 1)
            e.wait_ge(s["w_split"], 1)
            e.wait_ge(s["bias_split"], 1)
            e.wait_ge(s["ones_set"], 1)

            def body(b, par, half_b):
                if valid(b, n):
                    e.wait_ge(norm.s["h_lo_done"], C * (b + 1))
                    since(e, res.s["gated_done"], 2 * (b - 1))
                    for part in range(2):
                        for t in (2 * part, 2 * part + 1):
                            dst = out[par][part][:, t % 2 * D:(t % 2 + 1) * D]
                            e.matmul(dst, ones[:], bias_parts[0][:], start=True, stop=False)
                            e.matmul(dst, ones[:], bias_parts[1][:], start=False, stop=False)
                            for a, z in PASSES:
                                for kc in range(C):
                                    mm = e.matmul(dst, norm.h[par][z][:, kc, t * P:(t + 1) * P], w[a][:, kc, :],
                                                  start=False, stop=(a, z, kc) == (*PASSES[-1], C - 1))
                        mm.then_inc(s["out_ready"], 1)
                if valid(b + 1, n):
                    for c in range(C):
                        since(e, norm.s["h_hi_done"], C * b + c + 1)
                        since(e, norm.s["h32_done"], C * b + c + 1)
                        norm.transpose(e, b + 1, c, hT[c])

            bodies(e, n, body)


def program(nc, a, out):
    n = a["x"].shape[0]
    shape = [n, P, T, D]
    mid = [nc.dram_tensor(f"x_after{i}", shape, F32, kind="Internal").ap() for i in range(3)]
    gates = nc.dram_tensor("gates", [4, n, D], F32, kind="Internal").ap()
    with Memory(nc, "top") as top:
        consts = {"ident": top.sb("ident", [P, P]), "ident_bf": top.sb("ident_bf", [P, P], BF16),
                  "neg_mask": top.sb("neg_mask", [P, P], BF16), "minus_half": top.sb("minus_half", [P, T])}
        mods = [top.sb(f"mods{i}", [P, 4, C, n]) for i in range(2)]

        def pair(layer, which):
            return mods[layer][:, 2 * which + 1], mods[layer][:, 2 * which]

        with Memory(nc, "set") as m:
            setup_phase(nc, m, n, a["c"], a["wmod"], consts, mods, gates)
        with Memory(nc, "soft") as m:
            attention_phase(nc, m, n, 0, a["x"], mid[0], a["w_attn0"], gates[0], consts, pair(0, 0))
        with Memory(nc, "ffn") as m:
            ffn_phase(nc, m, n, mid[0], mid[1], ((a["a1"], a["b1"]), (a["a2"], a["b2"])), a["logits"], gates[1], consts,
                      pair(0, 1))
        with Memory(nc, "lin") as m:
            attention_phase(nc, m, n, 1, mid[1], mid[2], a["w_attn1"], gates[2], consts, pair(1, 0))
        with Memory(nc, "out") as m:
            linear_phase(nc, m, n, mid[2], out, a["w_lin"], a["bias"],
                         (a["lora_down_t"], a["down_aux"], a["lora_up_t"], a["up_aux_t"]), gates[3], consts, pair(1, 1))


def kernel(**inputs):
    import concourse.bacc as bacc
    from concourse.bass_utils import run_bass_kernel_spmd

    v = {name: np.asarray(x) for name, x in inputs.items()}
    n = v["L0_attn_x"].shape[0]
    flip = lambda x: np.ascontiguousarray(np.swapaxes(x, -1, -2))
    arrays = {
        "x": np.ascontiguousarray(v["L0_attn_x"].reshape(n, T, P, D).transpose(0, 2, 1, 3)),
        "c": np.stack([flip(v["L0_c"]), flip(v["L1_c"])]),
        "wmod": np.stack([v["L0_wmod"], v["L1_wmod"]]),
        "w_attn0": np.stack([flip(v[f"L0_attn_{x}_proj_weight"]) for x in "qkvo"]),
        "w_attn1": np.stack([v["L1_attn_w_attn"][:, i * D:(i + 1) * D] for i in range(3)] + [v["L1_attn_w_proj"]]),
        "a1": flip(v["L0_ffn_fc1_A"]), "b1": v["L0_ffn_fc1_B"], "a2": flip(v["L0_ffn_fc2_A"]), "b2": v["L0_ffn_fc2_B"],
        "logits": np.stack([v["L0_ffn_fc1_logits"], v["L0_ffn_fc2_logits"]]),
        "w_lin": flip(v["L1_ffn_W"]), "bias": v["L1_ffn_b"].reshape(1, D),
        "lora_down_t": flip(v["L1_ffn_lora_down"]), "down_aux": v["L1_ffn_down_aux"],
        "lora_up_t": flip(v["L1_ffn_lora_up"]), "up_aux_t": flip(v["L1_ffn_up_aux"]),
    }
    nc = bacc.Bacc("TRN2", target_bir_lowering=False, num_devices=1)
    aps = {name: nc.dram_tensor(f"in_{name}", x.shape, mybir.dt.from_np(x.dtype), kind="ExternalInput").ap()
           for name, x in arrays.items()}
    out = nc.dram_tensor("out", arrays["x"].shape, F32, kind="ExternalOutput").ap()
    program(nc, aps, out)
    r = run_bass_kernel_spmd(nc, [{f"in_{name}": x for name, x in arrays.items()}], core_ids=[0])
    y = r.results[0]["out"]
    return np.ascontiguousarray(y.transpose(0, 2, 1, 3)).reshape(n, T * P, D)
```

```python
from contextlib import ExitStack

import numpy as np

import concourse.bass as bass
from concourse import mybir

ALU = mybir.AluOpType
ACT = mybir.ActivationFunctionType
F32 = mybir.dt.float32
F32R = mybir.dt.float32r
BF16 = mybir.dt.bfloat16
U32 = mybir.dt.uint32
AX_X = mybir.AxisListType.X

P = 128
D = 256
C = D // P
S = 512
T = S // P
HEADS = 16
HD = D // HEADS
F = 1024
FT = F // P
TOPK = 32
RANK = 64
SLOT = 64
ONES_ROW = 48
NEG = -1e30
LN_EPS = 1e-5
PASSES = ((0, 0), (1, 0), (0, 1))

ds = bass.ds


def since(e, sem, n):
    if not isinstance(n, int) or n > 0:
        e.wait_ge(sem, n)


class Memory:

    def __init__(self, nc, prefix):
        self.nc, self.prefix, self.tensors, self.semaphores = nc, prefix, ExitStack(), []

    def __enter__(self):
        return self

    def __exit__(self, *error):
        if error[0] is None:
            self.nc.all_engine_barrier()
            self.nc.clear_and_free_semaphores(self.semaphores)
            self.nc.all_engine_barrier()
        self.tensors.close()

    def sb(self, name, shape, dt=F32):
        return self.tensors.enter_context(self.nc.sbuf_tensor(f"{self.prefix}_{name}", shape, dt))

    def ps(self, name, shape=(P, 512), dt=F32):
        return self.tensors.enter_context(self.nc.psum_tensor(f"{self.prefix}_{name}", list(shape), dt))

    def sem(self, name):
        self.semaphores.append(self.nc.alloc_semaphore(name=f"{self.prefix}_{name}"))
        return self.semaphores[-1]


def bodies(e, n, body, ahead=2):
    pairs = max(0, (n - 2 - ahead) // 2)
    for b in (-1, 0, 1):
        body(b, b % 2, b // 2)
    if pairs:
        with e.Fori(0, pairs) as i:
            body(i * 2 + 2, 0, i + 1)
            body(i * 2 + 3, 1, i + 1)
    for b in range(2 + 2 * pairs, n + 1):
        body(b, b % 2, b // 2)


def valid(b, n):
    return not isinstance(b, int) or 0 <= b < n


class Stream:

    def __init__(self, m, x_in, x_out, gates):
        self.x_in, self.x_out, self.gates, self.n = x_in, x_out, gates, x_in.shape[0]
        self.x = m.sb("x", [P, self.n, T, D])
        self.gated = m.sb("gated", [P, T, D])
        self.gate = m.sb("gate", [P, self.n, D])
        names = "x_loaded0 x_loaded1 gates_loaded gated_done x_done stored"
        self.s = {name: m.sem(name) for name in names.split()}

    def load_gates(self, e):
        e.dma_start(self.gate[:], self.gates.rearrange("(o b) d -> o b d", o=1).to_broadcast([P, self.n, D])).then_inc(
            self.s["gates_loaded"], 16)

    def load(self, e, b, par, half_b):
        since(e, self.s[f"x_loaded{par}"], 16 * half_b)
        e.dma_start(self.x[:, ds(b, 1)].rearrange("p o t d -> p (o t) d"),
                    self.x_in[ds(b, 1)].rearrange("o p t d -> p (o t) d")).then_inc(self.s[f"x_loaded{par}"], 16)

    def loaded(self, e, par, half_b):
        e.wait_ge(self.s[f"x_loaded{par}"], 16 * (half_b + 1))

    def multiply(self, e, b, part, bank):
        if part == 0:
            e.wait_ge(self.s["gates_loaded"], 16)
            since(e, self.s["x_done"], 2 * b)
        e.tensor_tensor(self.gated[:, 2 * part:2 * part + 2, :], bank[:].rearrange("p (t d) -> p t d", t=2),
                        self.gate[:, ds(b, 1), :].to_broadcast([P, 2, D]), ALU.mult).then_inc(self.s["gated_done"], 1)

    def add(self, e, b, part):
        e.wait_ge(self.s["gated_done"], 2 * b + part + 1)
        rows = slice(2 * part, 2 * part + 2)
        x = self.x[:, ds(b, 1), rows, :].rearrange("p o t d -> p (o t) d")
        e.tensor_tensor(x, x, self.gated[:, rows, :], ALU.add).then_inc(self.s["x_done"], 1)

    def store(self, e, b):
        e.wait_ge(self.s["x_done"], 2 * (b + 1))
        e.dma_start(self.x_out[ds(b, 1)].rearrange("o p t d -> p (o t) d"),
                    self.x[:, ds(b, 1)].rearrange("p o t d -> p (o t) d")).then_inc(self.s["stored"], 16)


class Norm:

    def __init__(self, m, x_in, consts, scale, shift, copies):
        self.x_in, self.k, self.scale, self.shift = x_in, consts, scale, shift
        self.stream = x_in if isinstance(x_in, Stream) else None
        self.x = self.stream.x if self.stream else m.sb("ln_x", [P, T, D])
        self.stats = m.sb("ln_stats", [P, T, 6])
        self.mv = m.sb("ln_mv", [P, T, 2])
        self.veps = m.sb("ln_veps", [P, T])
        self.rstd = m.sb("ln_rstd", [P, T])
        self.nmr = m.sb("ln_nmr", [P, T])
        self.n = m.sb("ln_n", [P, T, D])
        self.h32 = m.sb("ln_h32", [P, C, S])
        self.h = [[m.sb(f"ln_h{i}_{part}", [P, C, S], F32R) for part in ("hi", "lo")] for i in range(copies)]
        self.s = {}
        for name in ("x_loaded", "bn_done", "aggregating", "mv_done", "veps_done", "rstd_done", "nmr_done", "normed",
                     "hT_ready", "h32_done", "h_hi_done", "h_lo_done"):
            self.s[name] = m.sem(f"ln_{name}")

    def load(self, e, b):
        since(e, self.s["normed"], T * b)
        e.dma_start(self.x[:], self.x_in[b]).then_inc(self.s["x_loaded"], 16)

    def rows(self, b, t):
        return self.x[:, ds(b, 1), t, :].rearrange("p o d -> p (o d)") if self.stream else self.x[:, t, :]

    def statistics(self, e, b, t):
        if t == 0:
            if not self.stream:
                e.wait_ge(self.s["x_loaded"], 16 * (b + 1))
            since(e, self.s["mv_done"], T * b)
        e.bn_stats(self.stats[:, t, :], self.rows(b, t)).then_inc(self.s["bn_done"], 1)

    def variance(self, e, b):
        since(e, self.s["normed"], T * b)
        e.wait_ge(self.s["bn_done"], T * (b + 1))
        e.sem_inc(self.s["aggregating"], 1)
        for t in range(T):
            e.bn_aggr(self.mv[:, t, :], self.stats[:, t, :]).then_inc(self.s["mv_done"], 1)
        e.wait_ge(self.s["mv_done"], T * (b + 1))
        e.tensor_scalar(self.veps[:], self.mv[:, :, 1], LN_EPS, None, ALU.add).then_inc(self.s["veps_done"], 1)

    def rsqrt(self, e, b):
        e.wait_ge(self.s["veps_done"], b + 1)
        e.tensor_tensor(self.rstd[:], self.veps[:], self.k["minus_half"][:], ALU.pow).then_inc(self.s["rstd_done"], 1)

    def shift_of_mean(self, e, b):
        e.wait_ge(self.s["rstd_done"], b + 1)
        e.scalar_tensor_tensor(self.nmr[:], self.mv[:, :, 0], -1.0, self.rstd[:], ALU.mult,
                               ALU.mult).then_inc(self.s["nmr_done"], 1)

    def all_statistics(self, e, b):
        for t in range(T):
            self.statistics(e, b, t)
        self.variance(e, b)
        self.shift_of_mean(e, b)

    def normalise(self, e, b, t):
        if t == 0:
            e.wait_ge(self.s["nmr_done"], b + 1)
            since(e, self.s["hT_ready"], C * b)
        e.activation(self.n[:, t, :], self.rows(b, t), ACT.Identity, scale=self.rstd[:, t:t + 1],
                     bias=self.nmr[:, t:t + 1]).then_inc(self.s["normed"], 1)

    def transpose(self, e, b, c, bank):
        e.wait_ge(self.s["normed"], T * (b + 1))
        for t in range(T):
            mm = e.transpose(bank[:, t * P:(t + 1) * P], self.n[:, t, c * P:(c + 1) * P], self.k["ident"][:])
        mm.then_inc(self.s["hT_ready"], 1)

    def modulate(self, e, b, c, bank):
        e.wait_ge(self.s["hT_ready"], C * b + c + 1)
        since(e, self.s["h_lo_done"], C * (b - 1) + c + 1)
        e.activation(self.h32[:, c, :], bank[:], ACT.Identity, scale=self.scale[:, c, ds(b, 1)],
                     bias=self.shift[:, c, ds(b, 1)]).then_inc(self.s["h32_done"], 1)

    def modulate_hi(self, e, b, c, bank, copy):
        e.activation(self.h[copy][0][:, c, :], bank[:], ACT.Identity, scale=self.scale[:, c, ds(b, 1)],
                     bias=self.shift[:, c, ds(b, 1)]).then_inc(self.s["h_hi_done"], 1)

    def lo(self, e, b, c, copy):
        hi, lo = self.h[copy]
        e.wait_ge(self.s["h32_done"], C * b + c + 1)
        e.wait_ge(self.s["h_hi_done"], C * b + c + 1)
        e.tensor_tensor(lo[:, c, :], self.h32[:, c, :], hi[:, c, :].bitcast(F32),
                        ALU.subtract).then_inc(self.s["h_lo_done"], 1)

    def split(self, e, b, c, copy):
        hi, lo = self.h[copy]
        e.wait_ge(self.s["h32_done"], C * b + c + 1)
        e.tensor_copy(hi[:, c, :], self.h32[:, c, :]).then_inc(self.s["h_hi_done"], 1)
        e.wait_ge(self.s["h_hi_done"], C * b + c + 1)
        e.tensor_tensor(lo[:, c, :], self.h32[:, c, :], hi[:, c, :].bitcast(F32),
                        ALU.subtract).then_inc(self.s["h_lo_done"], 1)


def attention_phase(nc, m, n, layer, x_in, x_out, w_in, gates, consts, mods):
    softmax = layer == 0
    k = consts
    wt = [m.sb(f"w_{part}", [P, 4, C, D], F32R) for part in ("hi", "lo")]
    pack = [m.sb(f"pack{i}", [P, 2, 8, S], F32R) for i in range(2)]
    split = m.sb("split", [P, 4, C, S], F32R)
    QL, KH, QH, KL = range(4)
    PACKED = 4 * 4 * 16
    vaug = [m.sb(f"vaug{i}", [P, T, HEADS, 32]) for i in range(2)]
    pT = [m.sb(f"pT{i}", [P, 2, 2560]) for i in range(2)]
    norm = Norm(m, x_in, k, *mods, copies=1)
    h = norm.h[0]
    oT = m.sb("oT", [P, 2, S])
    rec = m.sb("rec", [P, T * 4])
    on = m.sb("on", [P, T, D])
    aT = [m.sb(f"aT_{part}", [P, C, S], F32R) for part in ("hi", "lo")]
    xres = m.sb("xres", [P, T, D])
    gated = m.sb("gated", [P, T, D])
    gate = m.sb("gate", [P, D])
    mcol = m.sb("mcol", [P, 2, 8])
    mrow = m.sb("mrow", [8, 2, P], F32R)
    if not softmax:
        low = m.sb("low", [P, S])
        ex = m.sb("ex", [P, S])
        feat = m.sb("feat", [P, S])
        den = m.sb("den", [P, T * 4])

    nat = [m.ps(f"nat{i}") for i in range(2)] if softmax else []
    st = [m.ps(f"st{i}") for i in range(2 if softmax else 4)]
    pv = m.ps("pv")
    gen = [m.ps(f"gen{i}") for i in range(2)]
    if softmax:
        mt = m.ps("mt")

    names = """w_loaded w_hi_done w_split ones_set xres_loaded gate_loaded packed0_0 packed0_1 packed1_0 packed1_1
        maxima_in0 maxima_in1 stored qk_ready v_ready nat_ready st_ready mT_ready pv_ready nrm_ready aT_ready
        o_ready qk_hi_done qk_lo_done v_done exp0_done exp1_done mrow_done pv_copied aT_hi_done aT_lo_done max_done
        rec_done on_done gated_done masking masked x_done ex_done low_done feat_done den_done"""
    s = {name: m.sem(name) for name in names.split()}

    if softmax:
        SHARED = [("hT", 0, 1, 0), ("hT", 1, 1, 1), ("nrm", 1, -1, 4), ("qk", 0, 1, 5), ("qk", 1, 1, 8), ("qk", 2, 1, 10),
                  ("qk", 3, 1, 13), ("nrm", 2, -1, 15), ("v", 0, 1, 18), ("v", 1, 1, 20), ("nrm", 3, -1, 23),
                  ("aT", 0, -1, 25), ("aT", 1, -1, 26), ("o", 0, -1, 29), ("nrm", 0, 0, 33), ("o", 1, -1, 35)]
    else:
        SHARED = [("hT", 0, 1, 0), ("hT", 1, 1, 1), ("nrm", 1, -1, 3), ("qk", 0, 1, 6), ("qk", 1, 1, 8), ("qk", 2, 1, 11),
                  ("qk", 3, 1, 13), ("nrm", 2, -1, 15), ("v", 0, 1, 18), ("v", 1, 1, 20), ("nrm", 3, -1, 23),
                  ("aT", 0, -1, 25), ("aT", 1, -1, 26), ("o", 0, -1, 30), ("nrm", 0, 0, 33), ("o", 1, -1, 35)]
    READ = {"nrm": (s["on_done"], 4), "hT": (norm.s["h32_done"], C),
            "qk": (s["qk_lo_done" if softmax else "feat_done"], 4), "v": (s["v_done"], 2),
            "aT": (s["aT_lo_done"], C), "o": (s["gated_done"], 2)}
    ACT_STEPS = {"hT": (("hT", 1),), "v": (("v", 1),), "aT": (("aT", 1),),
                 "qk": (("qk_hi", 1),) if softmax else (("ex", 1), ("qk_hi", 2))}
    DVE_STEPS = {"hT": (("hT", 1 if softmax else 2),), "nrm": (("nrm", 1),), "aT": (("aT", 2),), "o": (("o", 1),),
                 "qk": (("qk_lo", 1),) if softmax else (("feat", 1), ("qk_lo", 3))}
    STATISTICS = (12, 14, 17, 19)
    ONES_SET = 3 if softmax else 1
    SLOTS = 40

    def bank_of(j):
        return gen[j % 2]

    def bank_free(e, j, b):
        at, body = j - 2, b
        while True:
            if at < 0:
                at, body = at + len(SHARED), body - 1
            if isinstance(body, int) and body < -1:
                return
            what, part, off, _ = SHARED[at]
            if valid(body + off, n):
                sem, per = READ[what]
                e.wait_ge(sem, per * (body + off) + part + 1)
                return
            at -= 2

    def due(steps, b, slot_):
        for j, (what, part, off, at) in enumerate(SHARED):
            for step, later in steps.get(what, ()):
                bb = b + off - (at + later) // SLOTS
                if (at + later) % SLOTS == slot_ and valid(bb, n):
                    yield step, part, bb, bank_of(j)

    def exps_done(e, b, unit):
        for i in range(2):
            since(e, s[f"exp{i}_done"], 20 * b + (unit + 2 - i) // 2)

    def pair_of(b, p):
        return (b, p - 2) if p >= 2 else (b - 1, p + 6)

    def group_of(b, p):
        return (b, p // 2 - 2) if p >= 4 else (b - 1, p // 2 + 2)

    def slot(tile, which, slot_, g, rows, a, z):
        return tile[SLOT * slot_:SLOT * slot_ + rows, which, g, a:z]

    def where(p):
        c, u, sl = p // 4, p // 2 % 2, p % 2
        return 4 * c + 2 * u, sl

    def wstage(i):
        return pT[0][:, 0, 0:2048].rearrange("p (i c d) -> p i c d", i=4, c=C)[:, i]

    with nc.Block() as block:

        @block.sync
        def _(e):
            norm.load(e, 0)
            for i in range(4):
                e.dma_start(wstage(i), w_in[i].rearrange("(c p) n -> p c n", p=P)).then_inc(s["w_loaded"], 16)

            def store(b):
                e.wait_ge(s["x_done"], 2 * (b + 1))
                e.dma_start(x_out[b], xres[:]).then_inc(s["stored"], 16)

            def body(b, par, half_b):
                if valid(b + 2, n):
                    norm.load(e, b + 2)
                for p in range(8):
                    if softmax:
                        bm, pm = (b, p - 1) if p else (b - 1, 7)
                        if valid(bm, n):
                            g0, sl = where(pm)
                            copy = pack[par if p else 1 - par]
                            row = copy[SLOT * sl + ONES_ROW:SLOT * sl + ONES_ROW + 1, 0, g0:g0 + 2, :]
                            e.wait_ge(s["mrow_done"], 8 * bm + pm + 1)
                            e.dma_start(row.bitcast(F32).rearrange("o g (t q) -> o (g t) q", q=P),
                                        mrow[:, pm % 2, :].bitcast(F32)).then_inc(s[f"maxima_in{pm % 2}"], 16)
                    if p == 1 and valid(b - 2, n):
                        store(b - 2)
                    if p == 2 and valid(b - 1, n):
                        since(e, s["stored"], 16 * (b - 1))
                        e.dma_start(xres[:], x_in[b - 1]).then_inc(s["xres_loaded"], 16)
                        since(e, s["gated_done"], 2 * (b - 1))
                        e.dma_start(gate[:], gates[ds(b - 1, 1), :].to_broadcast([P, D])).then_inc(s["gate_loaded"], 16)
                    if 3 <= p < 7 and valid(b + 1, n):
                        if p == 3:
                            since(e, s["st_ready"], 40 * b)
                            if softmax and isinstance(b, int) and b < 1:
                                e.wait_ge(s["ones_set"], 3 * (b + 1) + 2)
                            e.wait_ge(s["qk_lo_done"], 4 * (b + 2))
                        for hh in ((0, 2), (1, 3), (4, 6), (5, 7))[p - 3]:
                            sl, gg = hh % 2, hh // 2
                            done = s[f"packed{1 - par}_{hh // 4}"]
                            src = split[HD * hh:HD * hh + HD].bitcast(F32)
                            for r, qv, kv in ((0, QH, KH), (1, QH, KL), (2, QL, KH)):
                                rows = pack[1 - par][SLOT * sl + HD * r:SLOT * sl + HD * r + HD].bitcast(F32)
                                dst = rows.rearrange("p w (c g) s -> p w c g s", c=C)[:, :, :, gg, :]
                                if kv == qv + 1:
                                    e.dma_start(dst, src[:, qv:qv + 2]).then_inc(done, 16)
                                else:
                                    e.dma_start(dst[:, 0], src[:, qv]).then_inc(done, 16)
                                    e.dma_start(dst[:, 1], src[:, kv]).then_inc(done, 16)

            bodies(e, n, body)
            store(n - 1)
            e.wait_ge(s["stored"], 16 * n)

        @block.gpsimd
        def _(e):
            norm.rsqrt(e, 0)
            e.wait_ge(norm.s["rstd_done"], 1)
            for i in range(2):
                if softmax:
                    e.memset(pack[i][32:64, 1, :, :].bitcast(F32), 1.0).then_inc(s["ones_set"], 1)
                    e.memset(pack[i][96:128, 1, :, :].bitcast(F32), 1.0).then_inc(s["ones_set"], 1)
                    e.wait_ge(s["ones_set"], 3 * i + 2)
                e.memset(vaug[i][:, :, :, HD:32], 1.0).then_inc(s["ones_set"], 1)
                if softmax:
                    e.wait_ge(s["ones_set"], 3 * i + 3)

            def add(b, i):
                e.wait_ge(s["gated_done"], 2 * b + i + 1)
                half = xres[:, 2 * i:2 * i + 2, :]
                e.tensor_tensor(half, half, gated[:, 2 * i:2 * i + 2, :], ALU.add).then_inc(s["x_done"], 1)

            def body(b, par, half_b):
                for p in range(8):
                    if p == 5 and valid(b + 2, n):
                        norm.rsqrt(e, b + 2)
                    bp, q = pair_of(b, p)
                    if valid(bp, n):
                        rows = pT[q // 2 % 2][:, q % 2, :]
                        for i, part in enumerate((rows[:, 0:2048].rearrange("p (a x) -> p a x", a=4)[:, :, 0:P],
                                                  rows[:, 0:2048].rearrange("p (a x) -> p a x", a=2)[:, :, 640:640 + P],
                                                  rows[:, 2048:2560].rearrange("p (a x) -> p a x", a=2)[:, :, 0:P])):
                            if i != 1:
                                exps_done(e, bp, 5 * q + (3 if i == 0 else 4))
                                e.sem_inc(s["masking"], 1)
                            e.affine_select(out=part, in_=part, pattern=[[0, part.shape[1]], [1, P]],
                                            compare_op=ALU.is_ge, fill=0.0, base=0,
                                            channel_multiplier=-1).then_inc(s["masked"], 1)
                    if p == 1 and valid(b - 2, n):
                        add(b - 2, 1)
                    if p == 7 and valid(b - 1, n):
                        e.wait_ge(s["xres_loaded"], 16 * b)
                        add(b - 1, 0)

            bodies(e, n, body)
            add(n - 1, 1)

        @block.scalar
        def _(e):
            def exp_unit(bp, q, u):
                i, bank = (5 * q + u) % 2, st[(5 * q + u) % len(st)]
                if softmax or i == 0:
                    if q % 2 == 0 and u < 2:
                        since(e, s["pv_ready"], 4 * bp + q // 2 - 1)
                    e.wait_ge(s["st_ready"], 40 * bp + 5 * q + u + 1)
                    dst = pT[q // 2 % 2][:, q % 2, 512 * u:512 * u + 512]
                    if softmax:
                        e.activation(dst, bank[:], ACT.Exp, scale=float(HD) ** -0.5).then_inc(s[f"exp{i}_done"], 1)
                    else:
                        e.activation(dst, bank[:], ACT.Copy).then_inc(s["exp0_done"], 1)

            def body(b, par, half_b):
                if isinstance(b, int) and b == -1:
                    for t in range(T):
                        norm.normalise(e, 0, t)
                for p in range(8):
                    bp, q = pair_of(b, p)
                    for u in range(5):
                        if valid(bp, n):
                            exp_unit(bp, q, u)
                        if u == 2 and softmax:
                            bm, pm = (b, p - 1) if p else (b - 1, 7)
                            if valid(bm, n):
                                e.wait_ge(s["mT_ready"], 8 * bm + pm + 1)
                                since(e, s[f"maxima_in{pm % 2}"], 16 * (4 * bm + pm // 2))
                                e.activation(mrow[:, pm % 2, :], mt[0:8, 0:P], ACT.Copy,
                                             scale=-1.0).then_inc(s["mrow_done"], 1)
                        if p % 2 == 0 and u == 0:
                            bg, G = group_of(b, p)
                            bg, G = (bg, G - 1) if G else (bg - 1, 3)
                            if valid(bg, n):
                                e.wait_ge(s["pv_ready"], 4 * bg + G + 1)
                                since(e, s["nrm_ready"], 4 * bg + G - 1)
                                e.activation(oT[:, G % 2, :], pv[:], ACT.Copy).then_inc(s["pv_copied"], 1)
                        if 5 * p + u in (32, 33, 34, 35) and valid(b + 2, n):
                            norm.normalise(e, b + 2, 5 * p + u - 32)
                        for step, part, bb, bank in due(ACT_STEPS, b, 5 * p + u):
                            if step == "hT":
                                norm.modulate(e, bb, part, bank)
                            if step == "ex":
                                e.wait_ge(s["qk_ready"], 4 * bb + part + 1)
                                since(e, s["low_done"], 4 * bb + part)
                                e.activation(ex[:], bank[:], ACT.Exp).then_inc(s["ex_done"], 1)
                            if step == "qk_hi":
                                which, c = (QH, KH)[part // 2], part % 2
                                if part == 0:
                                    for i in range(2):
                                        since(e, s[f"packed{par}_{i}"], PACKED * (half_b + 1))
                                e.wait_ge(s["qk_ready" if softmax else "feat_done"], 4 * bb + part + 1)
                                e.activation(split[:, which, c, :], bank[:] if softmax else feat[:],
                                             ACT.Copy).then_inc(s["qk_hi_done"], 1)
                            if step == "v":
                                e.wait_ge(s["v_ready"], 2 * bb + part + 1)
                                if part == 0:
                                    since(e, s["pv_ready"], 4 * (bb - 1))
                                e.activation(vaug[1 - par][:, 2 * part:2 * part + 2, :, 0:HD],
                                             bank[:].rearrange("p (t h d) -> p t h d", t=2, d=HD),
                                             ACT.Copy).then_inc(s["v_done"], 1)
                            if step == "aT":
                                e.wait_ge(s["aT_ready"], C * bb + part + 1)
                                since(e, s["o_ready"], 2 * bb)
                                e.activation(aT[0][:, part, :], bank[:], ACT.Copy).then_inc(s["aT_hi_done"], 1)

            bodies(e, n, body)

        @block.vector
        def _(e):
            norm.all_statistics(e, 0)
            e.wait_ge(s["w_loaded"], 64)
            for i in range(4):
                e.tensor_copy(wt[0][:, i], wstage(i)).then_inc(s["w_hi_done"], 1)
                e.wait_ge(s["w_hi_done"], i + 1)
                e.tensor_tensor(wt[1][:, i], wstage(i), wt[0][:, i].bitcast(F32), ALU.subtract).then_inc(s["w_split"], 1)

            def maxima(b, p, u):
                unit = 40 * b + 5 * p + u
                e.wait_ge(s["nat_ready"], unit + 1)
                if u == 0:
                    since(e, s["mT_ready"], 8 * b + p - 1)
                bank, cols = nat[(5 * p + u) % 2], mcol[:, p % 2, :]
                g = u // 2
                if u < 4 and u % 2 == 0:
                    e.tensor_reduce(cols[:, 4 * g + 3:4 * g + 4], bank[:], AX_X, ALU.max).then_inc(s["max_done"], 1)
                elif u < 4:
                    e.tensor_reduce(cols[:, 4 * g:4 * g + 1], bank[:, 384:512], AX_X, ALU.max)
                    e.tensor_reduce(cols[:, 4 * g + 2:4 * g + 3], bank[:, 0:384], AX_X,
                                    ALU.max).then_inc(s["max_done"], 1)
                else:
                    e.tensor_reduce(cols[:, 1:8:4], bank[:].rearrange("p (g k) -> p g k", g=2), AX_X,
                                    ALU.max).then_inc(s["max_done"], 1)

            def copy_unit(bp, q, u):
                if (5 * q + u) % 2:
                    if q % 2 == 0 and u < 2:
                        since(e, s["pv_ready"], 4 * bp + q // 2 - 1)
                    e.wait_ge(s["st_ready"], 40 * bp + 5 * q + u + 1)
                    e.tensor_copy(pT[q // 2 % 2][:, q % 2, 512 * u:512 * u + 512],
                                  st[(5 * q + u) % len(st)][:]).then_inc(s["exp1_done"], 1)

            def body(b, par, half_b):
                for slot_ in range(SLOTS):
                    p, u = slot_ // 5, slot_ % 5
                    bp, q = pair_of(b, p)
                    if softmax and valid(b, n):
                        maxima(b, p, u)
                    if not softmax and valid(bp, n):
                        copy_unit(bp, q, u)
                    if valid(b + 2, n):
                        if slot_ in STATISTICS:
                            norm.statistics(e, b + 2, STATISTICS.index(slot_))
                        if slot_ == 22:
                            norm.variance(e, b + 2)
                        if slot_ == 28:
                            norm.shift_of_mean(e, b + 2)
                    for step, part, bb, bank in due(DVE_STEPS, b, slot_):
                        if step == "hT":
                            since(e, s["v_ready"], 2 * bb)
                            norm.split(e, bb, part, 0)
                        if step == "feat":
                            e.wait_ge(s["ex_done"], 4 * bb + part + 1)
                            since(e, s["qk_lo_done"], 4 * bb + part)
                            e.tensor_scalar(low[:], ex[:], 1.0, None, ALU.min).then_inc(s["low_done"], 1)
                            e.wait_ge(s["low_done"], 4 * bb + part + 1)
                            e.scalar_tensor_tensor(feat[:], bank[:], 0.0, low[:], ALU.max,
                                                   ALU.add).then_inc(s["feat_done"], 1)
                        if step == "qk_lo":
                            hi, lo, c = (QH, KH)[part // 2], (QL, KL)[part // 2], part % 2
                            e.wait_ge(s["qk_hi_done"], 4 * bb + part + 1)
                            e.tensor_tensor(split[:, lo, c, :], bank[:] if softmax else feat[:],
                                            split[:, hi, c, :].bitcast(F32), ALU.subtract).then_inc(s["qk_lo_done"], 1)
                        if step == "nrm":
                            e.wait_ge(s["nrm_ready"], 4 * bb + part + 1)
                            heads = bank[:].rearrange("p (t h x) -> p t h x", t=T, h=4)
                            flat = bank[:].rearrange("p (a x) -> p a x", x=32)
                            src = flat[:, :, HD]
                            since(e, s["on_done"], 4 * bb + part)
                            if not softmax:
                                e.tensor_scalar(den[:], src, 1e-6, None, ALU.add).then_inc(s["den_done"], 1)
                                e.wait_ge(s["den_done"], 4 * bb + part + 1)
                                src = den[:]
                            e.reciprocal(rec[:], src).then_inc(s["rec_done"], 1)
                            e.wait_ge(s["rec_done"], 4 * bb + part + 1)
                            if part == 0:
                                since(e, s["aT_ready"], C * bb)
                            e.tensor_tensor(on[:, :, 64 * part:64 * part + 64].rearrange("p t (h x) -> p t h x", h=4),
                                            heads[:, :, :, 0:HD],
                                            rec[:].rearrange("p (t h o) -> p t h o", t=T, o=1).to_broadcast([P, T, 4, HD]),
                                            ALU.mult).then_inc(s["on_done"], 1)
                        if step == "aT":
                            e.wait_ge(s["aT_hi_done"], C * bb + part + 1)
                            e.tensor_tensor(aT[1][:, part, :], bank[:], aT[0][:, part, :].bitcast(F32),
                                            ALU.subtract).then_inc(s["aT_lo_done"], 1)
                        if step == "o":
                            e.wait_ge(s["o_ready"], 2 * bb + part + 1)
                            if part == 0:
                                e.wait_ge(s["gate_loaded"], 16 * (bb + 1))
                                since(e, s["x_done"], 2 * bb)
                            e.tensor_tensor(gated[:, 2 * part:2 * part + 2, :],
                                            bank[:].rearrange("p (t d) -> p t d", t=2),
                                            gate[:].rearrange("p (o d) -> p o d", o=1).to_broadcast([P, 2, D]),
                                            ALU.mult).then_inc(s["gated_done"], 1)

            bodies(e, n, body)

        @block.tensor
        def _(e):
            def scores(b, p, u, par, half_b):
                g0, sl = where(p)
                if p in (0, 2) and u == 0:
                    e.wait_ge(s[f"packed{par}_{p // 2}"], PACKED * (half_b + 1))
                since(e, s["max_done"], 40 * b + 5 * p + u - 1)
                bank = nat[(5 * p + u) % 2]
                parts = [[(g0, 3, 0)], [(g0, 2, 0), (g0, 0, 384)], [(g0 + 1, 3, 0)], [(g0 + 1, 2, 0), (g0 + 1, 0, 384)],
                         [(g0, 1, 0), (g0 + 1, 1, 256)]][u]
                for i, (g, t, at) in enumerate(parts):
                    keys = P * (t + 1)
                    e.matmul(bank[:, at:at + keys], slot(pack[par], 0, sl, g, 48, P * t, P * t + P),
                             slot(pack[par], 1, sl, g, 48, 0, keys), start=(i == 0), stop=False, skip_group_check=True)
                diagonal = [bank[:, 384:512], bank[:, 256:512], bank[:, 384:512], bank[:, 256:512],
                            bank[:].rearrange("p (a x) -> p a x", a=2)[:, :, P:2 * P]][u]
                mask = k["neg_mask"][:, 0:len(parts) * P]
                if u == 4:
                    mask = mask.rearrange("p (a x) -> p a x", a=2)
                e.matmul(diagonal, k["ident_bf"][:], mask, start=False, stop=True,
                         skip_group_check=True).then_inc(s["nat_ready"], 1)

            def scores_t(b, p, u, par, half_b):
                g0, sl = where(p)
                if u == 0 and softmax:
                    e.wait_ge(s[f"maxima_in{p % 2}"], 16 * (4 * b + p // 2 + 1))
                if u == 0 and not softmax and p in (0, 2):
                    e.wait_ge(s[f"packed{par}_{p // 2}"], PACKED * (half_b + 1))
                since(e, s[f"exp{(5 * p + u) % 2}_done"], 20 * b + (5 * p + u - len(st)) // 2 + 1)
                bank = st[(5 * p + u) % len(st)]
                parts = [[(g0, 0, 0)], [(g0, 3, 0), (g0, 1, P)], [(g0 + 1, 0, 0)], [(g0 + 1, 3, 0), (g0 + 1, 1, P)],
                         [(g0, 2, 0), (g0 + 1, 2, 256)]][u]
                rows = ONES_ROW + 1 if softmax else ONES_ROW
                for g, t, at in parts:
                    mm = e.matmul(bank[:, at:at + S - P * t], slot(pack[par], 1, sl, g, rows, P * t, P * t + P),
                                  slot(pack[par], 0, sl, g, rows, P * t, S), start=True, stop=True,
                                  skip_group_check=True)
                mm.then_inc(s["st_ready"], 1)

            def values(bg, G, j, par):
                if j < 3:
                    e.wait_ge(s["masked"], 24 * bg + 6 * G + 4 + j)
                if j == 0:
                    e.wait_ge(s["v_done"], 2 * (bg + 1))
                    since(e, s["pv_copied"], 4 * bg + G)
                for hd in range(4):
                    gi, sl = hd // 2, hd % 2
                    at = [1024 * gi, 1024 * gi + 640, 2048 + 256 * gi, 1024 * gi + 512][j]
                    mm = e.matmul(pv[32 * hd:32 * hd + 32, P * j:S], vaug[par][:, j, 4 * G + hd, :],
                                  pT[G % 2][:, sl, at:at + S - P * j], start=(j == 0), stop=(j == 3),
                                  tile_position=(0, 32 * hd), skip_group_check=True)
                if j == 3:
                    mm.then_inc(s["pv_ready"], 1)

            def shared(what, part, bb, bank):
                if what == "nrm":
                    e.wait_ge(s["pv_copied"], 4 * bb + part + 1)
                    for t in range(T):
                        mm = e.transpose(bank[:, t * P:(t + 1) * P], oT[:, part % 2, t * P:(t + 1) * P], k["ident"][:])
                    mm.then_inc(s["nrm_ready"], 1)
                if what == "hT":
                    norm.transpose(e, bb, part, bank)
                if what == "qk":
                    which, c = part // 2, part % 2
                    if part == 0:
                        e.wait_ge(norm.s["h_lo_done"], C * (bb + 1))
                        if isinstance(bb, int) and bb == 0:
                            e.wait_ge(s["w_split"], 4)
                    first = True
                    for a, z in PASSES:
                        for kc in range(C):
                            mm = e.matmul(bank[:], wt[a][:, which, kc, c * P:(c + 1) * P], h[z][:, kc, :],
                                          start=first, stop=(a, z, kc) == (*PASSES[-1], C - 1))
                            first = False
                    mm.then_inc(s["qk_ready"], 1)
                if what == "v":
                    for t in (2 * part, 2 * part + 1):
                        first = True
                        for a, z in PASSES:
                            for kc in range(C):
                                mm = e.matmul(bank[:, t % 2 * D:(t % 2 + 1) * D], h[z][:, kc, t * P:(t + 1) * P],
                                              wt[a][:, 2, kc, :], start=first,
                                              stop=(a, z, kc) == (*PASSES[-1], C - 1))
                                first = False
                    mm.then_inc(s["v_ready"], 1)
                if what == "aT":
                    e.wait_ge(s["on_done"], 4 * (bb + 1))
                    for t in range(T):
                        mm = e.transpose(bank[:, t * P:(t + 1) * P], on[:, t, part * P:(part + 1) * P], k["ident"][:])
                    mm.then_inc(s["aT_ready"], 1)
                if what == "o":
                    if part == 0:
                        e.wait_ge(s["aT_lo_done"], C * (bb + 1))
                    for t in (2 * part, 2 * part + 1):
                        first = True
                        for a, z in PASSES:
                            for kc in range(C):
                                mm = e.matmul(bank[:, t % 2 * D:(t % 2 + 1) * D], aT[z][:, kc, t * P:(t + 1) * P],
                                              wt[a][:, 3, kc, :], start=first,
                                              stop=(a, z, kc) == (*PASSES[-1], C - 1))
                                first = False
                    mm.then_inc(s["o_ready"], 1)

            def body(b, par, half_b):
                if isinstance(b, int) and 0 <= b < 2:
                    e.wait_ge(s["ones_set"], ONES_SET * (b + 1))
                for p in range(8):
                    bp, q = pair_of(b, p)
                    parq = par if p >= 2 else 1 - par
                    for u in range(5):
                        if softmax and valid(b, n):
                            scores(b, p, u, par, half_b)
                        if valid(bp, n):
                            scores_t(bp, q, u, parq, half_b if p >= 2 else half_b - 1 + par)
                        if u == 2 and softmax:
                            bm, pm = (b, p - 1) if p else (b - 1, 7)
                            if valid(bm, n):
                                e.wait_ge(s["max_done"], 40 * bm + 5 * (pm + 1))
                                since(e, s["mrow_done"], 8 * bm + pm)
                                e.transpose(mt[0:8, 0:P], mcol[:, pm % 2, :], k["ident"][:]).then_inc(s["mT_ready"], 1)
                        bg, G = group_of(b, p - p % 2)
                        if u in (2, 4) and valid(bg, n):
                            values(bg, G, p % 2 * 2 + u // 4, par if p >= 4 else 1 - par)
                        for j, (what, part, off, at) in enumerate(SHARED):
                            if at == 5 * p + u and valid(b + off, n):
                                bank_free(e, j, b)
                                shared(what, part, b + off, bank_of(j))

            bodies(e, n, body)



def setup_phase(nc, m, n, c_in, wmod_in, logits_in, consts, mods, gates, picked):
    k = consts
    idx, wcol = picked
    ROUNDS = TOPK // 8
    logit = m.sb("logit", [1, 2, 64])
    rest = m.sb("rest", [1, 2, 64])
    vals = m.sb("vals", [1, 2, TOPK])
    shift = m.sb("shift", [1, 2])
    ew = m.sb("ew", [1, 2, TOPK])
    total = m.sb("total", [1, 2])
    rtotal = m.sb("rtotal", [1, 2])
    weight = m.sb("weight", [1, 2, TOPK])
    ones = m.sb("ones", [1, P])
    pw = m.ps("pw")
    ct = [m.sb(f"ct{i}", [P, C, n]) for i in range(2)]
    ce = [m.sb(f"ce{i}", [P, C, n]) for i in range(2)]
    sc = [m.sb(f"sc{i}", [P, C, n]) for i in range(2)]
    wm = [m.sb(f"wm{i}", [P, C, 6 * D]) for i in range(2)]
    mag = m.sb("mag", [n, 2, 2 * D])
    minus = m.sb("minus", [n, 2, 2 * D])
    sign = m.sb("sign", [n, 2, 2 * D])
    guarded = m.sb("guarded", [n, 2, 2 * D])
    pm = [m.ps(f"pm{i}") for i in range(2)]
    pg = [m.ps(f"pg{i}") for i in range(2)]
    names = """loaded exp_done silu mods_ready mods_done gates_ready negated guard gates_stored blank chain
        logits_loaded ones_set picked pick_exp_done weights_done spread_ready spread_done copied"""
    s = {name: m.sem(name) for name in names.split()}
    COLS = (0, 1, 3, 4)

    with nc.Block() as block:

        @block.sync
        def _(e):
            e.dma_start(logit[:], logits_in.rearrange("(o f) x -> o f x", o=1)).then_inc(s["logits_loaded"], 16)
            for i in range(2):
                e.dma_start(ct[i][:], c_in[i].rearrange("(c p) b -> p c b", p=P)).then_inc(s["loaded"], 16)
                e.dma_start(wm[i][:], wmod_in[i].rearrange("(c p) j -> p c j", p=P)).then_inc(s["loaded"], 16)
            e.wait_ge(s["guard"], 6)
            e.dma_start(gates.rearrange("(l g) b d -> b l g d", l=2),
                        guarded[:].rearrange("b l (g d) -> b l g d", g=2)).then_inc(s["gates_stored"], 16)
            e.wait_ge(s["gates_stored"], 16)

        @block.gpsimd
        def _(e):
            e.memset(k["ident"][:], 0.0).then_inc(s["blank"], 1)
            e.memset(k["ident_bf"][:], 0.0).then_inc(s["blank"], 1)
            e.memset(k["neg_mask"][:], 0.0).then_inc(s["blank"], 1)
            e.memset(k["minus_half"][:], -0.5).then_inc(s["blank"], 1)
            e.wait_ge(s["blank"], 4)
            for t in ("ident", "ident_bf"):
                e.affine_select(out=k[t][:], in_=k[t][:], compare_op=ALU.not_equal, fill=1.0, base=0,
                                pattern=[[-1, P]], channel_multiplier=1).then_inc(s["blank"], 1)
            mask = k["neg_mask"][:].rearrange("p (a x) -> p a x", a=2)
            e.affine_select(out=mask, in_=mask, compare_op=ALU.is_ge, fill=NEG, base=0,
                            pattern=[[0, 2], [-1, P]], channel_multiplier=1).then_inc(s["blank"], 1)

        @block.scalar
        def _(e):
            e.wait_ge(s["picked"], 6 * ROUNDS)
            for f in range(2):
                e.activation(ew[:, f, :], vals[:, f, :], ACT.Exp, bias=shift[:, f:f + 1],
                             accum_out=total[:, f:f + 1]).then_inc(s["pick_exp_done"], 1)
            e.wait_ge(s["loaded"], 64)
            for i in range(2):
                e.activation(ce[i][:], ct[i][:], ACT.Exp, scale=-1.0).then_inc(s["exp_done"], 1)

        @block.vector
        def _(e):
            e.memset(ones[:], 1.0).then_inc(s["ones_set"], 1)
            e.wait_ge(s["logits_loaded"], 16)
            e.tensor_copy(rest[:], logit[:]).then_inc(s["copied"], 1)
            e.wait_ge(s["copied"], 1)
            done = 0
            for r in range(ROUNDS):
                top = slice(8 * r, 8 * r + 8)
                for f in range(2):
                    e.max(vals[:, f, top], rest[:, f, :]).then_inc(s["picked"], 1)
                done += 2
                e.wait_ge(s["picked"], done)
                for f in range(2):
                    e.max_index(idx[:, f, top], vals[:, f, top], rest[:, f, :]).then_inc(s["picked"], 1)
                done += 2
                e.wait_ge(s["picked"], done)
                if r < ROUNDS - 1:
                    for f in range(2):
                        e.match_replace(rest[:, f, :], vals[:, f, top], rest[:, f, :], -3.4e38).then_inc(s["picked"], 1)
                    done += 2
                    e.wait_ge(s["picked"], done)
            e.tensor_scalar(shift[:], vals[:, :, 0], -1.0, None, ALU.mult).then_inc(s["picked"], 2)
            assert done + 2 == 6 * ROUNDS
            e.wait_ge(s["pick_exp_done"], 2)
            e.reciprocal(rtotal[:], total[:]).then_inc(s["weights_done"], 1)
            e.wait_ge(s["weights_done"], 1)
            for f in range(2):
                e.tensor_scalar(weight[:, f, :], ew[:, f, :], rtotal[:, f:f + 1], None, ALU.mult).then_inc(s["weights_done"], 1)
            e.wait_ge(s["spread_ready"], 1)
            for hf in range(2):
                src = pw[64 * hf:64 * hf + 64, 0:2 * TOPK].rearrange("p (f k o) -> p f k o", f=2, o=2)[:, :, :, hf]
                e.tensor_copy(wcol[64 * hf:64 * hf + 64], src).then_inc(s["spread_done"], 1)
            e.wait_ge(s["spread_done"], 2)

            for i in range(2):
                e.wait_ge(s["exp_done"], i + 1)
                e.tensor_scalar(ce[i][:], ce[i][:], 1.0, None, ALU.add).then_inc(s["chain"], 1)
                e.wait_ge(s["chain"], 2 * i + 1)
                e.reciprocal(ce[i][:], ce[i][:]).then_inc(s["chain"], 1)
                e.wait_ge(s["chain"], 2 * i + 2)
                e.tensor_tensor(sc[i][:], ct[i][:], ce[i][:], ALU.mult).then_inc(s["silu"], 1)
            for i in range(2):
                e.wait_ge(s["mods_ready"], i + 1)
                for j in range(4):
                    src = pm[i][:, j * C * n:(j + 1) * C * n].rearrange("p (c b) -> p c b", c=C)
                    e.tensor_scalar(mods[i][:, j], src, float(j % 2), None, ALU.add).then_inc(s["mods_done"], 1)
                e.wait_ge(s["gates_ready"], i + 1)
                e.tensor_scalar(minus[:, i], pg[i][0:n, :], -1.0, None, ALU.mult).then_inc(s["negated"], 1)
                e.wait_ge(s["negated"], i + 1)
                e.scalar_tensor_tensor(mag[:, i], pg[i][0:n, :], 0.25, minus[:, i], ALU.max,
                                       ALU.max).then_inc(s["guard"], 1)
                e.tensor_scalar(sign[:, i], pg[i][0:n, :], 0.0, 2.0, ALU.is_ge, ALU.mult).then_inc(s["guard"], 1)
                e.wait_ge(s["guard"], 3 * i + 2)
                e.scalar_tensor_tensor(guarded[:, i], sign[:, i], -1.0, mag[:, i], ALU.add,
                                       ALU.mult).then_inc(s["guard"], 1)

        @block.tensor
        def _(e):
            e.wait_ge(s["ones_set"], 1)
            e.wait_ge(s["weights_done"], 3)
            e.matmul(pw[:, 0:2 * TOPK], ones[:], weight[:].rearrange("o f k -> o (f k)"), start=True,
                     stop=True).then_inc(s["spread_ready"], 1)
            for i in range(2):
                e.wait_ge(s["silu"], i + 1)
                for jj, j in enumerate(COLS):
                    for c in range(C):
                        for kc in range(C):
                            at = (jj * C + c) * n
                            mm = e.matmul(pm[i][:, at:at + n], wm[i][:, kc, j * D + c * P:j * D + (c + 1) * P],
                                          sc[i][:, kc, :], start=(kc == 0), stop=(kc == C - 1))
                mm.then_inc(s["mods_ready"], 1)
                for jj, j in enumerate((2, 5)):
                    for kc in range(C):
                        mm = e.matmul(pg[i][0:n, jj * D:(jj + 1) * D], sc[i][:, kc, :],
                                      wm[i][:, kc, j * D:(j + 1) * D], start=(kc == 0), stop=(kc == C - 1))
                mm.then_inc(s["gates_ready"], 1)


def compose(nc, m, w_ab, w1, w2, picked):
    RING = 8
    SLOTS = TOPK // 2
    ROUNDS = SLOTS // RING
    WIDTH = ((D, F), (F, D))
    idx, wcol = picked
    raw = m.sb("raw", [P, RING, D + F])
    hi = m.sb("hi", [P, RING, D + F], F32R)
    lo = m.sb("lo", [P, RING, D + F], F32R)
    acc = [[m.ps(f"acc{f}{i}") for i in range(4)] for f in range(2)]
    names = "a_hi_done b_hi_done waited split_done multiplied hi_done lo_done" + "".join(
        f" loaded{i}" for i in range(RING))
    s = {name: m.sem(name) for name in names.split()}
    out = (w1, w2)

    def part_of(part, f, i):
        if f == 0:
            return out[0][part][:, i // 2, (i % 2) * 512:(i % 2) * 512 + 512]
        return out[1][part][:, 2 * i:2 * i + 2, :].rearrange("p a d -> p (a d)")

    with nc.Block() as block:

        @block.sync
        def _(e):
            def load(f, round_, first):
                wa = WIDTH[f][0]
                _, chosen = nc.values_load_multi_w_load_instructions(
                    idx[0:1, f, ds(round_ * (2 * RING), 2 * RING)], [mybir.EngineType.SP], min_val=0, max_val=63)
                for r in range(RING):
                    if not first:
                        e.wait_ge(s["split_done"], 2 * (round_ * RING + (f * SLOTS + r - RING + 1)))
                    for half in range(2):
                        rows = slice(64 * half, 64 * half + 64)
                        which = chosen[2 * r + half]
                        e.dma_start(raw[rows, r, 0:wa],
                                    w_ab[f][0][ds(which, 1)].rearrange("o r x -> (o r) x")).then_inc(s[f"loaded{r}"], 16)
                        e.dma_start(raw[rows, r, wa:D + F],
                                    w_ab[f][1][ds(which, 1)].rearrange("o r x -> (o r) x")).then_inc(s[f"loaded{r}"], 16)

            for f in range(2):
                load(f, 0, f == 0)
                with e.Fori(1, ROUNDS) as i:
                    load(f, i, False)

        @block.scalar
        def _(e):
            def split_hi(f, slot, r, round_, first):
                wa = WIDTH[f][0]
                if not first:
                    e.wait_ge(s["multiplied"], slot + (f * SLOTS - RING + 1))
                e.wait_ge(s[f"loaded{r}"], 64 * (round_ + 1))
                e.sem_inc(s["waited"], 1)
                e.activation(hi[:, r, 0:wa], raw[:, r, 0:wa], ACT.Copy,
                             scale=wcol[:, f, ds(slot, 1)]).then_inc(s["a_hi_done"], 1)
                e.activation(hi[:, r, wa:D + F], raw[:, r, wa:D + F], ACT.Copy).then_inc(s["b_hi_done"], 1)

            def sums_hi(f):
                for i in range(4):
                    e.wait_ge(s["multiplied"], SLOTS * (f + 1))
                    e.activation(part_of(0, f, i), acc[f][i][:], ACT.Copy).then_inc(s["hi_done"], 1)

            for f in range(2):
                for r in range(RING):
                    split_hi(f, r, r, f * ROUNDS, f == 0)
                if f == 1:
                    sums_hi(0)
                with e.Fori(1, ROUNDS) as i:
                    for r in range(RING):
                        split_hi(f, i * RING + r, r, i + f * ROUNDS, False)
            sums_hi(1)

        @block.vector
        def _(e):
            def split_lo(f, slot, r):
                wa = WIDTH[f][0]
                e.wait_ge(s["a_hi_done"], slot + (f * SLOTS + 1))
                e.sem_inc(s["waited"], 1)
                e.scalar_tensor_tensor(lo[:, r, 0:wa], raw[:, r, 0:wa], wcol[:, f, ds(slot, 1)],
                                       hi[:, r, 0:wa].bitcast(F32), ALU.mult, ALU.subtract).then_inc(s["split_done"], 1)
                e.wait_ge(s["b_hi_done"], slot + (f * SLOTS + 1))
                e.tensor_tensor(lo[:, r, wa:D + F], raw[:, r, wa:D + F], hi[:, r, wa:D + F].bitcast(F32),
                                ALU.subtract).then_inc(s["split_done"], 1)

            def sums_lo(f):
                for i in range(4):
                    e.wait_ge(s["hi_done"], 4 * f + i + 1)
                    e.tensor_tensor(part_of(1, f, i), acc[f][i][:], part_of(0, f, i).bitcast(F32),
                                    ALU.subtract).then_inc(s["lo_done"], 1)

            for f in range(2):
                for r in range(RING):
                    split_lo(f, r, r)
                if f == 1:
                    sums_lo(0)
                with e.Fori(1, ROUNDS) as i:
                    for r in range(RING):
                        split_lo(f, i * RING + r, r)
            sums_lo(1)

        @block.tensor
        def _(e):
            def multiply(f, slot, r, first):
                wa = WIDTH[f][0]
                e.wait_ge(s["split_done"], 2 * (slot + (f * SLOTS + 1)))
                part = (hi, lo)
                for y, z in PASSES:
                    if f == 0:
                        for i in range(4):
                            c, half = i // 2, i % 2
                            mm = e.matmul(acc[0][i][:], part[y][:, r, c * P:(c + 1) * P],
                                          part[z][:, r, wa + half * 512:wa + half * 512 + 512],
                                          start=first and (y, z) == (0, 0), stop=False, skip_group_check=True)
                    else:
                        for ft in range(FT):
                            mm = e.matmul(acc[1][ft // 2][:, ft % 2 * D:(ft % 2 + 1) * D],
                                          part[y][:, r, ft * P:(ft + 1) * P], part[z][:, r, wa:wa + D],
                                          start=first and (y, z) == (0, 0) and ft % 2 == 0, stop=False,
                                          skip_group_check=True)
                mm.then_inc(s["multiplied"], 1)

            for f in range(2):
                for r in range(RING):
                    multiply(f, r, r, r == 0)
                with e.Fori(1, ROUNDS) as i:
                    for r in range(RING):
                        multiply(f, i * RING + r, r, False)


def ffn_phase(nc, m, n, x_in, x_out, w_ab, picked, gates, consts, mods):
    w1 = [m.sb(f"w1_{part}", [P, C, F], F32R) for part in ("hi", "lo")]
    w2 = [m.sb(f"w2_{part}", [P, FT, D], F32R) for part in ("hi", "lo")]
    with Memory(nc, "comp") as own:
        compose(nc, own, w_ab, w1, w2, picked)

    res = Stream(m, x_in, x_out, gates)
    norm = Norm(m, res, consts, *mods, copies=2)
    RING = 4
    g32 = m.sb("g32", [P, 2, S])
    g = [m.sb(f"g_{part}", [P, RING, S], F32R) for part in ("hi", "lo")]
    up = [m.ps(f"up{i}") for i in range(2)]
    down = [[m.ps(f"down{i}{j}") for j in range(2)] for i in range(2)]
    hT = [m.ps(f"hT{i}") for i in range(2)]
    names = "up_ready gelu_done g_hi_done g_lo_done down_ready"
    s = {name: m.sem(name) for name in names.split()}

    with nc.Block() as block:

        @block.sync
        def _(e):
            res.load(e, 0, 0, 0)
            res.load_gates(e)

            def body(b, par, half_b):
                if valid(b + 2, n):
                    res.load(e, b + 2, par, half_b + 1)
                if valid(b - 1, n):
                    res.store(e, b - 1)

            bodies(e, n, body)
            e.wait_ge(res.s["stored"], 16 * n)

        @block.gpsimd
        def _(e):
            def body(b, par, half_b):
                if valid(b + 1, n):
                    norm.rsqrt(e, b + 1)
                if valid(b - 1, n):
                    res.add(e, b - 1, 0)
                    res.add(e, b - 1, 1)

            bodies(e, n, body)

        @block.scalar
        def _(e):
            def body(b, par, half_b):
                for j in range(FT):
                    if j == 2 and valid(b + 1, n):
                        for t in range(T):
                            norm.normalise(e, b + 1, t)
                    if valid(b, n):
                        e.wait_ge(s["up_ready"], FT * b + j + 1)
                        since(e, s["g_lo_done"], FT * b + j - 1)
                        e.activation(g32[:, j % 2, :], up[j % 2][:], ACT.Gelu_apprx_tanh).then_inc(s["gelu_done"], 1)
                    if j == 5 and valid(b + 1, n):
                        for c in range(C):
                            norm.modulate(e, b + 1, c, hT[c])

            bodies(e, n, body)

        @block.vector
        def _(e):
            def body(b, par, half_b):
                for j in range(FT):
                    if j == 0 and valid(b + 1, n):
                        res.loaded(e, 1 - par, half_b + par)
                        norm.all_statistics(e, b + 1)
                    if j == 2 and valid(b - 1, n):
                        for part in range(2):
                            e.wait_ge(s["down_ready"], FT * b)
                            res.multiply(e, b - 1, part, down[1 - par][part])
                    if valid(b, n):
                        e.wait_ge(s["gelu_done"], FT * b + j + 1)
                        since(e, s["down_ready"], FT * b + j - RING + 1)
                        e.tensor_copy(g[0][:, j % RING, :], g32[:, j % 2, :]).then_inc(s["g_hi_done"], 1)
                        e.wait_ge(s["g_hi_done"], FT * b + j + 1)
                        e.tensor_tensor(g[1][:, j % RING, :], g32[:, j % 2, :], g[0][:, j % RING, :].bitcast(F32),
                                        ALU.subtract).then_inc(s["g_lo_done"], 1)
                    if j == 5 and valid(b + 1, n):
                        since(e, s["up_ready"], FT * b)
                        for c in range(C):
                            norm.split(e, b + 1, c, 1 - par)

            bodies(e, n, body)

        @block.tensor
        def _(e):
            def up_tile(b, j, par):
                if j == 0:
                    e.wait_ge(norm.s["h_lo_done"], C * (b + 1))
                since(e, s["gelu_done"], FT * b + j - 1)
                first = True
                for a, z in PASSES:
                    for kc in range(C):
                        mm = e.matmul(up[j % 2][:], w1[a][:, kc, j * P:(j + 1) * P], norm.h[par][z][:, kc, :],
                                      start=first, stop=(a, z, kc) == (*PASSES[-1], C - 1))
                        first = False
                mm.then_inc(s["up_ready"], 1)

            def down_tile(b, j, par):
                e.wait_ge(s["g_lo_done"], FT * b + j + 1)
                if j == 0:
                    since(e, res.s["gated_done"], 2 * (b - 1))
                for t in range(T):
                    bank = down[par][t // 2]
                    for i, (a, z) in enumerate(PASSES):
                        mm = e.matmul(bank[:, t % 2 * D:(t % 2 + 1) * D], g[z][:, j % RING, t * P:(t + 1) * P],
                                      w2[a][:, j, :], start=(i == 0 and j == 0 and t % 2 == 0),
                                      stop=(j == FT - 1 and i == 2), skip_group_check=True)
                mm.then_inc(s["down_ready"], 1)

            def body(b, par, half_b):
                for j in range(FT):
                    if valid(b, n):
                        up_tile(b, j, par)
                    if j < 2 and valid(b - 1, n):
                        down_tile(b - 1, FT - 2 + j, 1 - par)
                    if j >= 2 and valid(b, n):
                        down_tile(b, j - 2, par)
                    if j == 5 and valid(b + 1, n):
                        for c in range(C):
                            since(e, norm.s["h32_done"], C * (b + 1))
                            norm.transpose(e, b + 1, c, hT[c])

            bodies(e, n, body)


def linear_phase(nc, m, n, x_in, x_out, w_t, bias, low_rank, gates, consts, mods):
    lora_down_t, down_aux, lora_up_t, up_aux_t = low_rank
    rank, dd, ud = lora_down_t.shape[1], lora_down_t.shape[0], lora_up_t.shape[1]
    w = [m.sb(f"w_{part}", [P, C, D], F32R) for part in ("hi", "lo")]
    base = m.sb("base", [P, C, D])
    whole = m.sb("whole", [P, C, D])
    ldt = m.sb("ldt", [dd, rank])
    da = m.sb("da", [dd, D])
    lut = m.sb("lut", [rank, ud])
    uat = m.sb("uat", [ud, D])
    t1 = m.sb("t1", [rank, D])
    t2 = m.sb("t2", [ud, D])
    b32 = m.sb("b32", [1, D])
    bias_parts = [m.sb(f"b_{part}", [1, D], F32R) for part in ("hi", "lo")]
    ones = m.sb("ones", [1, P], F32R)
    res = Stream(m, x_in, x_out, gates)
    norm = Norm(m, res, consts, *mods, copies=2)
    out = [[m.ps(f"out{i}{j}") for j in range(2)] for i in range(2)]
    hT = [m.ps(f"hT{i}") for i in range(2)]
    names = """w_loaded t1_ready t1_done t2_ready t2_done w_ready whole_done w_hi_done w_split bias_hi_done bias_split
        ones_set out_ready"""
    s = {name: m.sem(name) for name in names.split()}

    with nc.Block() as block:

        @block.sync
        def _(e):
            res.load(e, 0, 0, 0)
            res.load(e, 1, 1, 0)
            for dst, src in ((base[:], w_t.rearrange("(c p) n -> p c n", p=P)), (ldt[:], lora_down_t), (da[:], down_aux),
                             (lut[:], lora_up_t), (uat[:], up_aux_t), (b32[:], bias)):
                e.dma_start(dst, src).then_inc(s["w_loaded"], 16)

            res.load_gates(e)

            def body(b, par, half_b):
                if valid(b + 3, n):
                    res.load(e, b + 3, 1 - par, half_b + 1 + par)
                if valid(b - 1, n):
                    res.store(e, b - 1)

            bodies(e, n, body, ahead=3)
            e.wait_ge(res.s["stored"], 16 * n)

        @block.gpsimd
        def _(e):
            norm.rsqrt(e, 0)

            def body(b, par, half_b):
                if valid(b + 2, n):
                    norm.rsqrt(e, b + 2)
                if valid(b - 1, n):
                    res.add(e, b - 1, 0)

            bodies(e, n, body)

        @block.scalar
        def _(e):
            def body(b, par, half_b):
                if valid(b + 1, n):
                    for t in range(T):
                        norm.normalise(e, b + 1, t)
                    since(e, s["out_ready"], 2 * b)
                    for c in range(C):
                        norm.modulate(e, b + 1, c, hT[c])
                        norm.modulate_hi(e, b + 1, c, hT[c], 1 - par)

            bodies(e, n, body)

        @block.vector
        def _(e):
            e.memset(ones[:].bitcast(F32), 1.0).then_inc(s["ones_set"], 1)
            res.loaded(e, 0, 0)
            norm.all_statistics(e, 0)
            e.wait_ge(s["w_loaded"], 96)
            e.tensor_copy(bias_parts[0][:], b32[:]).then_inc(s["bias_hi_done"], 1)
            e.wait_ge(s["bias_hi_done"], 1)
            e.tensor_tensor(bias_parts[1][:], b32[:], bias_parts[0][:].bitcast(F32), ALU.subtract).then_inc(s["bias_split"], 1)
            e.wait_ge(s["t1_ready"], 1)
            e.tensor_copy(t1[:], out[0][0][0:rank, 0:D]).then_inc(s["t1_done"], 1)
            e.wait_ge(s["t2_ready"], 1)
            e.tensor_copy(t2[:], out[0][0][0:ud, 0:D]).then_inc(s["t2_done"], 1)
            e.wait_ge(s["w_ready"], 1)
            e.tensor_tensor(whole[:], out[0][1][:].rearrange("p (c d) -> p c d", c=C), base[:],
                            ALU.add).then_inc(s["whole_done"], 1)
            e.wait_ge(s["whole_done"], 1)
            e.tensor_copy(w[0][:], whole[:]).then_inc(s["w_hi_done"], 1)
            e.wait_ge(s["w_hi_done"], 1)
            e.tensor_tensor(w[1][:], whole[:], w[0][:].bitcast(F32), ALU.subtract).then_inc(s["w_split"], 1)

            def body(b, par, half_b):
                if valid(b - 1, n):
                    for part in range(2):
                        e.wait_ge(s["out_ready"], 2 * (b - 1) + part + 1)
                        res.multiply(e, b - 1, part, out[1 - par][part])
                if valid(b + 2, n):
                    res.loaded(e, par, half_b + 1)
                    for t in range(T):
                        norm.statistics(e, b + 2, t)
                    norm.variance(e, b + 2)
                if valid(b - 1, n):
                    res.add(e, b - 1, 1)
                if valid(b + 2, n):
                    norm.shift_of_mean(e, b + 2)
                if valid(b + 1, n):
                    for c in range(C):
                        norm.lo(e, b + 1, c, 1 - par)

            bodies(e, n, body)

        @block.tensor
        def _(e):
            e.wait_ge(s["w_loaded"], 96)
            e.matmul(out[0][0][0:rank, 0:D], ldt[:], da[:], start=True, stop=True).then_inc(s["t1_ready"], 1)
            e.wait_ge(s["t1_done"], 1)
            e.matmul(out[0][0][0:ud, 0:D], lut[:], t1[:], start=True, stop=True).then_inc(s["t2_ready"], 1)
            e.wait_ge(s["t2_done"], 1)
            for c in range(C):
                mm = e.matmul(out[0][1][:, c * D:(c + 1) * D], t2[:, c * P:(c + 1) * P], uat[:], start=True, stop=True)
            mm.then_inc(s["w_ready"], 1)
            e.wait_ge(s["w_split"], 1)
            e.wait_ge(s["bias_split"], 1)
            e.wait_ge(s["ones_set"], 1)

            def body(b, par, half_b):
                for part in range(2):
                    if valid(b, n):
                        if part == 0:
                            e.wait_ge(norm.s["h_lo_done"], C * (b + 1))
                            since(e, res.s["gated_done"], 2 * (b - 1))
                        for t in (2 * part, 2 * part + 1):
                            dst = out[par][part][:, t % 2 * D:(t % 2 + 1) * D]
                            e.matmul(dst, ones[:], bias_parts[0][:], start=True, stop=False)
                            e.matmul(dst, ones[:], bias_parts[1][:], start=False, stop=False)
                            for a, z in PASSES:
                                for kc in range(C):
                                    mm = e.matmul(dst, norm.h[par][z][:, kc, t * P:(t + 1) * P], w[a][:, kc, :],
                                                  start=False, stop=(a, z, kc) == (*PASSES[-1], C - 1))
                        mm.then_inc(s["out_ready"], 1)
                    if part == 0 and valid(b + 1, n):
                        for c in range(C):
                            since(e, norm.s["h_hi_done"], C * b + c + 1)
                            since(e, norm.s["h32_done"], C * b + c + 1)
                            norm.transpose(e, b + 1, c, hT[c])

            bodies(e, n, body)


def program(nc, a, out):
    n = a["x"].shape[0]
    shape = [n, P, T, D]
    mid = [nc.dram_tensor(f"x_after{i}", shape, F32, kind="Internal").ap() for i in range(3)]
    gates = nc.dram_tensor("gates", [4, n, D], F32, kind="Internal").ap()
    with Memory(nc, "top") as top:
        consts = {"ident": top.sb("ident", [P, P]), "ident_bf": top.sb("ident_bf", [P, P], BF16),
                  "neg_mask": top.sb("neg_mask", [P, 2 * P], BF16), "minus_half": top.sb("minus_half", [P, T])}
        mods = [top.sb(f"mods{i}", [P, 4, C, n]) for i in range(2)]

        picked = (top.sb("idx", [1, 2, TOPK], U32), top.sb("wcol", [P, 2, TOPK // 2]))

        def pair(layer, which):
            return mods[layer][:, 2 * which + 1], mods[layer][:, 2 * which]

        with Memory(nc, "set") as m:
            setup_phase(nc, m, n, a["c"], a["wmod"], a["logits"], consts, mods, gates, picked)
        with Memory(nc, "soft") as m:
            attention_phase(nc, m, n, 0, a["x"], mid[0], a["w_attn0"], gates[0], consts, pair(0, 0))
        with Memory(nc, "ffn") as m:
            ffn_phase(nc, m, n, mid[0], mid[1], ((a["a1"], a["b1"]), (a["a2"], a["b2"])), picked, gates[1], consts,
                      pair(0, 1))
        with Memory(nc, "lin") as m:
            attention_phase(nc, m, n, 1, mid[1], mid[2], a["w_attn1"], gates[2], consts, pair(1, 0))
        with Memory(nc, "out") as m:
            linear_phase(nc, m, n, mid[2], out, a["w_lin"], a["bias"],
                         (a["lora_down_t"], a["down_aux"], a["lora_up_t"], a["up_aux_t"]), gates[3], consts, pair(1, 1))


def kernel(**inputs):
    import concourse.bacc as bacc
    from concourse.bass_utils import run_bass_kernel_spmd

    v = {name: np.asarray(x) for name, x in inputs.items()}
    n = v["L0_attn_x"].shape[0]
    flip = lambda x: np.ascontiguousarray(np.swapaxes(x, -1, -2))
    arrays = {
        "x": np.ascontiguousarray(v["L0_attn_x"].reshape(n, T, P, D).transpose(0, 2, 1, 3)),
        "c": np.stack([flip(v["L0_c"]), flip(v["L1_c"])]),
        "wmod": np.stack([v["L0_wmod"], v["L1_wmod"]]),
        "w_attn0": np.stack([flip(v[f"L0_attn_{x}_proj_weight"]) for x in "qkvo"]),
        "w_attn1": np.stack([v["L1_attn_w_attn"][:, i * D:(i + 1) * D] for i in range(3)] + [v["L1_attn_w_proj"]]),
        "a1": flip(v["L0_ffn_fc1_A"]), "b1": v["L0_ffn_fc1_B"], "a2": flip(v["L0_ffn_fc2_A"]), "b2": v["L0_ffn_fc2_B"],
        "logits": np.stack([v["L0_ffn_fc1_logits"], v["L0_ffn_fc2_logits"]]),
        "w_lin": flip(v["L1_ffn_W"]), "bias": v["L1_ffn_b"].reshape(1, D),
        "lora_down_t": flip(v["L1_ffn_lora_down"]), "down_aux": v["L1_ffn_down_aux"],
        "lora_up_t": flip(v["L1_ffn_lora_up"]), "up_aux_t": flip(v["L1_ffn_up_aux"]),
    }
    nc = bacc.Bacc("TRN2", target_bir_lowering=False, num_devices=1)
    aps = {name: nc.dram_tensor(f"in_{name}", x.shape, mybir.dt.from_np(x.dtype), kind="ExternalInput").ap()
           for name, x in arrays.items()}
    out = nc.dram_tensor("out", arrays["x"].shape, F32, kind="ExternalOutput").ap()
    program(nc, aps, out)
    r = run_bass_kernel_spmd(nc, [{f"in_{name}": x for name, x in arrays.items()}], core_ids=[0])
    y = r.results[0]["out"]
    return np.ascontiguousarray(y.transpose(0, 2, 1, 3)).reshape(n, T * P, D)
```
